# Optimizing a Trainium2 kernel written in Bass

```python
import numpy as np
import jax
import jax.numpy as jnp

def _softmax(x, axis=-1):
    return jax.nn.softmax(x, axis=axis)

def _gelu(x):
    return jax.nn.gelu(x, approximate=True)

def _silu(x):
    return jax.nn.silu(x)

def _sigmoid(x):
    return jax.nn.sigmoid(x)

def _layernorm(x, axis=-1, eps=1e-05):
    m = jnp.mean(x, axis=axis, keepdims=True)
    v = jnp.var(x, axis=axis, keepdims=True)
    return (x - m) / jnp.sqrt(v + eps)

def _scatter_add(tgt, idx, src, axis=0):
    return tgt.at[idx].add(src)

def _segment_sum(src, seg, n):
    return jax.ops.segment_sum(src, seg, n)
kernel_name = 'mk_lm_tower_d2_tok_ids256_r4_097586'

def setup_inputs(seed: int=0):
    np.random.seed(seed)
    _w = jnp.asarray

    def _rec_inputs():
        import jax
        import jax.numpy as jnp
        _rk = jax.random.key(seed)
        x = jax.random.randint(jax.random.fold_in(_rk, 1), (16, 512), 0, 64, jnp.int32)
        itok_BS_0_255 = jax.random.randint(jax.random.fold_in(_rk, 21), (16, 512), 0, 64, jnp.int32)
        itok_BS_0_511 = jax.random.randint(jax.random.fold_in(_rk, 22), (16, 512), 0, 128, jnp.int32)
        itok_BS_0_127 = jax.random.randint(jax.random.fold_in(_rk, 23), (16, 512), 0, 128, jnp.int32)
        itok_BS_0_63 = jax.random.randint(jax.random.fold_in(_rk, 24), (16, 512), 0, 64, jnp.int32)
        itok_BS_0_3 = jax.random.randint(jax.random.fold_in(_rk, 25), (16, 512), 0, 4, jnp.int32)
        return (x, itok_BS_0_255, itok_BS_0_511, itok_BS_0_127, itok_BS_0_63, itok_BS_0_3)
    x, itok_BS_0_255, itok_BS_0_511, itok_BS_0_127, itok_BS_0_63, itok_BS_0_3 = _rec_inputs()

    def _L0_tok_setup():
        import jax, jax.numpy as jnp
        import numpy as np
        B, S = (128, 512)
        D_OUT = 64
        EMB = 16
        EPS_W = 1e-08
        EPS_LN = 1e-05

        def ternary_linear(x, W, b):
            scale = jnp.mean(jnp.abs(W))
            w_q = jnp.clip(jnp.round(W / (scale + EPS_W)), -1.0, 1.0) * scale
            w_eff = W + jax.lax.stop_gradient(w_q - W)
            return jnp.einsum('bsk,ok->bso', x, w_eff) + b

        def layer_norm(x, gamma, beta):
            mu = jnp.mean(x, axis=-1, keepdims=True)
            var = jnp.mean(jnp.square(x - mu), axis=-1, keepdims=True)
            return (x - mu) * jax.lax.rsqrt(var + EPS_LN) * gamma + beta
        key = jax.random.key(seed)
        ks = jax.random.split(key, 16)
        vocabs = {'event_type': 64, 'fault_class': 64, 'syscall_class': 128, 'opcode_family': 128, 'transition_type': 64, 'result_class': 4}
        inp = {}
        for i, (name, v) in enumerate(vocabs.items()):
            inp[name] = jax.random.randint(ks[i], (B, S), 0, v, dtype=jnp.int64)
        inp['E_et'] = jax.random.normal(ks[6], (64, EMB), dtype=jnp.float32)
        inp['E_fc'] = jax.random.normal(ks[7], (64, EMB), dtype=jnp.float32)
        inp['E_sc'] = jax.random.normal(ks[8], (128, EMB), dtype=jnp.float32)
        inp['E_of'] = jax.random.normal(ks[9], (128, EMB), dtype=jnp.float32)
        inp['E_tt'] = jax.random.normal(ks[10], (64, EMB), dtype=jnp.float32)
        inp['E_rc'] = jax.random.normal(ks[11], (4, EMB), dtype=jnp.float32)
        inp['W'] = jax.random.normal(ks[12], (D_OUT, 96), dtype=jnp.float32) * 0.1
        inp['b'] = jnp.zeros((D_OUT,), dtype=jnp.float32)
        inp['gamma'] = jnp.ones((D_OUT,), dtype=jnp.float32)
        inp['beta'] = jnp.zeros((D_OUT,), dtype=jnp.float32)
        return inp
    _L0_tok_all = _L0_tok_setup()
    _L0_tok_in = {k: v for k, v in _L0_tok_all.items() if k in ('E_et', 'E_fc', 'E_sc', 'E_of', 'E_tt', 'E_rc', 'W', 'b', 'gamma', 'beta')}
    del _L0_tok_all

    def _L0_attn_setup():
        import jax, jax.numpy as jnp
        import numpy as np
        D_K = 64
        SPARSITY = 0.5
        key = jax.random.key(seed)
        k1, k2, k3, k4, k5 = jax.random.split(key, 5)
        B, N, d_model, d_k, d_v = (4, 1024, 64, 64, 64)
        x = jax.random.normal(k1, (B, N, d_model), dtype=jnp.float32)
        W_qkv = jax.random.normal(k2, (d_model, 2 * d_k + d_v), dtype=jnp.float32) * 0.02
        b_qkv = jnp.zeros((2 * d_k + d_v,), dtype=jnp.float32)
        W_out = jax.random.normal(k3, (d_v, d_model), dtype=jnp.float32) * 0.02
        b_out = jnp.zeros((d_model,), dtype=jnp.float32)
        return {'x': x, 'W_qkv': W_qkv, 'b_qkv': b_qkv, 'W_out': W_out, 'b_out': b_out}
    _L0_attn_all = _L0_attn_setup()
    _L0_attn_in = {k: v for k, v in _L0_attn_all.items() if k in ('W_qkv', 'b_qkv', 'W_out', 'b_out')}
    del _L0_attn_all

    def _L0_ffn_setup():
        import jax, jax.numpy as jnp
        import numpy as np
        B, S, D, H, E, K = (8, 2048, 64, 256, 8, 2)
        key = jax.random.key(seed)
        ks = jax.random.split(key, 7)
        s_in = 1.0 / np.sqrt(D)
        s_hid = 1.0 / np.sqrt(H)
        return {'x': jax.random.normal(ks[0], (B, S, D), dtype=jnp.float32), 'Wg': jax.random.uniform(ks[1], (E, D), jnp.float32, -s_in, s_in), 'bg': jax.random.uniform(ks[2], (E,), jnp.float32, -s_in, s_in), 'W1': jax.random.uniform(ks[3], (E, H, D), jnp.float32, -s_in, s_in), 'b1': jax.random.uniform(ks[4], (E, H), jnp.float32, -s_in, s_in), 'W2': jax.random.uniform(ks[5], (E, D, H), jnp.float32, -s_hid, s_hid), 'b2': jax.random.uniform(ks[6], (E, D), jnp.float32, -s_hid, s_hid)}
    _L0_ffn_all = _L0_ffn_setup()
    _L0_ffn_in = {k: v for k, v in _L0_ffn_all.items() if k in ('Wg', 'bg', 'W1', 'b1', 'W2', 'b2')}
    del _L0_ffn_all

    def _L1_attn_setup():
        import jax, jax.numpy as jnp
        import numpy as np
        B, L, H, N = (8, 2048, 64, 32)

        def _s4_forward(u, log_dt, A_real_log, A_imag, C_re, C_im, D, W_out, b_out):
            Lq = u.shape[-1]
            Hd = u.shape[1]
            dt = jnp.exp(log_dt)[:, None]
            A = -jnp.exp(A_real_log) + 1j * A_imag
            dtA = dt * A
            C = C_re + 1j * C_im
            Cd = C * (jnp.exp(dtA) - 1.0) / A
            vand = jnp.exp(dtA[:, :, None] * jnp.arange(Lq))
            K = 2.0 * jnp.einsum('chn,hnl->chl', Cd, vand).real
            k_fwd, k_bwd = (K[0], K[1])
            zeros = jnp.zeros_like(k_fwd)
            k = jnp.concatenate([k_fwd, zeros], -1) + jnp.concatenate([zeros, jnp.flip(k_bwd, -1)], -1)
            k_f = jnp.fft.rfft(k, n=2 * Lq)
            u_f = jnp.fft.rfft(u, n=2 * Lq)
            y = jnp.fft.irfft(u_f * k_f, n=2 * Lq)[..., :Lq]
            y = y + u * D[:, None]
            y = jax.nn.gelu(y, approximate=False)
            y = jnp.einsum('bhl,gh->bgl', y, W_out) + b_out[None, :, None]
            return y[:, :Hd] * jax.nn.sigmoid(y[:, Hd:])
        key = jax.random.key(seed)
        ks = jax.random.split(key, 8)
        x = jax.random.normal(ks[0], (B, L, H), jnp.float32)
        log_dt = jnp.log(0.001) + jax.random.uniform(ks[1], (H,), jnp.float32) * (jnp.log(0.1) - jnp.log(0.001))
        A_real_log = jnp.log(0.5 * jnp.ones((H, N), jnp.float32))
        A_imag = jnp.pi * jnp.broadcast_to(jnp.arange(N, dtype=jnp.float32), (H, N))
        C_re = jax.random.normal(ks[2], (2, H, N), jnp.float32) * 0.5 ** 0.5
        C_im = jax.random.normal(ks[3], (2, H, N), jnp.float32) * 0.5 ** 0.5
        D = jax.random.normal(ks[4], (H,), jnp.float32)
        W_out = jax.random.normal(ks[5], (2 * H, H), jnp.float32) / np.sqrt(H).astype(np.float32)
        b_out = jnp.zeros((2 * H,), jnp.float32)
        gamma = jnp.ones((H,), jnp.float32)
        beta = jnp.zeros((H,), jnp.float32)
        return dict(x=x, log_dt=log_dt, A_real_log=A_real_log, A_imag=A_imag, C_re=C_re, C_im=C_im, D=D, W_out=W_out, b_out=b_out, gamma=gamma, beta=beta)
    _L1_attn_all = _L1_attn_setup()
    _L1_attn_in = {k: v for k, v in _L1_attn_all.items() if k in ('log_dt', 'A_real_log', 'A_imag', 'C_re', 'C_im', 'D', 'W_out', 'b_out', 'gamma', 'beta')}
    del _L1_attn_all

    def _L1_ffn_setup():
        import jax, jax.numpy as jnp
        import numpy as np
        B, K, D = (128, 16, 64)
        E = 32
        H = int(D * 0.25)
        key = jax.random.key(seed)
        ks = jax.random.split(key, 7)
        d_rs = D ** (-0.5)
        h_rs = H ** (-0.5)
        x = jax.random.normal(ks[0], (B, K, D), dtype=jnp.float32)
        router_w = jax.random.uniform(ks[1], (E, D), jnp.float32, -d_rs, d_rs)
        router_b = jax.random.uniform(ks[2], (E,), jnp.float32, -d_rs, d_rs)
        W1 = jax.random.uniform(ks[3], (E, D, H), jnp.float32, -h_rs, h_rs)
        b1 = jax.random.uniform(ks[4], (E, H), jnp.float32, -h_rs, h_rs)
        W2 = jax.random.uniform(ks[5], (E, H, D), jnp.float32, -d_rs, d_rs)
        b2 = jax.random.uniform(ks[6], (E, D), jnp.float32, -d_rs, d_rs)
        return {'x': x, 'router_w': router_w, 'router_b': router_b, 'W1': W1, 'b1': b1, 'W2': W2, 'b2': b2}
    _L1_ffn_all = _L1_ffn_setup()
    _L1_ffn_in = {k: v for k, v in _L1_ffn_all.items() if k in ('router_w', 'router_b', 'W1', 'b1', 'W2', 'b2')}
    del _L1_ffn_all
    return {'x': x, 'itok_BS_0_255': itok_BS_0_255, 'itok_BS_0_511': itok_BS_0_511, 'itok_BS_0_127': itok_BS_0_127, 'itok_BS_0_63': itok_BS_0_63, 'itok_BS_0_3': itok_BS_0_3, 'L0_tok_E_et': _L0_tok_in['E_et'], 'L0_tok_E_fc': _L0_tok_in['E_fc'], 'L0_tok_E_sc': _L0_tok_in['E_sc'], 'L0_tok_E_of': _L0_tok_in['E_of'], 'L0_tok_E_tt': _L0_tok_in['E_tt'], 'L0_tok_E_rc': _L0_tok_in['E_rc'], 'L0_tok_W': _L0_tok_in['W'], 'L0_tok_b': _L0_tok_in['b'], 'L0_tok_gamma': _L0_tok_in['gamma'], 'L0_tok_beta': _L0_tok_in['beta'], 'L0_attn_W_qkv': _L0_attn_in['W_qkv'], 'L0_attn_b_qkv': _L0_attn_in['b_qkv'], 'L0_attn_W_out': _L0_attn_in['W_out'], 'L0_attn_b_out': _L0_attn_in['b_out'], 'L0_ffn_Wg': _L0_ffn_in['Wg'], 'L0_ffn_bg': _L0_ffn_in['bg'], 'L0_ffn_W1': _L0_ffn_in['W1'], 'L0_ffn_b1': _L0_ffn_in['b1'], 'L0_ffn_W2': _L0_ffn_in['W2'], 'L0_ffn_b2': _L0_ffn_in['b2'], 'L1_attn_log_dt': _L1_attn_in['log_dt'], 'L1_attn_A_real_log': _L1_attn_in['A_real_log'], 'L1_attn_A_imag': _L1_attn_in['A_imag'], 'L1_attn_C_re': _L1_attn_in['C_re'], 'L1_attn_C_im': _L1_attn_in['C_im'], 'L1_attn_D': _L1_attn_in['D'], 'L1_attn_W_out': _L1_attn_in['W_out'], 'L1_attn_b_out': _L1_attn_in['b_out'], 'L1_attn_gamma': _L1_attn_in['gamma'], 'L1_attn_beta': _L1_attn_in['beta'], 'L1_ffn_router_w': _L1_ffn_in['router_w'], 'L1_ffn_router_b': _L1_ffn_in['router_b'], 'L1_ffn_W1': _L1_ffn_in['W1'], 'L1_ffn_b1': _L1_ffn_in['b1'], 'L1_ffn_W2': _L1_ffn_in['W2'], 'L1_ffn_b2': _L1_ffn_in['b2']}

def reference(x, itok_BS_0_255, itok_BS_0_511, itok_BS_0_127, itok_BS_0_63, itok_BS_0_3, L0_tok_E_et, L0_tok_E_fc, L0_tok_E_sc, L0_tok_E_of, L0_tok_E_tt, L0_tok_E_rc, L0_tok_W, L0_tok_b, L0_tok_gamma, L0_tok_beta, L0_attn_W_qkv, L0_attn_b_qkv, L0_attn_W_out, L0_attn_b_out, L0_ffn_Wg, L0_ffn_bg, L0_ffn_W1, L0_ffn_b1, L0_ffn_W2, L0_ffn_b2, L1_attn_log_dt, L1_attn_A_real_log, L1_attn_A_imag, L1_attn_C_re, L1_attn_C_im, L1_attn_D, L1_attn_W_out, L1_attn_b_out, L1_attn_gamma, L1_attn_beta, L1_ffn_router_w, L1_ffn_router_b, L1_ffn_W1, L1_ffn_b1, L1_ffn_W2, L1_ffn_b2):
    import jax
    import jax.numpy as jnp

    def _L0_tok_ref(event_type, fault_class, syscall_class, opcode_family, transition_type, result_class, E_et, E_fc, E_sc, E_of, E_tt, E_rc, W, b, gamma, beta):
        import jax, jax.numpy as jnp
        import numpy as np
        B, S = (128, 512)
        D_OUT = 64
        EMB = 16
        EPS_W = 1e-08
        EPS_LN = 1e-05

        def ternary_linear(x, W, b):
            scale = jnp.mean(jnp.abs(W))
            w_q = jnp.clip(jnp.round(W / (scale + EPS_W)), -1.0, 1.0) * scale
            w_eff = W + jax.lax.stop_gradient(w_q - W)
            return jnp.einsum('bsk,ok->bso', x, w_eff) + b

        def layer_norm(x, gamma, beta):
            mu = jnp.mean(x, axis=-1, keepdims=True)
            var = jnp.mean(jnp.square(x - mu), axis=-1, keepdims=True)
            return (x - mu) * jax.lax.rsqrt(var + EPS_LN) * gamma + beta
        combined = jnp.concatenate([E_et[event_type], E_fc[fault_class], E_sc[syscall_class], E_of[opcode_family], E_tt[transition_type], E_rc[result_class]], axis=-1)
        z = ternary_linear(combined, W, b)
        return layer_norm(z, gamma, beta)

    def _L0_attn_ref(x, W_qkv, b_qkv, W_out, b_out):
        import jax, jax.numpy as jnp
        import numpy as np
        D_K = 64
        SPARSITY = 0.5
        d_k = D_K
        qkv = x @ W_qkv + b_qkv
        q = qkv[..., :d_k]
        k = qkv[..., d_k:2 * d_k]
        v = qkv[..., 2 * d_k:]
        scores = jnp.einsum('bqd,bkd->bqk', q, k) / jnp.sqrt(jnp.float32(d_k))
        topk = int(SPARSITY * scores.shape[-1])
        thr = jax.lax.top_k(scores, topk)[0][..., -1:]
        sparse_mask = (scores >= thr).astype(scores.dtype)
        attn = jax.nn.softmax(scores * sparse_mask, axis=-1)
        out = jnp.einsum('bqk,bkd->bqd', attn, v)
        return out @ W_out + b_out

    def _L0_ffn_ref(x, Wg, bg, W1, b1, W2, b2):
        import jax, jax.numpy as jnp
        import numpy as np
        B, S, D, H, E, K = (8, 2048, 64, 256, 8, 2)
        gate_scores = jnp.einsum('bsd,ed->bse', x, Wg) + bg
        topk_scores, topk_idx = jax.lax.top_k(gate_scores, K)
        topk_probs = jax.nn.softmax(topk_scores, axis=-1)
        combine = jnp.sum(topk_probs[..., None] * jax.nn.one_hot(topk_idx, E, dtype=x.dtype), axis=-2)
        out = jnp.zeros_like(x)
        for e in range(E):
            h = jax.nn.relu(jnp.einsum('bsd,hd->bsh', x, W1[e]) + b1[e])
            y = jnp.einsum('bsh,dh->bsd', h, W2[e]) + b2[e]
            out = out + combine[..., e:e + 1] * y
        return out

    def _L1_attn_ref(x, log_dt, A_real_log, A_imag, C_re, C_im, D, W_out, b_out, gamma, beta):
        import jax, jax.numpy as jnp
        import numpy as np
        B, L, H, N = (8, 2048, 64, 32)

        def _s4_forward(u, log_dt, A_real_log, A_imag, C_re, C_im, D, W_out, b_out):
            Lq = u.shape[-1]
            Hd = u.shape[1]
            dt = jnp.exp(log_dt)[:, None]
            A = -jnp.exp(A_real_log) + 1j * A_imag
            dtA = dt * A
            C = C_re + 1j * C_im
            Cd = C * (jnp.exp(dtA) - 1.0) / A
            vand = jnp.exp(dtA[:, :, None] * jnp.arange(Lq))
            K = 2.0 * jnp.einsum('chn,hnl->chl', Cd, vand).real
            k_fwd, k_bwd = (K[0], K[1])
            zeros = jnp.zeros_like(k_fwd)
            k = jnp.concatenate([k_fwd, zeros], -1) + jnp.concatenate([zeros, jnp.flip(k_bwd, -1)], -1)
            k_f = jnp.fft.rfft(k, n=2 * Lq)
            u_f = jnp.fft.rfft(u, n=2 * Lq)
            y = jnp.fft.irfft(u_f * k_f, n=2 * Lq)[..., :Lq]
            y = y + u * D[:, None]
            y = jax.nn.gelu(y, approximate=False)
            y = jnp.einsum('bhl,gh->bgl', y, W_out) + b_out[None, :, None]
            return y[:, :Hd] * jax.nn.sigmoid(y[:, Hd:])
        u = jnp.swapaxes(x, -1, -2)
        z = _s4_forward(u, log_dt, A_real_log, A_imag, C_re, C_im, D, W_out, b_out)
        r = z + u
        r = jnp.swapaxes(r, -1, -2)
        mu = r.mean(-1, keepdims=True)
        var = r.var(-1, keepdims=True)
        return (r - mu) / jnp.sqrt(var + 1e-05) * gamma + beta

    def _L1_ffn_ref(x, router_w, router_b, W1, b1, W2, b2):
        import jax, jax.numpy as jnp
        import numpy as np
        B, K, D = (128, 16, 64)
        E = 32
        H = int(D * 0.25)
        xf = x.reshape(-1, D)
        logits = xf @ router_w.T + router_b
        idx = jnp.argmax(logits, axis=-1)
        w1t = jnp.take(W1, idx, axis=0)
        h = jnp.einsum('nd,ndh->nh', xf, w1t) + jnp.take(b1, idx, axis=0)
        h = jax.nn.relu(h)
        w2t = jnp.take(W2, idx, axis=0)
        out = jnp.einsum('nh,nhd->nd', h, w2t) + jnp.take(b2, idx, axis=0)
        out = jax.nn.relu(out)
        return out.reshape(x.shape)
    h = _L0_tok_ref(x, itok_BS_0_255, itok_BS_0_511, itok_BS_0_127, itok_BS_0_63, itok_BS_0_3, L0_tok_E_et, L0_tok_E_fc, L0_tok_E_sc, L0_tok_E_of, L0_tok_E_tt, L0_tok_E_rc, L0_tok_W, L0_tok_b, L0_tok_gamma, L0_tok_beta)
    h = h + _L0_attn_ref(_layernorm(h, axis=-1), L0_attn_W_qkv, L0_attn_b_qkv, L0_attn_W_out, L0_attn_b_out)
    h = h + _L0_ffn_ref(_layernorm(h, axis=-1), L0_ffn_Wg, L0_ffn_bg, L0_ffn_W1, L0_ffn_b1, L0_ffn_W2, L0_ffn_b2)
    h = h + _L1_attn_ref(_layernorm(h, axis=-1), L1_attn_log_dt, L1_attn_A_real_log, L1_attn_A_imag, L1_attn_C_re, L1_attn_C_im, L1_attn_D, L1_attn_W_out, L1_attn_b_out, L1_attn_gamma, L1_attn_beta)
    h = h + _L1_ffn_ref(_layernorm(h, axis=-1), L1_ffn_router_w, L1_ffn_router_b, L1_ffn_W1, L1_ffn_b1, L1_ffn_W2, L1_ffn_b2)
    return h

_drawn_inputs = setup_inputs


def setup_inputs(seed=0):
    import zlib

    import numpy as np

    out = dict(_drawn_inputs(seed))
    spreads = {'L0_tok_b': (0.0, 0.1),
     'L0_tok_gamma': (1.0, 0.2),
     'L0_tok_beta': (0.0, 0.1),
     'L0_attn_b_qkv': (0.0, 0.1),
     'L0_attn_b_out': (0.0, 0.1),
     'L1_attn_A_real_log': (-0.6931471824645996, 0.581),
     'L1_attn_b_out': (0.0, 0.286),
     'L1_attn_gamma': (1.0, 0.2),
     'L1_attn_beta': (0.0, 0.1)}
    factors = {'L0_attn_W_qkv': 3.728, 'L1_ffn_b1': 6.308}
    for name, (base, spread) in spreads.items():
        noise = np.random.default_rng([zlib.crc32(name.encode()), seed]).standard_normal(out[name].shape)
        drawn = base * np.exp(spread * noise) if base else spread * noise
        out[name] = jnp.asarray(drawn.astype(out[name].dtype))
    for name, factor in factors.items():
        out[name] = (out[name] * factor).astype(out[name].dtype)
    return out
```

```python
from contextlib import ExitStack

import concourse.bass as bass
from concourse import mybir

F32 = mybir.dt.float32
BF16 = mybir.dt.bfloat16
I32 = mybir.dt.int32
U32 = mybir.dt.uint32
ALU = mybir.AluOpType
ACT = mybir.ActivationFunctionType
AX_X = mybir.AxisListType.X
ts = bass.ts

P = 128
NB, S, D = 16, 512, 64
TJ = S // P
ROW = TJ * D
NE, HID = 8, 256
HH = HID // P
NX, XH = 32, 16
XC = NX * XH // P
NS = 32
NHI, NLO = 16, 32
KROW = 2 * S
TW = (2 * TJ - 1) * P
HG = 4
SEARCH = 4
AIM = S / 2 - 4.5
BISECT = 32
FAR = 1e30
MAGIC = 1.5 * 2.0 ** 23
TWO_PI_HI = 6.28125
TWO_PI_LO = 0.0019353071795864769
PI_SAFE = 3.1415925
BIG = 2.0 ** 60
EPS = 1e-5


class Count:

    def __init__(self, eng, sem, base=0):
        self.eng, self.sem, self.base, self.n = eng, sem, base, 0

    def step(self, ins):
        ins.then_inc(self.sem, 1)
        self.n += 1

    def settle(self):
        self.eng.wait_ge(self.sem, self.base + self.n)

    def one(self, ins):
        self.step(ins)
        self.settle()


class Signal:

    def __init__(self, sem, each=1):
        self.sem, self.each = sem, each

    def grant(self, eng):
        eng.sem_inc(self.sem, self.each)

    def nth(self, b, n=None):
        return self.each * b + self.each + (self.each if n is None else n)

    def before(self, b):
        return self.each * b + self.each


def apart(eng, spare):
    eng.sem_inc(spare, 1)


def bc(ap, shape):
    return ap.to_broadcast(shape)


def split3(dve, c, x, rest, parts):
    a, b, last = parts
    c.one(dve.tensor_copy(a, x))
    c.one(dve.tensor_tensor(rest, x, a, ALU.subtract))
    c.one(dve.tensor_copy(b, rest))
    c.one(dve.tensor_tensor(x, rest, b, ALU.subtract))
    c.one(dve.tensor_copy(last, x))


def tower(nc, A, out):
    with ExitStack() as ctx:
        def sb(name, shape, dt=F32):
            return ctx.enter_context(nc.sbuf_tensor(name, shape, dt))

        def sem(name):
            return ctx.enter_context(nc.semaphore(name))

        bank = [ctx.enter_context(nc.psum_tensor(f"bank{i}", [P, 512], F32)) for i in range(8)]
        taps = nc.dram_tensor("taps", (D, KROW), F32, kind="Internal")

        h = sb("h", [P, NB * ROW])
        u = sb("u", [P, NB * TJ, D])
        gy = sb("gy", [P, NB, TJ, D])
        identf = sb("identf", [P, P])
        identb = sb("identb", [P, P], BF16)
        WT = sb("WT", [96, D])
        Et = sb("Et", [96, 4, P])
        table = sb("table", [P, 4, 3, D], BF16)
        gam0, bet0 = sb("gam0", [P, D]), sb("bet0", [P, D])
        gam1, bet1 = sb("gam1", [P, D]), sb("bet1", [P, D])
        tokb = sb("tokb", [P, D])
        Wqkv = sb("Wqkv", [D + 1, 3 * D])
        Wo = sb("Wo", [D, D])
        bo = sb("bo", [P, D])
        Wg = sb("Wg", [D + 1, NE])
        W1 = sb("W1", [D + 1, NE * HID])
        W2 = sb("W2", [P, NE * HH, D])
        b2f = sb("b2f", [3 * NE, D])
        b2p = sb("b2p", [3 * NE, 3, D], BF16)
        sel = sb("sel", [3 * NE, NE, D + 1], BF16)
        Wglu = sb("Wglu", [D + 1, 2 * D])
        Wr = sb("Wr", [D + 1, NX])
        Wx1 = sb("Wx1", [P, XC * P])
        Wx2 = sb("Wx2", [P, XC, D])
        bx2 = sb("bx2", [P, D])

        w_in = sem("w_in")
        spare = sem("spare")
        consts = sem("consts")
        NW = 32
        LOADS = [
            (WT[:], A["WT"]), (Et[:], A["Et"].rearrange("k (c v) -> k c v", c=4)),
            (gam0[:], A["gam0"].partition_broadcast(P)), (bet0[:], A["bet0"].partition_broadcast(P)),
            (gam1[:], A["gam1"].partition_broadcast(P)), (bet1[:], A["bet1"].partition_broadcast(P)),
            (tokb[:], A["tokb"].partition_broadcast(P)),
            (Wqkv[0:D, :], A["Wqkv"]), (Wqkv[D:D + 1, :], A["bqkv"].unsqueeze(0)),
            (Wo[:], A["Wo"]), (bo[:], A["bo"].partition_broadcast(P)),
            (Wg[0:D, :], A["WgT"]), (Wg[D:D + 1, :], A["bg"].unsqueeze(0)),
            (W1[0:D, :], A["W1T"]), (W1[D:D + 1, :], A["b1"].unsqueeze(0)),
            (W2[:], A["W2T"].rearrange("(c p) d -> p c d", p=P)),
            (Wglu[0:D, :], A["WgluT"]), (Wglu[D:D + 1, :], A["bglu"].unsqueeze(0)),
            (Wr[0:D, :], A["WrT"]), (Wr[D:D + 1, :], A["br"].unsqueeze(0)),
            (Wx2[:], A["Wx2"].rearrange("(c p) d -> p c d", p=P)),
        ] + [(b2f[NE * i:NE * i + NE, :], A["b2"]) for i in range(3)]

        with ExitStack() as own:
            def tmp(name, shape, dt=F32):
                return own.enter_context(nc.sbuf_tensor(name, shape, dt))

            onesf = tmp("onesf", [P, P])
            absw, rowsum, half, nhalf, scl = (tmp(n, [96, k]) for n, k in
                                              (("absw", D), ("rowsum", 1), ("half", 1), ("nhalf", 1), ("scl", 1)))
            wpos, wneg, weff = tmp("wpos", [96, D]), tmp("wneg", [96, D]), tmp("weff", [96, D])
            tabf, tabr = tmp("tabf", [P, 4, D]), tmp("tabr", [P, 4, D])
            b2r = tmp("b2r", [3 * NE, D])
            M = 2 * NS
            ldt, arl, aim = tmp("ldt", [M, D]), tmp("arl", [M, D]), tmp("aim", [M, D])
            cre, cim = tmp("cre", [M, 2, D]), tmp("cim", [M, 2, D])
            skip = tmp("skip", [1, D])
            ki = tmp("ki", [M, NLO + NHI], I32)
            kf = tmp("kf", [M, NLO + NHI])
            phase, sgn = tmp("phase", [M, 1]), tmp("sgn", [M, 1])
            dt_, are, w, a = (tmp(n, [M, D]) for n in ("dt_", "are", "w", "a"))
            NK = NLO + NHI
            theta, turns, mag = (tmp(n, [M, D, NK]) for n in ("theta", "turns", "mag"))
            th2, tn2, sc2 = (tmp(n, [M, 2, D]) for n in ("th2", "tn2", "sc2"))
            q1, q2, q3, q4, em = (tmp(n, [M, D]) for n in ("q1", "q2", "q3", "q4", "em"))
            er, ei, yr, yi = (tmp(n, [M, D]) for n in ("er", "ei", "yr", "yi"))
            cr, ci, cs = tmp("cr", [M, 2, D]), tmp("ci", [M, 2, D]), tmp("cs", [M, 2, D])
            hi_sw = tmp("hi_sw", [M, D, NHI])
            left, lt2 = tmp("left", [M, 2, D, NHI]), tmp("lt2", [M, 2, D, NHI])
            lo_rev = tmp("lo_rev", [M, D, NLO])
            lbuf, mbuf = tmp("lbuf", [M, 2, HG, NHI]), tmp("mbuf", [M, 2, HG, NLO])
            rows = tmp("rows", [NHI, 2, D, NLO])
            p_in = sem("p_in")
            g_clear = sem("g_clear")
            PLOADS = [(cre[NS * r:NS * r + NS], A["CreT"].rearrange("n (c h) -> n c h", c=2)) for r in range(2)]
            PLOADS += [(cim[NS * r:NS * r + NS], A["CimT"].rearrange("n (c h) -> n c h", c=2)) for r in range(2)]
            PLOADS += [(arl[NS * r:NS * r + NS, :], A["ArlT"]) for r in range(2)]
            PLOADS += [(aim[NS * r:NS * r + NS, :], A["AimT"]) for r in range(2)]
            PLOADS += [(ldt[:], A["ldt"].partition_broadcast(M)), (skip[:], A["skip"].unsqueeze(0))]

            g_step, v_step = sem("g_step_setup"), sem("v_step_setup")
            a_dt, a_tanh, a_sin2, a_mag, a_sin = (sem(n) for n in ("a_dt", "a_tanh", "a_sin2", "a_mag", "a_sin"))
            v_a, v_w2, v_prod, v_theta, v_abs, v_weff = (
                sem(n) for n in ("v_a", "v_w2", "v_prod", "v_theta", "v_abs", "v_weff"))
            t_sum, t_tab, t_bx = sem("t_sum"), sem("t_tab"), sem("t_bx")
            v_left, v_lbuf, v_mbuf, t_taps, v_rows, taps_out = (
                sem(n) for n in ("v_left", "v_lbuf", "v_mbuf", "t_taps", "v_rows", "taps_out"))

            with nc.Block() as block:
                @block.sync
                def _(sp):
                    for dst, src in PLOADS:
                        sp.dma_start(dst, src).then_inc(p_in, 16)
                    for dst, src in LOADS:
                        sp.dma_start(dst, src).then_inc(w_in, 16)
                    sp.wait_ge(g_clear, 1)
                    sp.dma_start(Wx1[0:D, :], A["Wx1"]).then_inc(w_in, 16)
                    sp.dma_start(Wx1[D:D + 1, :], A["bx1"].unsqueeze(0)).then_inc(w_in, 16)
                    sp.dma_start(bx2[96:P, :], A["bx2"]).then_inc(w_in, 16)
                    sp.wait_ge(v_rows, 2 * D // HG + 1)
                    sp.dma_start(taps.ap().rearrange("h (c a b) -> a c h b", c=2, a=NHI)[:, 0], rows[:, 0])\
                      .then_inc(taps_out, 16)
                    sp.dma_start(taps.ap().rearrange("h (c a b) -> a c h b", c=2, a=NHI)[:, 1], rows[:, 1])\
                      .then_inc(taps_out, 16)
                    sp.wait_ge(taps_out, 32)

                @block.gpsimd
                def _(pool):
                    c = Count(pool, g_step)
                    c.one(pool.memset(identf[:], 0.0))
                    c.one(pool.memset(identb[:], 0.0))
                    c.one(pool.memset(sel[:], 1.0))
                    c.one(pool.memset(onesf[:], 1.0))
                    c.one(pool.memset(phase[0:NS, :], 0.25))
                    c.one(pool.memset(phase[NS:M, :], 0.0))
                    c.one(pool.memset(sgn[0:NS, :], 1.0))
                    c.one(pool.memset(sgn[NS:M, :], -1.0))
                    c.one(pool.memset(Wx1[:], 0.0))
                    c.one(pool.iota(ki[:, 0:NLO], pattern=[[1, NLO]], base=0, channel_multiplier=0))
                    c.one(pool.iota(ki[:, NLO:NK], pattern=[[NLO, NHI]], base=0, channel_multiplier=0))
                    c.settle()
                    for m in (identf, identb):
                        c.step(pool.affine_select(out=m[:], in_=m[:], compare_op=ALU.not_equal, fill=1.0, base=0,
                                                  pattern=[[-1, P]], channel_multiplier=1))
                    for lo in (0, NE, 2 * NE):
                        c.one(pool.affine_select(out=sel[:], in_=sel[:], compare_op=ALU.not_equal, fill=2.0, base=-lo,
                                                 pattern=[[-1, NE], [0, D + 1]], channel_multiplier=1))
                    c.one(pool.tensor_scalar(sel[:], sel[:], 1.0, None, ALU.subtract))
                    c.one(pool.tensor_copy(kf[:], ki[:]))
                    c.one(pool.memset(Wx1[96:P, :], BIG))
                    big = Wx1[96:P, :].rearrange("k (e x) -> k e x", x=XH)
                    c.one(pool.affine_select(out=big, in_=big, compare_op=ALU.is_equal, fill=0.0, base=0,
                                             pattern=[[-1, NX], [0, XH]], channel_multiplier=1))
                    pool.memset(bx2[:], 0.0).then_inc(g_clear, 1)
                    pool.wait_ge(w_in, 16 * (len(LOADS) + 3))
                    pool.sem_inc(consts, 1)

                @block.scalar
                def _(act):
                    act.wait_ge(p_in, 16 * len(PLOADS))
                    act.activation(dt_[:], ldt[:], ACT.Exp).then_inc(a_dt, 1)
                    act.activation(are[:], arl[:], ACT.Exp).then_inc(a_dt, 1)
                    act.wait_ge(v_a, 1)
                    act.activation(q1[:], a[:], ACT.Tanh, scale=0.5).then_inc(a_tanh, 1)
                    act.wait_ge(v_prod, 1)
                    act.activation(mag[:], mag[:], ACT.Exp).then_inc(a_mag, 1)
                    act.wait_ge(v_w2, 1)
                    act.activation(sc2[:], th2[:], ACT.Sin).then_inc(a_sin2, 1)
                    act.wait_ge(v_theta, 1)
                    act.activation(theta[:], theta[:], ACT.Sin).then_inc(a_sin, 1)

                @block.tensor
                def _(pe):
                    pe.wait_ge(v_abs, 1)
                    pe.matmul(bank[0][0:96, 0:1], onesf[0:96, 0:96], rowsum[:], start=True, stop=True).then_inc(t_sum, 1)
                    pe.wait_ge(v_weff, 1)
                    for c in range(4):
                        last = pe.matmul(bank[1][:, ts(c, D)], Et[:, c, :], weff[:], start=True, stop=True)
                    last.then_inc(t_tab, 1)
                    pe.wait_ge(consts, 1)
                    pe.matmul(bank[4][:, 0:D], onesf[96:P, :], bx2[96:P, :], start=True, stop=True).then_inc(t_bx, 1)
                    pe.wait_ge(v_left, 1)
                    with pe.Fori(0, D // HG) as g:
                        pe.wait_ge(v_lbuf, g + 1)
                        pe.wait_ge(v_mbuf, 2 * g + 2)
                        apart(pe, spare)
                        for hh in range(HG):
                            for c in range(2):
                                last = pe.matmul(bank[2 + c][0:NHI, ts(hh, NLO)], lbuf[:, c, hh, :], mbuf[:, c, hh, :],
                                                 start=True, stop=True)
                        last.then_inc(t_taps, 1)

                @block.vector
                def _(dve):
                    c = Count(dve, v_step)

                    def reduced(ang, trn, plus):
                        c.one(dve.tensor_scalar(trn, ang, 1.0 / (2.0 * 3.141592653589793), plus, ALU.mult, ALU.add))
                        c.one(dve.tensor_scalar(trn, trn, MAGIC, MAGIC, ALU.add, ALU.subtract))
                        c.one(dve.scalar_tensor_tensor(out=ang, in0=trn, scalar=-TWO_PI_HI, in1=ang,
                                                       op0=ALU.mult, op1=ALU.add))
                        c.one(dve.scalar_tensor_tensor(out=ang, in0=trn, scalar=-TWO_PI_LO, in1=ang,
                                                       op0=ALU.mult, op1=ALU.add))

                    dve.wait_ge(consts, 1)
                    c.one(dve.scalar_tensor_tensor(out=absw[:], in0=WT[:], scalar=-1.0, in1=WT[:],
                                                   op0=ALU.mult, op1=ALU.max))
                    dve.tensor_reduce(rowsum[:], absw[:], AX_X, ALU.add).then_inc(v_abs, 1)
                    dve.wait_ge(t_sum, 1)
                    c.one(dve.tensor_scalar(scl[:], bank[0][0:96, 0:1], 1.0 / (96 * D), None, ALU.mult))
                    c.one(dve.tensor_scalar(half[:], scl[:], 1e-8, 0.5, ALU.add, ALU.mult))
                    c.one(dve.tensor_scalar(nhalf[:], half[:], -1.0, None, ALU.mult))
                    c.step(dve.tensor_scalar(wpos[:], WT[:], half[:], None, ALU.is_gt))
                    c.one(dve.tensor_scalar(wneg[:], WT[:], nhalf[:], None, ALU.is_lt))
                    c.one(dve.tensor_tensor(wpos[:], wpos[:], wneg[:], ALU.subtract))
                    c.one(dve.scalar_tensor_tensor(out=wneg[:], in0=wpos[:], scalar=scl[:], in1=WT[:],
                                                   op0=ALU.mult, op1=ALU.subtract))
                    dve.tensor_tensor(weff[:], wneg[:], WT[:], ALU.add).then_inc(v_weff, 1)
                    dve.wait_ge(t_tab, 1)
                    c.one(dve.tensor_copy(tabf[:].rearrange("p c d -> p (c d)"), bank[1][:, 0:4 * D]))
                    c.one(dve.tensor_tensor(tabf[0:64, 0, :], tabf[0:64, 0, :], tokb[0:64, :], ALU.add))
                    for x, r, parts in ((tabf, tabr, [table[:, :, i, :] for i in range(3)]),
                                        (b2f, b2r, [b2p[:, i, :] for i in range(3)])):
                        split3(dve, c, x[:], r[:], parts)
                    dve.wait_ge(t_bx, 1)
                    c.one(dve.tensor_copy(bx2[D:D + 1, :], bank[4][D:D + 1, 0:D]))
                    dve.wait_ge(a_dt, 2)
                    c.one(dve.tensor_scalar(are[:], are[:], -1.0, None, ALU.mult))
                    c.step(dve.tensor_tensor(w[:], dt_[:], aim[:], ALU.mult))
                    c.one(dve.tensor_tensor(a[:], dt_[:], are[:], ALU.mult))
                    dve.engine_nop().then_inc(v_a, 1)
                    kb = bc(kf[:].unsqueeze(1), [M, D, NK])
                    dve.tensor_tensor(mag[:], bc(a[:].unsqueeze(2), [M, D, NK]), kb, ALU.mult).then_inc(v_prod, 1)
                    c.one(dve.tensor_scalar(th2[:, 0, :], w[:], 0.5, None, ALU.mult))
                    c.one(dve.tensor_scalar(th2[:, 1, :], th2[:, 0, :], 1.0, None, ALU.mult))
                    reduced(th2[:, 0, :], tn2[:, 0, :], 0.0)
                    reduced(th2[:, 1, :], tn2[:, 1, :], 0.25)
                    c.one(dve.tensor_scalar(th2[:, 1, :], th2[:, 1, :], 1.5707963267948966, None, ALU.add))
                    c.one(dve.tensor_scalar(th2[:], th2[:], PI_SAFE, -PI_SAFE, ALU.min, ALU.max))
                    dve.engine_nop().then_inc(v_w2, 1)
                    c.one(dve.tensor_tensor(theta[:], bc(w[:].unsqueeze(2), [M, D, NK]), kb, ALU.mult))
                    reduced(theta[:], turns[:], phase[:, 0:1])
                    c.one(dve.tensor_scalar(q4[:, 0:1], phase[:], 4 * 1.5707963267948966, None, ALU.mult))
                    c.one(dve.tensor_scalar(theta[:], theta[:], q4[:, 0:1], PI_SAFE, ALU.add, ALU.min))
                    c.one(dve.tensor_scalar(theta[:], theta[:], -PI_SAFE, None, ALU.max))
                    dve.engine_nop().then_inc(v_theta, 1)
                    dve.wait_ge(a_tanh, 1)
                    c.one(dve.tensor_scalar(q2[:], q1[:], -1.0, 1.0, ALU.mult, ALU.add))
                    c.one(dve.reciprocal(q3[:], q2[:]))
                    c.one(dve.scalar_tensor_tensor(out=em[:], in0=q1[:], scalar=2.0, in1=q3[:],
                                                   op0=ALU.mult, op1=ALU.mult))
                    dve.wait_ge(a_sin2, 1)
                    c.step(dve.scalar_tensor_tensor(out=q1[:], in0=sc2[:, 0, :], scalar=-2.0, in1=sc2[:, 0, :],
                                                    op0=ALU.mult, op1=ALU.mult))
                    c.one(dve.scalar_tensor_tensor(out=q2[:], in0=sc2[:, 0, :], scalar=2.0, in1=sc2[:, 1, :],
                                                   op0=ALU.mult, op1=ALU.mult))
                    c.one(dve.scalar_tensor_tensor(out=q3[:], in0=q1[:], scalar=1.0, in1=em[:],
                                                   op0=ALU.add, op1=ALU.mult))
                    c.step(dve.tensor_tensor(er[:], q3[:], q1[:], ALU.add))
                    c.one(dve.scalar_tensor_tensor(out=ei[:], in0=em[:], scalar=1.0, in1=q2[:],
                                                   op0=ALU.add, op1=ALU.mult))
                    c.step(dve.tensor_tensor(q1[:], are[:], are[:], ALU.mult))
                    c.one(dve.tensor_tensor(q2[:], aim[:], aim[:], ALU.mult))
                    c.one(dve.tensor_tensor(q3[:], q1[:], q2[:], ALU.add))
                    c.one(dve.reciprocal(q1[:], q3[:]))
                    c.step(dve.tensor_tensor(yr[:], er[:], are[:], ALU.mult))
                    c.step(dve.tensor_tensor(q2[:], ei[:], aim[:], ALU.mult))
                    c.step(dve.tensor_tensor(yi[:], ei[:], are[:], ALU.mult))
                    c.one(dve.tensor_tensor(q4[:], er[:], aim[:], ALU.mult))
                    c.step(dve.tensor_tensor(yr[:], yr[:], q2[:], ALU.add))
                    c.one(dve.tensor_tensor(yi[:], yi[:], q4[:], ALU.subtract))
                    c.step(dve.scalar_tensor_tensor(out=yr[:], in0=yr[:], scalar=2.0, in1=q1[:], op0=ALU.mult, op1=ALU.mult))
                    c.one(dve.scalar_tensor_tensor(out=yi[:], in0=yi[:], scalar=2.0, in1=q1[:], op0=ALU.mult, op1=ALU.mult))
                    yrb, yib = bc(yr[:].unsqueeze(1), [M, 2, D]), bc(yi[:].unsqueeze(1), [M, 2, D])
                    c.step(dve.tensor_tensor(cr[:], cre[:], yrb, ALU.mult))
                    c.one(dve.tensor_tensor(cs[:], cim[:], yib, ALU.mult))
                    c.one(dve.tensor_tensor(cr[:], cr[:], cs[:], ALU.subtract))
                    c.step(dve.tensor_tensor(ci[:], cre[:], yib, ALU.mult))
                    c.one(dve.tensor_tensor(cs[:], cim[:], yrb, ALU.mult))
                    c.one(dve.tensor_tensor(ci[:], ci[:], cs[:], ALU.add))
                    c.step(dve.tensor_scalar(cr[:], cr[:], sgn[:, 0:1], None, ALU.mult))
                    c.one(dve.tensor_scalar(ci[:], ci[:], -1.0, None, ALU.mult))
                    dve.wait_ge(a_mag, 1)
                    dve.wait_ge(a_sin, 1)
                    c.one(dve.tensor_tensor(theta[:], theta[:], mag[:], ALU.mult))
                    c.step(dve.tensor_copy(hi_sw[0:NS], theta[NS:M, :, NLO:NK]))
                    c.step(dve.tensor_copy(hi_sw[NS:M], theta[0:NS, :, NLO:NK]))
                    c.one(dve.tensor_copy(lo_rev[:], theta[:, :, 0:NLO][:, :, ::-1]))
                    for way, src in ((0, 1), (1, 0)):
                        e1, e2 = theta[:, :, NLO:NK], hi_sw[:]
                        if way == 0:
                            e1, e2 = e1[:, :, ::-1], e2[:, :, ::-1]
                        c.step(dve.tensor_tensor(left[:, way], bc(cr[:, src, :].unsqueeze(2), [M, D, NHI]), e1, ALU.mult))
                        c.one(dve.tensor_tensor(lt2[:, way], bc(ci[:, src, :].unsqueeze(2), [M, D, NHI]), e2, ALU.mult))
                        c.one(dve.tensor_tensor(left[:, way], left[:, way], lt2[:, way], ALU.add))
                    dve.engine_nop().then_inc(v_left, 1)
                    with dve.Fori(0, D // HG) as g:
                        dve.tensor_copy(mbuf[:, 0], lo_rev[:, bass.ds(g * HG, HG), :]).then_inc(v_mbuf, 1)
                        dve.tensor_copy(mbuf[:, 1], theta[:, bass.ds(g * HG, HG), 0:NLO]).then_inc(v_mbuf, 1)
                        dve.tensor_copy(lbuf[:], left[:, :, bass.ds(g * HG, HG), :]).then_inc(v_lbuf, 1)
                        dve.wait_ge(t_taps, g + 1)
                        dve.tensor_copy(rows[:, 0, bass.ds(g * HG, HG), :],
                                        bank[2][0:NHI, 0:HG * NLO].rearrange("a (h b) -> a h b", h=HG))\
                           .then_inc(v_rows, 1)
                        dve.tensor_copy(rows[:, 1, bass.ds(g * HG, HG), :],
                                        bank[3][0:NHI, 0:HG * NLO].rearrange("a (h b) -> a h b", h=HG))\
                           .then_inc(v_rows, 1)
                    dve.wait_ge(v_rows, 2 * D // HG)
                    dve.tensor_tensor(rows[0:1, 1, :, 0], rows[0:1, 1, :, 0], skip[:], ALU.add).then_inc(v_rows, 1)

        def stats(dve, c, x, st, mv, done):
            apart(dve, spare)
            for j in range(TJ):
                c.step(dve.bn_stats(st[:, j, :], x[:, j, :]))
            c.settle()
            apart(dve, spare)
            for j in range(TJ):
                last = dve.bn_aggr(mv[:, j, :], st[:, j, :])
                if j < TJ - 1:
                    c.step(last)
            last.then_inc(done.sem, 1)

        def rstd(pool, c, ready, b, mv, rs, power, done):
            pool.wait_ge(ready.sem, ready.nth(b))
            apart(pool, spare)
            c.one(pool.tensor_scalar(rs[:], mv[:, :, 1], EPS, None, ALU.add))
            pool.tensor_tensor(rs[:], rs[:], power[:], ALU.pow).then_inc(done.sem, 1)

        def centre(dve, c, x, mv, rs, dst):
            for j in range(TJ):
                c.step(dve.tensor_scalar(dst[:, j, :], x[:, j, :], mv[:, j, 0:1], rs[:, j:j + 1],
                                         ALU.subtract, ALU.mult))

        def tiled(ap):
            return ap.rearrange("p (j d) -> p j d", j=TJ)

        with ExitStack() as own:
            def tmp(name, shape, dt=F32):
                return own.enter_context(nc.sbuf_tensor(name, shape, dt))

            ids = [tmp(f"ids{i}", [P, 4, S], I32) for i in range(2)]
            onehot = tmp("onehot", [P, 4, S], BF16)
            rowi = tmp("rowi", [P, 2], I32)
            rowf = tmp("rowf", [P, 2])
            st, mv, rs = tmp("st_e", [P, TJ, 6]), tmp("mv_e", [P, TJ, 2]), tmp("rs_e", [P, TJ])
            power = tmp("power_e", [P, TJ])
            xn, xg = tmp("xn_e", [P, TJ, D]), tmp("xg_e", [P, TJ, D])
            ids_in = [sem("ids_in_even"), sem("ids_in_odd")]
            g_row = sem("g_row")
            v_hot, t_z = Signal(sem("v_hot"), 2), Signal(sem("t_z"))
            v_stats, g_rstd = Signal(sem("v_stats_e")), Signal(sem("g_rstd_e"))
            v_norm, g_gain, g_h = Signal(sem("v_norm_e"), TJ), Signal(sem("g_gain_e")), Signal(sem("g_h"))
            g_step, v_step = sem("g_step_e"), sem("v_step_e")
            IDS = [(0, 0, 64, "x"), (0, 64, P, "itok_BS_0_255"), (2, 0, P, "itok_BS_0_511"),
                   (3, 0, P, "itok_BS_0_127"), (1, 0, 64, "itok_BS_0_63"), (1, 64, 68, "itok_BS_0_3")]
            VSTEP, GSTEP = 2 * TJ - 1, 1

            with nc.Block() as block:
                @block.sync
                def _(sp):
                    sp.wait_ge(g_row, 5)
                    with sp.Fori(0, NB // 2) as i:
                        for r in range(2):
                            sp.wait_ge(v_hot.sem, v_hot.before(2 * i))
                            for c, lo, hi, name in IDS:
                                src = A[name][bass.ds(2 * i + r, 1), :].rearrange("a s -> (a s)")
                                sp.dma_start(ids[r][lo:hi, c, :], src.partition_broadcast(hi - lo))\
                                  .then_inc(ids_in[r], 16)

                @block.gpsimd
                def _(pool):
                    c = Count(pool, g_row)
                    c.one(pool.memset(ids[0][64:P, 1, :], -1))
                    c.one(pool.memset(ids[1][64:P, 1, :], -1))
                    c.one(pool.memset(power[:], -0.5))
                    c.one(pool.iota(rowi[:, 1:2], pattern=[[0, 1]], base=0, channel_multiplier=1))
                    c.one(pool.iota(rowi[0:64, 0:1], pattern=[[0, 1]], base=0, channel_multiplier=1))
                    c.one(pool.iota(rowi[64:P, 0:1], pattern=[[0, 1]], base=0, channel_multiplier=1))
                    c.one(pool.tensor_copy(rowf[:], rowi[:]))
                    g_gain.grant(pool)
                    g_rstd.grant(pool)
                    g_h.grant(pool)
                    with pool.Fori(0, NB) as b:
                        c = Count(pool, g_step, GSTEP * b)
                        rstd(pool, c, v_stats, b, mv, rs, power, g_rstd)
                        pool.wait_ge(v_norm.sem, v_norm.nth(b))
                        pool.tensor_tensor(xg[:], xn[:], bc(gam0[:].unsqueeze(1), [P, TJ, D]), ALU.mult).then_inc(g_gain.sem, 1)
                        pool.wait_ge(g_gain.sem, g_gain.nth(b))
                        pool.tensor_tensor(tiled(h[:, ts(b, ROW)]), xg[:], bc(bet0[:].unsqueeze(1), [P, TJ, D]), ALU.add)\
                            .then_inc(g_h.sem, 1)

                @block.vector
                def _(dve):
                    dve.wait_ge(g_row, 7)
                    for s in (v_hot, v_stats, v_norm):
                        s.grant(dve)
                    with dve.Fori(0, NB // 2) as i:
                        for r in range(2):
                            b = 2 * i + r
                            c = Count(dve, v_step, VSTEP * b)
                            dve.wait_ge(ids_in[r], 96 * (i + 1))
                            dve.wait_ge(t_z.sem, t_z.before(b))
                            for half_, col in ((0, 0), (1, 1)):
                                dve.tensor_scalar(onehot[:, 2 * half_:2 * half_ + 2, :], ids[r][:, 2 * half_:2 * half_ + 2, :],
                                                  rowf[:, col:col + 1], None, ALU.is_equal).then_inc(v_hot.sem, 1)
                            dve.wait_ge(t_z.sem, t_z.nth(b))
                            z = tiled(bank[0][:, 0:ROW])
                            stats(dve, c, z, st, mv, v_stats)
                            dve.wait_ge(g_rstd.sem, g_rstd.nth(b))
                            dve.wait_ge(g_gain.sem, g_gain.before(b))
                            for j in range(TJ):
                                dve.tensor_scalar(xn[:, j, :], z[:, j, :], mv[:, j, 0:1], rs[:, j:j + 1],
                                                  ALU.subtract, ALU.mult).then_inc(v_norm.sem, 1)

                @block.tensor
                def _(pe):
                    t_z.grant(pe)
                    with pe.Fori(0, NB) as b:
                        pe.wait_ge(v_hot.sem, v_hot.nth(b))
                        pe.wait_ge(v_norm.sem, v_norm.before(b))
                        for j in range(TJ):
                            for k in range(12):
                                c, part = k // 3, k % 3
                                last = pe.matmul(bank[0][:, ts(j, D)], onehot[:, c, ts(j, P)], table[:, c, part, :],
                                                 start=(k == 0), stop=(k == 11))
                        last.then_inc(t_z.sem, 1)

        with ExitStack() as own:
            def tmp(name, shape, dt=F32):
                return own.enter_context(nc.sbuf_tensor(name, shape, dt))

            def signals(names, each=1):
                return (Signal(sem(n), each) for n in names.split())

            power, root = tmp("power", [P, TJ]), tmp("root", [P, TJ])
            tiny = [[tmp(f"{n}{k}", [P, TJ] + s) for n, s in (("st", [6]), ("mv", [2]), ("rs", []))] for k in range(4)]
            hb, xn = tmp("hb", [P, TJ, D]), tmp("xn", [P, TJ, D])
            xT, qT, kT, vT = tmp("xT", [D + 1, S]), tmp("qT", [D, S]), tmp("kT", [D, S]), tmp("vT", [D, S])
            vo = tmp("vo", [P, TJ, D])
            sc, ms = tmp("sc", [P, TJ, S]), tmp("ms", [P, TJ, S])
            above = tmp("above", [P, S], BF16)
            mx, nm, rsum, rinv = (tmp(n, [P, TJ]) for n in ("mx", "nm", "rsum", "rinv"))
            ksum = tmp("ksum", [D, 1])
            point, low, high, gap = (tmp(n, [P, 2, TJ]) for n in ("point", "low", "high", "gap"))
            is_low, is_high = tmp("is_low", [P, TJ], U32), tmp("is_high", [P, TJ], U32)
            frac, inv, asum = tmp("frac", [P, TJ]), tmp("inv", [P, TJ]), tmp("asum", [P, TJ])
            exact, rank, thr, near, bad = (tmp(n, [P, TJ]) for n in ("exact", "rank", "thr", "near", "bad"))
            top8, hit8, order8 = tmp("top8", [P, TJ, 8]), tmp("hit8", [P, TJ, 8]), tmp("order8", [P, 8])
            order8i = tmp("order8i", [P, 8], I32)
            nbadf, nbad = tmp("nbadf", [1, 1]), tmp("nbad", [1, 1], I32)
            onecol = tmp("onecol", [P, 1])
            junk, ajunk = tmp("junk", [P, TJ, S], BF16), tmp("ajunk", [P, TJ, S], BF16)
            lo, mid, delta, cnt, up = (tmp(n, [P, TJ]) for n in ("lo", "mid", "delta", "cnt", "up"))
            eT = tmp("eT", [P, 2, TJ, P])
            xn2, x2T = tmp("xn2", [P, TJ, D]), tmp("x2T", [D + 1, S])
            gate, top = tmp("gate", [P, TJ, NE]), tmp("top", [P, TJ, NE])
            gd, ge, gm, comb, cres = (tmp(n, [P, TJ, NE]) for n in ("gd", "ge", "gm", "comb", "cres"))
            gsum, grec = tmp("gsum", [P, TJ]), tmp("grec", [P, TJ])
            c24 = tmp("c24", [P, TJ, 3, NE], BF16)
            cT = tmp("cT", [3 * NE, S], BF16)
            xe = tmp("xe", [D + 1, 2, S])
            hid = tmp("hid", [P, 2, HH, S])

            v_stats, v_xn, v_k, v_nm = signals("v_stats v_xn v_k v_nm")
            g_rstd, g_hb = signals("g_rstd g_hb")
            t_xT, t_qk, t_vT, t_vo = signals("t_xT t_qk t_vT t_vo")
            a_xT, a_q, a_vT, a_vo, a_mean = signals("a_xT a_q a_vT a_vo a_mean")
            t_s, v_sc, v_ms, a_e, t_eT, t_o, v_h1 = signals("t_s v_sc v_ms a_e t_eT t_o v_h1", TJ)
            v_eT, a_eT = signals("v_eT a_eT", TJ // 2)
            v_st2, v_xn2, v_gd, v_c24 = signals("v_st2 v_xn2 v_gd v_c24")
            g_rs2, g_rs3 = signals("g_rs2 g_rs3")
            t_x2T, t_gate, t_cT, t_out = signals("t_x2T t_gate t_cT t_out")
            a_x2T, a_ge, a_cT = signals("a_x2T a_ge a_cT")
            t_bc, v_xe, t_h0, t_h1, a_hid, v_hid, t_w2 = signals("t_bc v_xe t_h0 t_h1 a_hid v_hid t_w2", NE)
            v_gate, v_h2, v_st3, v_u = signals("v_gate v_h2 v_st3 v_u")
            g_step, v_step, v_bis, ones_in = sem("g_step0"), sem("v_step0"), sem("v_bis"), sem("ones_in")
            v_pt, v_cnt, a_cnt = Signal(sem("v_pt"), SEARCH), Signal(sem("v_cnt"), SEARCH * TJ // 2), Signal(sem("a_cnt"), SEARCH * TJ // 2)
            v_bad, t_bad = Signal(sem("v_bad")), Signal(sem("t_bad"))
            BSTEP = 8
            FSTEP = 3 + BSTEP * BISECT + 1
            VSTEP, GSTEP = 111, 3

            with nc.Block() as block:
                @block.gpsimd
                def _(pool):
                    for k, (t, value) in enumerate(((power[:], -0.5), (root[:], 0.5), (xT[D:D + 1, :], 1.0),
                                                    (x2T[D:D + 1, :], 1.0))):
                        pool.memset(t, value).then_inc(ones_in, 1)
                        pool.wait_ge(ones_in, k + 1)
                    pool.memset(onecol[:], 1.0).then_inc(ones_in, 1)
                    pool.iota(order8i[:], pattern=[[1, 8]], base=0, channel_multiplier=0).then_inc(ones_in, 1)
                    pool.wait_ge(ones_in, 6)
                    pool.tensor_copy(order8[:], order8i[:]).then_inc(ones_in, 1)
                    for s in (g_rstd, g_hb, g_rs2, g_rs3):
                        s.grant(pool)
                    with pool.Fori(0, NB) as b:
                        c = Count(pool, g_step, GSTEP * b)
                        rstd(pool, c, v_stats, b, tiny[0][1], tiny[0][2], power, g_rstd)
                        pool.wait_ge(v_h1.sem, v_h1.before(b))
                        pool.tensor_tensor(hb[:], tiled(h[:, ts(b, ROW)]), bc(bo[:].unsqueeze(1), [P, TJ, D]), ALU.add)\
                            .then_inc(g_hb.sem, 1)
                        rstd(pool, c, v_st2, b, tiny[2][1], tiny[2][2], power, g_rs2)
                        rstd(pool, c, v_st3, b, tiny[3][1], tiny[3][2], power, g_rs3)
                        assert c.n == GSTEP

                @block.scalar
                def _(act):
                    for s in (a_mean, a_cnt, a_xT, a_q, a_vT, a_vo, a_e, a_eT, a_x2T, a_ge, a_cT, a_hid):
                        s.grant(act)
                    with act.Fori(0, NB) as b:
                        act.wait_ge(t_xT.sem, t_xT.nth(b))
                        act.activation(xT[0:D, :], bank[0][0:D, :], ACT.Copy).then_inc(a_xT.sem, 1)
                        act.wait_ge(t_qk.sem, t_qk.nth(b))
                        act.activation(qT[:], bank[1][0:D, :], ACT.Copy).then_inc(a_q.sem, 1)
                        act.wait_ge(t_vT.sem, t_vT.nth(b))
                        act.activation(vT[:], bank[2][0:D, :], ACT.Copy).then_inc(a_vT.sem, 1)
                        act.wait_ge(t_vo.sem, t_vo.nth(b))
                        act.activation(vo[:], tiled(bank[0][:, 0:ROW]), ACT.Copy).then_inc(a_vo.sem, 1)
                        act.activation(point[:, 0, :], bank[0][:, ROW:ROW + TJ], ACT.Copy, scale=1.0 / S).then_inc(a_mean.sem, 1)
                        for k in range(SEARCH):
                            act.wait_ge(v_pt.sem, v_pt.nth(b, k + 1))
                            for j in range(TJ // 2, TJ):
                                if k:
                                    act.wait_ge(a_cnt.sem, a_cnt.nth(b, (k - 1) * TJ // 2 + j - TJ // 2 + 1))
                                act.activation(ajunk[:, j, :], sc[:, j, :], ACT.Sign, bias=point[:, 0, j:j + 1], scale=-1.0,
                                               accum_out=asum[:, j:j + 1]).then_inc(a_cnt.sem, 1)
                        act.wait_ge(v_nm.sem, v_nm.nth(b))
                        for j in range(TJ):
                            act.wait_ge(v_ms.sem, v_ms.nth(b, j + 1))
                            act.activation(ms[:, j, :], ms[:, j, :], ACT.Exp, bias=nm[:, j:j + 1], scale=0.125,
                                           accum_out=rsum[:, j:j + 1]).then_inc(a_e.sem, 1)
                            if j % 2:
                                act.wait_ge(t_eT.sem, t_eT.nth(b, j + 1))
                                act.wait_ge(t_o.sem, t_o.nth(b, j - 1) if j > 1 else t_o.before(b))
                                act.activation(eT[:, 1], bank[3][:].rearrange("p (c q) -> p c q", c=TJ), ACT.Copy)\
                                   .then_inc(a_eT.sem, 1)
                        act.wait_ge(t_x2T.sem, t_x2T.nth(b))
                        act.activation(x2T[0:D, :], bank[4][0:D, :], ACT.Copy).then_inc(a_x2T.sem, 1)
                        act.wait_ge(v_gd.sem, v_gd.nth(b))
                        act.activation(ge[:], gd[:], ACT.Exp).then_inc(a_ge.sem, 1)
                        act.wait_ge(t_cT.sem, t_cT.nth(b))
                        act.activation(cT[:], bank[4][:].bitcast(BF16)[0:3 * NE, 0:S], ACT.Copy).then_inc(a_cT.sem, 1)
                        for e in range(NE):
                            act.wait_ge(t_h0.sem, t_h0.nth(b, e + 1))
                            act.wait_ge(t_w2.sem, t_w2.nth(b, e - 1) if e > 1 else t_w2.before(b))
                            act.activation(hid[:, e % 2, 0, :], bank[6][:], ACT.Relu).then_inc(a_hid.sem, 1)

                @block.tensor
                def _(pe):
                    for s in (t_bad, t_xT, t_qk, t_vT, t_vo, t_s, t_eT, t_o, t_x2T, t_gate, t_cT, t_out, t_bc, t_h0, t_h1, t_w2):
                        s.grant(pe)
                    pe.wait_ge(ones_in, 7)

                    def features(x, ready, into, done, b):
                        pe.wait_ge(ready.sem, ready.nth(b))
                        apart(pe, spare)
                        for j in range(TJ):
                            last = pe.transpose(into[0:D, ts(j, P)], x[:, j, :], identf[:])
                        last.then_inc(done.sem, 1)

                    with pe.Fori(0, NB) as b:
                        pe.wait_ge(v_h1.sem, v_h1.before(b))
                        features(xn, v_xn, bank[0], t_xT, b)
                        pe.wait_ge(a_xT.sem, a_xT.nth(b))
                        pe.wait_ge(v_eT.sem, v_eT.before(b))
                        pe.matmul(bank[1][:], Wqkv[:, 0:2 * D], xT[:], start=True, stop=True).then_inc(t_qk.sem, 1)
                        pe.wait_ge(v_sc.sem, v_sc.before(b))
                        pe.matmul(bank[2][0:D, :], Wqkv[:, 2 * D:3 * D], xT[:], start=True, stop=True)\
                          .then_inc(t_vT.sem, 1)
                        pe.wait_ge(a_vT.sem, a_vT.nth(b))
                        for j in range(TJ):
                            pe.matmul(bank[0][:, ts(j, D)], vT[:, ts(j, P)], Wo[:], start=True, stop=True)
                        pe.wait_ge(a_q.sem, a_q.nth(b))
                        pe.wait_ge(v_k.sem, v_k.nth(b))
                        for j in range(TJ):
                            last = pe.matmul(bank[0][:, ROW + j:ROW + j + 1], qT[:, ts(j, P)], ksum[:], start=True, stop=True)
                        last.then_inc(t_vo.sem, 1)
                        pe.wait_ge(a_eT.sem, a_eT.before(b))
                        for j in range(TJ):
                            if j >= 2:
                                pe.wait_ge(v_sc.sem, v_sc.nth(b, j - 1))
                            pe.matmul(bank[2 + j % 2][:], qT[:, ts(j, P)], kT[:], start=True, stop=True)\
                              .then_inc(t_s.sem, 1)
                        pe.wait_ge(a_vo.sem, a_vo.nth(b))
                        pe.wait_ge(v_sc.sem, v_sc.nth(b))
                        pe.wait_ge(v_bad.sem, v_bad.nth(b))
                        pe.matmul(bank[0][0:1, 0:TJ], onecol[:], bad[:], start=True, stop=True).then_inc(t_bad.sem, 1)

                        def weighted(j):
                            done = (v_eT, a_eT)[j % 2]
                            pe.wait_ge(done.sem, done.nth(b, j // 2 + 1))
                            for k in range(TJ):
                                last = pe.matmul(bank[0][:, ts(j, D)], eT[:, j % 2, k, :], vo[:, k, :],
                                                 start=(k == 0), stop=(k == TJ - 1))
                            last.then_inc(t_o.sem, 1)

                        for j in range(TJ):
                            pe.wait_ge(a_e.sem, a_e.nth(b, j + 1))
                            if j >= 2:
                                weighted(j - 2)
                            for k in range(TJ):
                                last = pe.transpose(bank[1 + 2 * (j % 2)][:, ts(k, P)], ms[:, j, ts(k, P)], identf[:])
                            last.then_inc(t_eT.sem, 1)
                        weighted(TJ - 2)
                        weighted(TJ - 1)
                        pe.wait_ge(v_h2.sem, v_h2.before(b))
                        features(xn2, v_xn2, bank[4], t_x2T, b)
                        pe.wait_ge(a_x2T.sem, a_x2T.nth(b))
                        for j in range(TJ):
                            last = pe.matmul(bank[4][:, ts(j, NE)], x2T[:, ts(j, P)], Wg[:], start=True, stop=True)
                        last.then_inc(t_gate.sem, 1)
                        pe.wait_ge(v_c24.sem, v_c24.nth(b))
                        for j in range(TJ):
                            last = pe.transpose(bank[4][:].bitcast(BF16)[0:3 * NE, ts(j, P)],
                                                c24[:, j].rearrange("p k e -> p (k e)"), identb[:])
                        last.then_inc(t_cT.sem, 1)
                        pe.wait_ge(a_cT.sem, a_cT.nth(b))

                        def share(e):
                            pe.wait_ge(v_xe.sem, v_xe.nth(b, e) if e else v_xe.before(b))
                            pe.matmul(bank[5][0:D + 1, :], sel[:, e, :], cT[:], start=True, stop=True).then_inc(t_bc.sem, 1)

                        def second(e):
                            pe.wait_ge(a_hid.sem, a_hid.nth(b, e + 1))
                            pe.wait_ge(v_hid.sem, v_hid.nth(b, e + 1))
                            for half_ in range(HH):
                                for j in range(TJ):
                                    last = pe.matmul(bank[4][:, ts(j, D)], hid[:, e % 2, half_, ts(j, P)],
                                                     W2[:, HH * e + half_, :], start=False,
                                                     stop=(e == NE - 1 and half_ == HH - 1), skip_group_check=True)
                            last.then_inc(t_w2.sem, 1)

                        share(0)
                        for j in range(TJ):
                            for k in range(3):
                                pe.matmul(bank[4][:, ts(j, D)], cT[:, ts(j, P)], b2p[:, k, :],
                                          start=(j == 0 and k == 0), stop=False, skip_group_check=True)
                        for e in range(NE):
                            pe.wait_ge(v_xe.sem, v_xe.nth(b, e + 1))
                            for half_, taken, done in ((0, a_hid, t_h0), (1, v_hid, t_h1)):
                                pe.wait_ge(taken.sem, taken.nth(b, e) if e else taken.before(b))
                                pe.matmul(bank[6 + half_][:], W1[:, ts(HH * e + half_, P)], xe[:, e % 2, :],
                                          start=True, stop=True).then_inc(done.sem, 1)
                            if e + 1 < NE:
                                share(e + 1)
                            if e:
                                second(e - 1)
                        second(NE - 1)

                @block.vector
                def _(dve):
                    for s in (v_pt, v_cnt, v_bad, v_stats, v_xn, v_k, v_nm, v_sc, v_ms, v_h1, v_eT, v_st2, v_xn2, v_gd, v_c24,
                              v_xe, v_hid, v_gate, v_h2, v_st3, v_u):
                        s.grant(dve)
                    dve.wait_ge(ones_in, 7)
                    with dve.Fori(0, NB) as b:
                        c = Count(dve, v_step, VSTEP * b)
                        hrow = tiled(h[:, ts(b, ROW)])
                        st, mv, rs = tiny[0]
                        stats(dve, c, hrow, st, mv, v_stats)
                        dve.wait_ge(g_rstd.sem, g_rstd.nth(b))
                        centre(dve, c, hrow, mv, rs, xn)
                        c.settle()
                        dve.sem_inc(v_xn.sem, 1)
                        dve.wait_ge(t_qk.sem, t_qk.nth(b))
                        dve.tensor_scalar(kT[:], bank[1][D:2 * D, :], 1.0, None, ALU.mult, ALU.add, accum_out=ksum[:])\
                           .then_inc(v_k.sem, 1)
                        st, mv, rs = tiny[1]
                        for j in range(TJ):
                            dve.wait_ge(t_s.sem, t_s.nth(b, j + 1))
                            dve.tensor_scalar(sc[:, j, :], bank[2 + j % 2][:], 1.0, None, ALU.mult, ALU.max,
                                              accum_out=mx[:, j:j + 1]).then_inc(v_sc.sem, 1)
                        dve.wait_ge(v_sc.sem, v_sc.nth(b))
                        c.step(dve.tensor_scalar(nm[:], mx[:], 0.0, -0.125, ALU.max, ALU.mult))
                        dve.wait_ge(a_mean.sem, a_mean.nth(b))
                        c.one(dve.tensor_tensor(frac[:], mx[:], point[:, 0, :], ALU.subtract))
                        dve.sem_inc(v_nm.sem, 1)
                        dve.sem_inc(v_pt.sem, 1)
                        c.step(dve.memset(low[:, 1, :], 0.84 * S))
                        c.step(dve.memset(high[:, 1, :], 0.16 * S))
                        c.one(dve.tensor_scalar(frac[:], frac[:], 1.0 / 3.0, None, ALU.mult))
                        c.step(dve.tensor_tensor(low[:, 0, :], point[:, 0, :], frac[:], ALU.subtract))
                        c.step(dve.tensor_tensor(high[:, 0, :], point[:, 0, :], frac[:], ALU.add))

                        def pair(ap):
                            return bc(ap.unsqueeze(1), [P, 2, TJ])

                        for k in range(SEARCH):
                            for j in range(TJ // 2):
                                dve.tensor_scalar(junk[:, j, :], sc[:, j, :], point[:, 0, j:j + 1], None, ALU.is_ge, ALU.add,
                                                  accum_out=point[:, 1, j:j + 1]).then_inc(v_cnt.sem, 1)
                            dve.wait_ge(a_cnt.sem, a_cnt.nth(b, (k + 1) * TJ // 2))
                            c.step(dve.tensor_scalar(point[:, 1, TJ // 2:], asum[:, TJ // 2:], -0.5, S / 2, ALU.mult, ALU.add))
                            dve.wait_ge(v_cnt.sem, v_cnt.nth(b, (k + 1) * TJ // 2))
                            c.settle()
                            c.step(dve.tensor_scalar(is_low[:], point[:, 1, :], S / 2 - 0.5, None, ALU.is_ge))
                            c.one(dve.tensor_scalar(is_high[:], point[:, 1, :], S / 2 - 0.5, None, ALU.is_lt))
                            apart(dve, spare)
                            c.step(dve.copy_predicated(low[:], pair(is_low[:]), point[:]))
                            c.one(dve.copy_predicated(high[:], pair(is_high[:]), point[:]))
                            if k == SEARCH - 1:
                                break
                            c.step(dve.tensor_scalar(frac[:], high[:, 1, :], AIM, 0.0, ALU.subtract, ALU.min))
                            c.one(dve.tensor_tensor(gap[:], low[:], high[:], ALU.subtract))
                            c.step(dve.reciprocal(inv[:], gap[:, 1, :]))
                            c.one(dve.tensor_tensor(frac[:], frac[:], gap[:, 0, :], ALU.mult))
                            c.one(dve.tensor_tensor(frac[:], frac[:], inv[:], ALU.mult))
                            dve.tensor_tensor(point[:, 0, :], high[:, 0, :], frac[:], ALU.subtract).then_inc(v_pt.sem, 1)
                            dve.wait_ge(v_pt.sem, v_pt.nth(b, k + 2))
                        for j in range(TJ):
                            c.step(dve.tensor_scalar(ms[:, j, :], sc[:, j, :], high[:, 0, j:j + 1], None, ALU.is_ge, ALU.add,
                                                     accum_out=exact[:, j:j + 1]))
                        c.settle()
                        for j in range(TJ):
                            c.step(dve.scalar_tensor_tensor(out=ms[:, j, :], in0=ms[:, j, :], scalar=-FAR, in1=sc[:, j, :],
                                                            op0=ALU.mult, op1=ALU.add))
                        c.step(dve.tensor_scalar(rank[:], exact[:], -1.0, S / 2 - 1.0, ALU.mult, ALU.add))
                        c.settle()
                        apart(dve, spare)
                        for j in range(TJ):
                            c.step(dve.max(top8[:, j, :], ms[:, j, :]))
                        c.one(dve.tensor_tensor(hit8[:], bc(order8[:].unsqueeze(1), [P, TJ, 8]),
                                                bc(rank[:].unsqueeze(2), [P, TJ, 8]), ALU.is_equal))
                        c.step(dve.tensor_reduce(near[:], hit8[:], AX_X, ALU.add))
                        c.one(dve.tensor_tensor(top8[:], top8[:], hit8[:], ALU.mult))
                        dve.tensor_scalar(bad[:], near[:], -1.0, 1.0, ALU.mult, ALU.add).then_inc(v_bad.sem, 1)
                        c.one(dve.tensor_reduce(thr[:], top8[:], AX_X, ALU.add))
                        dve.wait_ge(t_bad.sem, t_bad.nth(b))
                        c.one(dve.tensor_reduce(nbadf[:], bank[0][0:1, 0:TJ], AX_X, ALU.add))
                        c.one(dve.tensor_copy(nbad[:], nbadf[:]))
                        apart(dve, spare)
                        missed = dve.value_load(nbad[:], min_val=0, max_val=P * TJ)
                        with dve.If(missed > 0):
                            f = Count(dve, v_bis, FSTEP * b)
                            f.one(dve.tensor_reduce(lo[:], sc[:], AX_X, ALU.min))
                            f.one(dve.tensor_tensor(delta[:], mx[:], lo[:], ALU.subtract))
                            f.one(dve.tensor_scalar(delta[:], delta[:], 0.50001, 1e-30, ALU.mult, ALU.add))
                            apart(dve, spare)
                            with dve.Fori(0, BISECT) as i:
                                k = Count(dve, v_bis, FSTEP * b + 3 + BSTEP * i)
                                k.one(dve.tensor_tensor(mid[:], lo[:], delta[:], ALU.add))
                                for j in range(TJ):
                                    k.step(dve.tensor_scalar(junk[:, j, :], sc[:, j, :], mid[:, j:j + 1], None, ALU.is_ge, ALU.add,
                                                             accum_out=cnt[:, j:j + 1]))
                                k.settle()
                                k.one(dve.scalar_tensor_tensor(out=up[:], in0=cnt[:], scalar=S / 2 - 0.5, in1=delta[:],
                                                               op0=ALU.is_ge, op1=ALU.mult))
                                k.step(dve.tensor_tensor(lo[:], lo[:], up[:], ALU.add))
                                k.one(dve.tensor_scalar(delta[:], delta[:], 0.5, None, ALU.mult))
                                assert k.n == BSTEP
                            f.n += BSTEP * BISECT
                            f.one(dve.tensor_copy(thr[:], lo[:]))
                            assert f.n == FSTEP
                            apart(dve, spare)
                        with dve.Else():
                            dve.sem_inc(v_bis, FSTEP)
                        for j in range(TJ):
                            dve.scalar_tensor_tensor(out=ms[:, j, :], in0=sc[:, j, :], scalar=thr[:, j:j + 1], in1=sc[:, j, :],
                                                     op0=ALU.is_ge, op1=ALU.mult).then_inc(v_ms.sem, 1)
                        for j in range(0, TJ, 2):
                            dve.wait_ge(t_eT.sem, t_eT.nth(b, j + 1))
                            dve.wait_ge(t_o.sem, t_o.nth(b, j - 1) if j else t_o.before(b))
                            dve.tensor_copy(eT[:, 0], bank[1][:].rearrange("p (c q) -> p c q", c=TJ)).then_inc(v_eT.sem, 1)
                        dve.wait_ge(a_e.sem, a_e.nth(b))
                        c.one(dve.reciprocal(rinv[:], rsum[:]))
                        dve.wait_ge(g_hb.sem, g_hb.nth(b))
                        dve.wait_ge(t_o.sem, t_o.nth(b))
                        for j in range(TJ):
                            dve.scalar_tensor_tensor(out=hrow[:, j, :], in0=bank[0][:, ts(j, D)], scalar=rinv[:, j:j + 1],
                                                     in1=hb[:, j, :], op0=ALU.mult, op1=ALU.add).then_inc(v_h1.sem, 1)
                        dve.wait_ge(v_h1.sem, v_h1.nth(b))
                        st, mv, rs = tiny[2]
                        stats(dve, c, hrow, st, mv, v_st2)
                        dve.wait_ge(g_rs2.sem, g_rs2.nth(b))
                        centre(dve, c, hrow, mv, rs, xn2)
                        c.settle()
                        dve.sem_inc(v_xn2.sem, 1)
                        dve.wait_ge(t_gate.sem, t_gate.nth(b))
                        c.one(dve.tensor_copy(gate[:], bank[4][:, 0:TJ * NE].rearrange("p (j e) -> p j e", j=TJ)))
                        apart(dve, spare)
                        for j in range(TJ):
                            c.step(dve.max(top[:, j, :], gate[:, j, :]))
                        c.settle()
                        c.step(dve.tensor_tensor(gd[:], gate[:], bc(top[:, :, 0:1], [P, TJ, NE]), ALU.subtract))
                        c.one(dve.tensor_tensor(gm[:], gate[:], bc(top[:, :, 1:2], [P, TJ, NE]), ALU.is_ge))
                        dve.sem_inc(v_gd.sem, 1)
                        dve.wait_ge(a_ge.sem, a_ge.nth(b))
                        c.one(dve.tensor_tensor(gm[:], ge[:], gm[:], ALU.mult))
                        c.one(dve.tensor_reduce(gsum[:], gm[:], AX_X, ALU.add))
                        c.one(dve.reciprocal(grec[:], gsum[:]))
                        c.one(dve.tensor_tensor(comb[:], gm[:], bc(grec[:].unsqueeze(2), [P, TJ, NE]), ALU.mult))
                        split3(dve, c, comb[:], cres[:], [c24[:, :, k, :] for k in range(3)])
                        dve.sem_inc(v_c24.sem, 1)
                        dve.wait_ge(a_x2T.sem, a_x2T.nth(b))

                        def hidden(e):
                            dve.wait_ge(t_h1.sem, t_h1.nth(b, e + 1))
                            dve.wait_ge(t_w2.sem, t_w2.nth(b, e - 1) if e > 1 else t_w2.before(b))
                            dve.tensor_scalar(hid[:, e % 2, 1, :], bank[7][:], 0.0, None, ALU.max).then_inc(v_hid.sem, 1)

                        for e in range(NE):
                            dve.wait_ge(t_bc.sem, t_bc.nth(b, e + 1))
                            dve.wait_ge(t_h1.sem, t_h1.nth(b, e - 1) if e > 1 else t_h1.before(b))
                            dve.tensor_tensor(xe[:, e % 2, :], x2T[:], bank[5][0:D + 1, :], ALU.mult).then_inc(v_xe.sem, 1)
                            if e:
                                hidden(e - 1)
                        hidden(NE - 1)
                        dve.wait_ge(t_w2.sem, t_w2.nth(b))
                        dve.tensor_tensor(hrow, hrow, tiled(bank[4][:, 0:ROW]), ALU.add).then_inc(v_h2.sem, 1)
                        dve.wait_ge(v_h2.sem, v_h2.nth(b))
                        st, mv, rs = tiny[3]
                        stats(dve, c, hrow, st, mv, v_st3)
                        dve.wait_ge(g_rs3.sem, g_rs3.nth(b))
                        centre(dve, c, hrow, mv, rs, u[:, bass.ds(TJ * b, TJ), :])
                        c.settle()
                        assert c.n == VSTEP, c.n

        with ExitStack() as own:
            def tmp(name, shape, dt=F32):
                return own.enter_context(nc.sbuf_tensor(name, shape, dt))

            skew = [tmp(f"skew{r}", [P, HG, TW]) for r in range(2)]
            skew_in = [sem("skew_in_even"), sem("skew_in_odd")]
            t_y, a_gy = Signal(sem("t_y")), Signal(sem("a_gy"))
            back = tmp("back", [P, NB * TJ, D])
            flip = tmp("flip", [P, P])
            cols = [tmp(f"cols{r}", [P, NB * TJ, HG]) for r in range(2)]
            v_cols = Signal(sem("v_cols"))
            t_flip, a_back, g_flip = Signal(sem("t_flip")), Signal(sem("a_back")), sem("g_flip")
            FL = S // D

            with nc.Block() as block:
                @block.sync
                def _(sp):
                    with sp.Fori(0, D // HG // 2) as i:
                        for r in range(2):
                            g = 2 * i + r
                            sp.wait_ge(t_y.sem, t_y.before(g) - r)
                            src = bass.AP(taps, g * (HG * KROW) + 1, [[1, P], [KROW, HG], [1, TW]])
                            sp.dma_start(skew[r][:], src).then_inc(skew_in[r], 16)

                @block.gpsimd
                def _(pool):
                    pool.memset(flip[:], 0.0).then_inc(g_flip, 1)
                    pool.wait_ge(g_flip, 1)
                    pool.affine_select(out=flip[:], in_=flip[:], compare_op=ALU.not_equal, fill=1.0, base=1 - P,
                                       pattern=[[1, P]], channel_multiplier=1).then_inc(g_flip, 1)

                @block.tensor
                def _(pe):
                    t_flip.grant(pe)
                    pe.wait_ge(g_flip, 2)
                    with pe.Fori(0, NB * TJ // FL // 2) as i:
                        for r in range(2):
                            n = 2 * i + r
                            pe.wait_ge(a_back.sem, a_back.before(n) - r)
                            pe.matmul(bank[2 + r][:], flip[:], u[:, bass.ds(n * FL, FL), :], start=True, stop=True)\
                              .then_inc(t_flip.sem, 1)
                    pe.wait_ge(a_back.sem, a_back.before(NB * TJ // FL))
                    t_y.grant(pe)
                    with pe.Fori(0, D // HG // 2) as i:
                        for r in range(2):
                            g = 2 * i + r
                            pe.wait_ge(skew_in[r], 16 * i + 16)
                            pe.wait_ge(v_cols.sem, v_cols.nth(g))
                            pe.wait_ge(a_gy.sem, a_gy.before(g) - r)
                            for hh in range(HG):
                                for lc in range(TJ):
                                    for s in range(TJ):
                                        at = P * (TJ - 1 + lc - s)
                                        last = pe.matmul(bank[r][:, ts(TJ * hh + lc, NB)], skew[r][:, hh, at:at + P],
                                                         cols[r][:, s::TJ, hh], start=(s == 0), stop=(s == TJ - 1))
                            last.then_inc(t_y.sem, 1)

                @block.vector
                def _(dve):
                    v_cols.grant(dve)
                    dve.wait_ge(a_back.sem, a_back.before(NB * TJ // FL))
                    with dve.Fori(0, D // HG // 2) as i:
                        for r in range(2):
                            g = 2 * i + r
                            dve.wait_ge(t_y.sem, t_y.before(g) - r)
                            dve.tensor_copy(cols[r][:], back[:, :, bass.ds(g * HG, HG)]).then_inc(v_cols.sem, 1)

                @block.scalar
                def _(act):
                    a_back.grant(act)
                    with act.Fori(0, NB * TJ // FL // 2) as i:
                        for r in range(2):
                            n = 2 * i + r
                            act.wait_ge(t_flip.sem, t_flip.nth(n))
                            act.activation(back[:, bass.ds(n * FL, FL), :],
                                           bank[2 + r][:].rearrange("p (t d) -> p t d", d=D), ACT.Copy).then_inc(a_back.sem, 1)
                    a_gy.grant(act)
                    with act.Fori(0, D // HG // 2) as i:
                        for r in range(2):
                            g = 2 * i + r
                            act.wait_ge(t_y.sem, t_y.nth(g))
                            src = bank[r][:, 0:HG * TJ * NB].rearrange("p (h l b) -> p h l b", h=HG, l=TJ)
                            dst = gy[:, :, :, bass.ds(g * HG, HG)].rearrange("p b l h -> p h l b")
                            act.activation(dst, src, ACT.Gelu).then_inc(a_gy.sem, 1)

        with ExitStack() as own:
            def tmp(name, shape, dt=F32):
                return own.enter_context(nc.sbuf_tensor(name, shape, dt))

            def signals(names, each=1):
                return (Signal(sem(n), each) for n in names.split())

            power = tmp("power_f", [P, TJ])
            tiny = [[tmp(f"{n}f{k}", [P, TJ] + s) for n, s in (("st", [6]), ("mv", [2]), ("rs", []))] for k in range(2)]
            gT = tmp("gT", [D + 1, S])
            sg, z, r_, rn, rg, xn = (tmp(n, [P, TJ, D]) for n in ("sg", "z", "r_", "rn", "rg", "xn_f"))
            rowsT = tmp("rowsT", [P, S])
            lg, best, off = tmp("lg", [P, TJ, NX]), tmp("best", [P, TJ, 8]), tmp("off", [P, TJ, NX])
            hid = tmp("hid_f", [P, XC, S])
            y = [tmp(f"y{r}", [P, TJ, D]) for r in range(2)]
            t_gT, t_glu, t_xT, t_lg, t_off, t_y = signals("t_gT t_glu t_xT_f t_lg t_off t_out_f")
            a_gT, a_sg, a_xT, a_off = signals("a_gT a_sg a_xT_f a_off")
            v_r, v_st, v_rn, v_h3, v_st4, v_xn, v_off, v_y, v_z = signals(
                "v_r v_st_f v_rn v_h3 v_st4 v_xn_f v_off v_y v_z")
            g_rs, g_rg, g_rs4 = signals("g_rs_f g_rg g_rs4")
            t_hid = Signal(sem("t_hid_f"), XC)
            a_hid, v_hid = signals("a_hid_f v_hid_f", XC // 2)
            y_out = [sem("y_out_even"), sem("y_out_odd")]
            v_step, g_step, ready = sem("v_step_f"), sem("g_step_f"), sem("ready_f")
            VSTEP, GSTEP = 32, 3

            with nc.Block() as block:
                @block.sync
                def _(sp):
                    with sp.Fori(0, NB // 2) as i:
                        for r in range(2):
                            b = 2 * i + r
                            sp.wait_ge(v_y.sem, v_y.nth(b))
                            sp.dma_start(out[bass.ds(b, 1)].rearrange("a (j p) d -> p (a j) d", p=P), y[r][:])\
                              .then_inc(y_out[r], 16)
                    for r in range(2):
                        sp.wait_ge(y_out[r], 16 * (NB // 2) + 16)

                @block.gpsimd
                def _(pool):
                    for k, (t, value) in enumerate(((power[:], -0.5), (gT[D:D + 1, :], 1.0), (rowsT[:], 0.0),
                                                    (rowsT[D:D + 1, :], 1.0))):
                        pool.memset(t, value).then_inc(ready, 1)
                        pool.wait_ge(ready, k + 1)
                    for s in (g_rs, g_rg, g_rs4):
                        s.grant(pool)
                    with pool.Fori(0, NB) as b:
                        c = Count(pool, g_step, GSTEP * b)
                        rstd(pool, c, v_st, b, tiny[0][1], tiny[0][2], power, g_rs)
                        pool.wait_ge(v_rn.sem, v_rn.nth(b))
                        c.one(pool.tensor_tensor(rg[:], rn[:], bc(gam1[:].unsqueeze(1), [P, TJ, D]), ALU.mult))
                        pool.tensor_tensor(rg[:], rg[:], bc(bet1[:].unsqueeze(1), [P, TJ, D]), ALU.add).then_inc(g_rg.sem, 1)
                        rstd(pool, c, v_st4, b, tiny[1][1], tiny[1][2], power, g_rs4)
                        assert c.n == GSTEP, c.n

                @block.scalar
                def _(act):
                    for s in (a_gT, a_sg, a_xT, a_off, a_hid):
                        s.grant(act)
                    act.wait_ge(ready, 4)
                    with act.Fori(0, NB) as b:
                        act.wait_ge(t_gT.sem, t_gT.nth(b))
                        act.activation(gT[0:D, :], bank[0][0:D, :], ACT.Copy).then_inc(a_gT.sem, 1)
                        act.wait_ge(t_glu.sem, t_glu.nth(b))
                        act.wait_ge(v_r.sem, v_r.before(b))
                        act.activation(sg[:], bank[1][:].rearrange("p (j f) -> p j f", j=TJ)[:, :, D:2 * D], ACT.Sigmoid)\
                           .then_inc(a_sg.sem, 1)
                        act.wait_ge(t_xT.sem, t_xT.nth(b))
                        act.activation(rowsT[0:D, :], bank[2][0:D, :], ACT.Copy).then_inc(a_xT.sem, 1)
                        act.wait_ge(t_off.sem, t_off.nth(b))
                        act.activation(rowsT[96:P, :], bank[3][0:NX, :], ACT.Copy).then_inc(a_off.sem, 1)
                        for k in range(0, XC, 2):
                            act.wait_ge(t_hid.sem, t_hid.nth(b, k + 1))
                            act.wait_ge(t_y.sem, t_y.before(b))
                            act.activation(hid[:, k, :], bank[4 + k][:], ACT.Relu).then_inc(a_hid.sem, 1)

                @block.tensor
                def _(pe):
                    for s in (t_gT, t_glu, t_xT, t_lg, t_off, t_y, t_hid):
                        s.grant(pe)
                    pe.wait_ge(ready, 4)
                    with pe.Fori(0, NB) as b:
                        pe.wait_ge(v_z.sem, v_z.nth(b))
                        pe.wait_ge(v_y.sem, v_y.before(b))
                        apart(pe, spare)
                        for j in range(TJ):
                            last = pe.transpose(bank[0][0:D, ts(j, P)], z[:, j, :], identf[:])
                        last.then_inc(t_gT.sem, 1)
                        pe.wait_ge(a_gT.sem, a_gT.nth(b))
                        pe.wait_ge(v_r.sem, v_r.before(b))
                        for j in range(TJ):
                            last = pe.matmul(bank[1][:, ts(j, 2 * D)], gT[:, ts(j, P)], Wglu[:], start=True, stop=True)
                        last.then_inc(t_glu.sem, 1)
                        pe.wait_ge(v_xn.sem, v_xn.nth(b))
                        apart(pe, spare)
                        for j in range(TJ):
                            last = pe.transpose(bank[2][0:D, ts(j, P)], xn[:, j, :], identf[:])
                        last.then_inc(t_xT.sem, 1)
                        pe.wait_ge(a_xT.sem, a_xT.nth(b))
                        for j in range(TJ):
                            last = pe.matmul(bank[3][:, ts(j, NX)], rowsT[0:D + 1, ts(j, P)], Wr[:], start=True, stop=True)
                        last.then_inc(t_lg.sem, 1)
                        pe.wait_ge(v_off.sem, v_off.nth(b))
                        apart(pe, spare)
                        for j in range(TJ):
                            last = pe.transpose(bank[3][0:NX, ts(j, P)], off[:, j, :], identf[:])
                        last.then_inc(t_off.sem, 1)
                        pe.wait_ge(a_off.sem, a_off.nth(b))
                        for k in range(XC):
                            pe.matmul(bank[4 + k][:], Wx1[:, ts(k, P)], rowsT[:], start=True, stop=True).then_inc(t_hid.sem, 1)
                        pe.wait_ge(a_hid.sem, a_hid.nth(b))
                        pe.wait_ge(v_hid.sem, v_hid.nth(b))
                        for j in range(TJ):
                            pe.matmul(bank[0][:, ts(j, D)], rowsT[:, ts(j, P)], bx2[:], start=True, stop=False)
                            for k in range(XC):
                                last = pe.matmul(bank[0][:, ts(j, D)], hid[:, k, ts(j, P)], Wx2[:, k, :],
                                                 start=False, stop=(k == XC - 1))
                        last.then_inc(t_y.sem, 1)

                @block.vector
                def _(dve):
                    for s in (v_r, v_st, v_rn, v_h3, v_st4, v_xn, v_off, v_y, v_hid, v_z):
                        s.grant(dve)
                    for r in range(2):
                        dve.sem_inc(y_out[r], 16)
                    dve.wait_ge(ready, 4)
                    with dve.Fori(0, NB // 2) as i:
                        for r in range(2):
                            b = 2 * i + r
                            c = Count(dve, v_step, VSTEP * b)
                            hrow = tiled(h[:, ts(b, ROW)])
                            dve.wait_ge(t_gT.sem, t_gT.before(b))
                            dve.tensor_copy(z[:], gy[:, bass.ds(b, 1)].rearrange("p a l h -> p (a l) h")).then_inc(v_z.sem, 1)
                            dve.wait_ge(a_sg.sem, a_sg.nth(b))
                            c.one(dve.tensor_tensor(r_[:], bank[1][:].rearrange("p (j f) -> p j f", j=TJ)[:, :, 0:D], sg[:], ALU.mult))
                            dve.tensor_tensor(r_[:], r_[:], u[:, bass.ds(TJ * b, TJ), :], ALU.add).then_inc(v_r.sem, 1)
                            dve.wait_ge(v_r.sem, v_r.nth(b))
                            st, mv, rs = tiny[0]
                            stats(dve, c, r_, st, mv, v_st)
                            dve.wait_ge(g_rs.sem, g_rs.nth(b))
                            centre(dve, c, r_, mv, rs, rn)
                            c.settle()
                            dve.sem_inc(v_rn.sem, 1)
                            dve.wait_ge(g_rg.sem, g_rg.nth(b))
                            dve.tensor_tensor(hrow, hrow, rg[:], ALU.add).then_inc(v_h3.sem, 1)
                            dve.wait_ge(v_h3.sem, v_h3.nth(b))
                            st, mv, rs = tiny[1]
                            stats(dve, c, hrow, st, mv, v_st4)
                            dve.wait_ge(g_rs4.sem, g_rs4.nth(b))
                            centre(dve, c, hrow, mv, rs, xn)
                            c.settle()
                            dve.sem_inc(v_xn.sem, 1)
                            dve.wait_ge(t_lg.sem, t_lg.nth(b))
                            c.one(dve.tensor_copy(lg[:], bank[3][:, 0:TJ * NX].rearrange("p (j e) -> p j e", j=TJ)))
                            apart(dve, spare)
                            for j in range(TJ):
                                c.step(dve.max(best[:, j, :], lg[:, j, :]))
                            c.settle()
                            for j in range(TJ):
                                c.step(dve.tensor_scalar(off[:, j, :], lg[:, j, :], best[:, j, 0:1], 1.0, ALU.is_ge, ALU.subtract))
                            c.settle()
                            dve.sem_inc(v_off.sem, 1)
                            for k in range(1, XC, 2):
                                dve.wait_ge(t_hid.sem, t_hid.nth(b, k + 1))
                                dve.tensor_scalar(hid[:, k, :], bank[4 + k][:], 0.0, None, ALU.max).then_inc(v_hid.sem, 1)
                            dve.wait_ge(t_y.sem, t_y.nth(b))
                            dve.wait_ge(y_out[r], 16 * i + 16)
                            dve.scalar_tensor_tensor(out=y[r][:], in0=tiled(bank[0][:, 0:ROW]), scalar=0.0, in1=hrow,
                                                     op0=ALU.max, op1=ALU.add).then_inc(v_y.sem, 1)
                            assert c.n == VSTEP, c.n


def kernel(**inputs):
    import numpy as np
    import concourse.bacc as bacc
    from concourse.bass_utils import run_bass_kernel_spmd

    v = {k: np.asarray(a) for k, a in inputs.items()}
    L = {k: v[k] for k in ("x", "itok_BS_0_255", "itok_BS_0_511", "itok_BS_0_127", "itok_BS_0_63", "itok_BS_0_3")}
    et = np.zeros((96, 4, P), np.float32)
    for t, (name, chunk, col) in enumerate((("et", 0, 0), ("fc", 0, 64), ("sc", 2, 0), ("of", 3, 0), ("tt", 1, 0), ("rc", 1, 64))):
        e = v[f"L0_tok_E_{name}"]
        et[16 * t:16 * t + 16, chunk, col:col + e.shape[0]] = e.T
    L["Et"] = et.reshape(96, 4 * P)
    L["WT"] = v["L0_tok_W"].T
    L.update(tokb=v["L0_tok_b"], gam0=v["L0_tok_gamma"], bet0=v["L0_tok_beta"])
    L.update(Wqkv=v["L0_attn_W_qkv"], bqkv=v["L0_attn_b_qkv"], Wo=v["L0_attn_W_out"], bo=v["L0_attn_b_out"])
    L.update(WgT=v["L0_ffn_Wg"].T, bg=v["L0_ffn_bg"], W1T=v["L0_ffn_W1"].reshape(-1, D).T, b1=v["L0_ffn_b1"].reshape(-1),
             W2T=v["L0_ffn_W2"].transpose(0, 2, 1).reshape(-1, D), b2=v["L0_ffn_b2"])
    L.update(ldt=v["L1_attn_log_dt"], ArlT=v["L1_attn_A_real_log"].T, AimT=v["L1_attn_A_imag"].T,
             CreT=v["L1_attn_C_re"].transpose(2, 0, 1).reshape(NS, -1), CimT=v["L1_attn_C_im"].transpose(2, 0, 1).reshape(NS, -1),
             skip=v["L1_attn_D"], WgluT=v["L1_attn_W_out"].T, bglu=v["L1_attn_b_out"], gam1=v["L1_attn_gamma"],
             bet1=v["L1_attn_beta"])
    L.update(WrT=v["L1_ffn_router_w"].T, br=v["L1_ffn_router_b"], Wx1=v["L1_ffn_W1"].transpose(1, 0, 2).reshape(D, -1),
             bx1=v["L1_ffn_b1"].reshape(-1), Wx2=v["L1_ffn_W2"].reshape(-1, D), bx2=v["L1_ffn_b2"])
    nc = bacc.Bacc("TRN2", target_bir_lowering=False, num_devices=1)
    arrays, A = {}, {}
    for name, a in L.items():
        arrays[f"in_{name}"] = a = np.ascontiguousarray(a)
        A[name] = nc.dram_tensor(f"in_{name}", a.shape, mybir.dt.from_np(a.dtype), kind="ExternalInput").ap()
    out = nc.dram_tensor("out_0", (NB, S, D), F32, kind="ExternalOutput").ap()
    tower(nc, A, out)
    return run_bass_kernel_spmd(nc, [arrays], core_ids=[0]).results[0]["out_0"]
```

```python
from contextlib import ExitStack

import concourse.bass as bass
from concourse import mybir

F32 = mybir.dt.float32
BF16 = mybir.dt.bfloat16
I32 = mybir.dt.int32
U32 = mybir.dt.uint32
ALU = mybir.AluOpType
ACT = mybir.ActivationFunctionType
AX_X = mybir.AxisListType.X
ts = bass.ts

P = 128
NB, S, D = 16, 512, 64
TJ = S // P
ROW = TJ * D
NE, HID = 8, 256
HH = HID // P
NX, XH = 32, 16
XC = NX * XH // P
NS = 32
NHI, NLO = 16, 32
KROW = 2 * S
TW = (2 * TJ - 1) * P
HG = 4
SEARCH = 5
OWN = 1
AIM = S / 2 - 4.5
BISECT = 32
FAR = 1e30
MAGIC = 1.5 * 2.0 ** 23
TWO_PI_HI = 6.28125
TWO_PI_LO = 0.0019353071795864769
PI_SAFE = 3.1415925
BIG = 2.0 ** 60
EPS = 1e-5


class Count:

    def __init__(self, eng, sem, base=0):
        self.eng, self.sem, self.base, self.n = eng, sem, base, 0

    def step(self, ins):
        ins.then_inc(self.sem, 1)
        self.n += 1

    def settle(self):
        self.eng.wait_ge(self.sem, self.base + self.n)

    def one(self, ins):
        self.step(ins)
        self.settle()


class Signal:

    def __init__(self, sem, each=1):
        self.sem, self.each = sem, each

    def grant(self, eng):
        eng.sem_inc(self.sem, self.each)

    def nth(self, b, n=None):
        return self.each * b + self.each + (self.each if n is None else n)

    def before(self, b):
        return self.each * b + self.each


def apart(eng, spare):
    eng.sem_inc(spare, 1)


def bc(ap, shape):
    return ap.to_broadcast(shape)


def split3(dve, c, x, rest, parts):
    a, b, last = parts
    c.one(dve.tensor_copy(a, x))
    c.one(dve.tensor_tensor(rest, x, a, ALU.subtract))
    c.one(dve.tensor_copy(b, rest))
    c.one(dve.tensor_tensor(x, rest, b, ALU.subtract))
    c.one(dve.tensor_copy(last, x))


def tower(nc, A, out):
    with ExitStack() as ctx:
        def sb(name, shape, dt=F32):
            return ctx.enter_context(nc.sbuf_tensor(name, shape, dt))

        def sem(name):
            return ctx.enter_context(nc.semaphore(name))

        bank = [ctx.enter_context(nc.psum_tensor(f"bank{i}", [P, 512], F32)) for i in range(8)]
        taps = nc.dram_tensor("taps", (D, KROW), F32, kind="Internal")

        h = sb("h", [P, NB * ROW])
        u = sb("u", [P, NB * TJ, D])
        gy = sb("gy", [P, NB, TJ, D])
        identf = sb("identf", [P, P])
        identb = sb("identb", [P, P], BF16)
        WT = sb("WT", [96, D])
        Et = sb("Et", [96, 4, P])
        table = sb("table", [P, 4, 3, D], BF16)
        gam0, bet0 = sb("gam0", [P, D]), sb("bet0", [P, D])
        gam1, bet1 = sb("gam1", [P, D]), sb("bet1", [P, D])
        tokb = sb("tokb", [P, D])
        Wqkv = sb("Wqkv", [P, 3 * D])
        Wo = sb("Wo", [D, D])
        bo = sb("bo", [P, D])
        Wg = sb("Wg", [D + 1, NE])
        W1 = sb("W1", [P, NE * HID])
        W2 = sb("W2", [P, NE * HH, D])
        b2f = sb("b2f", [3 * NE, D])
        b2p = sb("b2p", [3 * NE, 3, D], BF16)
        sel = sb("sel", [P, NE, D + 1], BF16)
        Wglu = sb("Wglu", [D + 1, 2 * D])
        Wr = sb("Wr", [D + 1, NX])
        Wx1 = sb("Wx1", [P, XC * P])
        Wx2 = sb("Wx2", [P, XC, D])
        bx2 = sb("bx2", [P, D])

        w_in = sem("w_in")
        spare = sem("spare")
        consts = sem("consts")
        NW = 32
        LOADS = [
            (WT[:], A["WT"]), (Et[:], A["Et"].rearrange("k (c v) -> k c v", c=4)),
            (gam0[:], A["gam0"].partition_broadcast(P)), (bet0[:], A["bet0"].partition_broadcast(P)),
            (gam1[:], A["gam1"].partition_broadcast(P)), (bet1[:], A["bet1"].partition_broadcast(P)),
            (tokb[:], A["tokb"].partition_broadcast(P)),
            (Wqkv[0:D, :], A["Wqkv"]),
            (Wo[:], A["Wo"]), (bo[:], A["bo"].partition_broadcast(P)),
            (Wg[0:D, :], A["WgT"]), (Wg[D:D + 1, :], A["bg"].unsqueeze(0)),
            (W1[0:D, :], A["W1T"]),
            (W2[:], A["W2T"].rearrange("(c p) d -> p c d", p=P)),
            (Wglu[0:D, :], A["WgluT"]), (Wglu[D:D + 1, :], A["bglu"].unsqueeze(0)),
            (Wr[0:D, :], A["WrT"]), (Wr[D:D + 1, :], A["br"].unsqueeze(0)),
            (Wx2[:], A["Wx2"].rearrange("(c p) d -> p c d", p=P)),
        ] + [(b2f[NE * i:NE * i + NE, :], A["b2"]) for i in range(3)]

        with ExitStack() as own:
            def tmp(name, shape, dt=F32):
                return own.enter_context(nc.sbuf_tensor(name, shape, dt))

            onesf = tmp("onesf", [P, P])
            absw, rowsum, half, nhalf, scl = (tmp(n, [96, k]) for n, k in
                                              (("absw", D), ("rowsum", 1), ("half", 1), ("nhalf", 1), ("scl", 1)))
            wpos, wneg, weff = tmp("wpos", [96, D]), tmp("wneg", [96, D]), tmp("weff", [96, D])
            tabf, tabr = tmp("tabf", [P, 4, D]), tmp("tabr", [P, 4, D])
            b2r = tmp("b2r", [3 * NE, D])
            M = 2 * NS
            ldt, arl, aim = tmp("ldt", [M, D]), tmp("arl", [M, D]), tmp("aim", [M, D])
            cre, cim = tmp("cre", [M, 2, D]), tmp("cim", [M, 2, D])
            skip = tmp("skip", [1, D])
            ki = tmp("ki", [M, NLO + NHI], I32)
            kf = tmp("kf", [M, NLO + NHI])
            phase, sgn = tmp("phase", [M, 1]), tmp("sgn", [M, 1])
            dt_, are, w, a = (tmp(n, [M, D]) for n in ("dt_", "are", "w", "a"))
            NK = NLO + NHI
            theta, turns, mag = (tmp(n, [M, D, NK]) for n in ("theta", "turns", "mag"))
            th2, tn2, sc2 = (tmp(n, [M, 2, D]) for n in ("th2", "tn2", "sc2"))
            q1, q2, q3, q4, em = (tmp(n, [M, D]) for n in ("q1", "q2", "q3", "q4", "em"))
            er, ei, yr, yi = (tmp(n, [M, D]) for n in ("er", "ei", "yr", "yi"))
            cr, ci, cs = tmp("cr", [M, 2, D]), tmp("ci", [M, 2, D]), tmp("cs", [M, 2, D])
            hi_sw = tmp("hi_sw", [M, D, NHI])
            left, lt2 = tmp("left", [M, 2, D, NHI]), tmp("lt2", [M, 2, D, NHI])
            lo_rev = tmp("lo_rev", [M, D, NLO])
            lbuf, mbuf = tmp("lbuf", [M, 2, HG, NHI]), tmp("mbuf", [M, 2, HG, NLO])
            rows = tmp("rows", [NHI, 2, D, NLO])
            p_in = sem("p_in")
            g_clear = sem("g_clear")
            PLOADS = [(cre[NS * r:NS * r + NS], A["CreT"].rearrange("n (c h) -> n c h", c=2)) for r in range(2)]
            PLOADS += [(cim[NS * r:NS * r + NS], A["CimT"].rearrange("n (c h) -> n c h", c=2)) for r in range(2)]
            PLOADS += [(arl[NS * r:NS * r + NS, :], A["ArlT"]) for r in range(2)]
            PLOADS += [(aim[NS * r:NS * r + NS, :], A["AimT"]) for r in range(2)]
            PLOADS += [(ldt[:], A["ldt"].partition_broadcast(M)), (skip[:], A["skip"].unsqueeze(0))]

            g_step, v_step = sem("g_step_setup"), sem("v_step_setup")
            a_dt, a_tanh, a_sin2, a_mag, a_sin = (sem(n) for n in ("a_dt", "a_tanh", "a_sin2", "a_mag", "a_sin"))
            v_a, v_w2, v_prod, v_theta, v_abs, v_weff = (
                sem(n) for n in ("v_a", "v_w2", "v_prod", "v_theta", "v_abs", "v_weff"))
            t_sum, t_tab, t_bx = sem("t_sum"), sem("t_tab"), sem("t_bx")
            v_left, v_lbuf, v_mbuf, t_taps, v_rows, taps_out = (
                sem(n) for n in ("v_left", "v_lbuf", "v_mbuf", "t_taps", "v_rows", "taps_out"))

            with nc.Block() as block:
                @block.sync
                def _(sp):
                    for dst, src in PLOADS:
                        sp.dma_start(dst, src).then_inc(p_in, 16)
                    for dst, src in LOADS:
                        sp.dma_start(dst, src).then_inc(w_in, 16)
                    sp.wait_ge(g_clear, 1)
                    sp.dma_start(Wx1[0:D, :], A["Wx1"]).then_inc(w_in, 16)
                    sp.dma_start(Wx1[D:D + 1, :], A["bx1"].unsqueeze(0)).then_inc(w_in, 16)
                    sp.dma_start(Wqkv[D:D + 1, :], A["bqkv"].unsqueeze(0)).then_inc(w_in, 16)
                    sp.dma_start(W1[D:D + 1, :], A["b1"].unsqueeze(0)).then_inc(w_in, 16)
                    sp.dma_start(bx2[96:P, :], A["bx2"]).then_inc(w_in, 16)
                    sp.wait_ge(v_rows, 2 * D // HG + 1)
                    sp.dma_start(taps.ap().rearrange("h (c a b) -> a c h b", c=2, a=NHI)[:, 0], rows[:, 0])\
                      .then_inc(taps_out, 16)
                    sp.dma_start(taps.ap().rearrange("h (c a b) -> a c h b", c=2, a=NHI)[:, 1], rows[:, 1])\
                      .then_inc(taps_out, 16)
                    sp.wait_ge(taps_out, 32)

                @block.gpsimd
                def _(pool):
                    c = Count(pool, g_step)
                    c.one(pool.memset(identf[:], 0.0))
                    c.one(pool.memset(identb[:], 0.0))
                    c.one(pool.memset(sel[:], 0.0))
                    c.one(pool.memset(sel[0:3 * NE], 1.0))
                    c.one(pool.memset(Wqkv[D:P, :], 0.0))
                    c.one(pool.memset(W1[D:P, :], 0.0))
                    c.one(pool.memset(onesf[:], 1.0))
                    c.one(pool.memset(phase[0:NS, :], 0.25))
                    c.one(pool.memset(phase[NS:M, :], 0.0))
                    c.one(pool.memset(sgn[0:NS, :], 1.0))
                    c.one(pool.memset(sgn[NS:M, :], -1.0))
                    c.one(pool.memset(Wx1[:], 0.0))
                    c.one(pool.iota(ki[:, 0:NLO], pattern=[[1, NLO]], base=0, channel_multiplier=0))
                    c.one(pool.iota(ki[:, NLO:NK], pattern=[[NLO, NHI]], base=0, channel_multiplier=0))
                    c.settle()
                    for m in (identf, identb):
                        c.step(pool.affine_select(out=m[:], in_=m[:], compare_op=ALU.not_equal, fill=1.0, base=0,
                                                  pattern=[[-1, P]], channel_multiplier=1))
                    for lo in (0, NE, 2 * NE):
                        c.one(pool.affine_select(out=sel[0:3 * NE], in_=sel[0:3 * NE], compare_op=ALU.not_equal, fill=2.0, base=-lo,
                                                 pattern=[[-1, NE], [0, D + 1]], channel_multiplier=1))
                    c.one(pool.tensor_scalar(sel[0:3 * NE], sel[0:3 * NE], 1.0, None, ALU.subtract))
                    c.one(pool.tensor_copy(kf[:], ki[:]))
                    c.one(pool.memset(Wx1[96:P, :], BIG))
                    big = Wx1[96:P, :].rearrange("k (e x) -> k e x", x=XH)
                    c.one(pool.affine_select(out=big, in_=big, compare_op=ALU.is_equal, fill=0.0, base=0,
                                             pattern=[[-1, NX], [0, XH]], channel_multiplier=1))
                    pool.memset(bx2[:], 0.0).then_inc(g_clear, 1)
                    pool.wait_ge(w_in, 16 * (len(LOADS) + 5))
                    pool.sem_inc(consts, 1)

                @block.scalar
                def _(act):
                    act.wait_ge(p_in, 16 * len(PLOADS))
                    act.activation(dt_[:], ldt[:], ACT.Exp).then_inc(a_dt, 1)
                    act.activation(are[:], arl[:], ACT.Exp).then_inc(a_dt, 1)
                    act.wait_ge(v_a, 1)
                    act.activation(q1[:], a[:], ACT.Tanh, scale=0.5).then_inc(a_tanh, 1)
                    act.wait_ge(v_prod, 1)
                    act.activation(mag[:], mag[:], ACT.Exp).then_inc(a_mag, 1)
                    act.wait_ge(v_w2, 1)
                    act.activation(sc2[:], th2[:], ACT.Sin).then_inc(a_sin2, 1)
                    act.wait_ge(v_theta, 1)
                    act.activation(theta[:], theta[:], ACT.Sin).then_inc(a_sin, 1)

                @block.tensor
                def _(pe):
                    pe.wait_ge(v_abs, 1)
                    pe.matmul(bank[0][0:96, 0:1], onesf[0:96, 0:96], rowsum[:], start=True, stop=True).then_inc(t_sum, 1)
                    pe.wait_ge(v_weff, 1)
                    for c in range(4):
                        last = pe.matmul(bank[1][:, ts(c, D)], Et[:, c, :], weff[:], start=True, stop=True)
                    last.then_inc(t_tab, 1)
                    pe.wait_ge(consts, 1)
                    pe.matmul(bank[4][:, 0:D], onesf[96:P, :], bx2[96:P, :], start=True, stop=True).then_inc(t_bx, 1)
                    pe.wait_ge(v_left, 1)
                    with pe.Fori(0, D // HG) as g:
                        pe.wait_ge(v_lbuf, g + 1)
                        pe.wait_ge(v_mbuf, 2 * g + 2)
                        apart(pe, spare)
                        for hh in range(HG):
                            for c in range(2):
                                last = pe.matmul(bank[2 + c][0:NHI, ts(hh, NLO)], lbuf[:, c, hh, :], mbuf[:, c, hh, :],
                                                 start=True, stop=True)
                        last.then_inc(t_taps, 1)

                @block.vector
                def _(dve):
                    c = Count(dve, v_step)

                    def reduced(ang, trn, plus):
                        c.one(dve.tensor_scalar(trn, ang, 1.0 / (2.0 * 3.141592653589793), plus, ALU.mult, ALU.add))
                        c.one(dve.tensor_scalar(trn, trn, MAGIC, MAGIC, ALU.add, ALU.subtract))
                        c.one(dve.scalar_tensor_tensor(out=ang, in0=trn, scalar=-TWO_PI_HI, in1=ang,
                                                       op0=ALU.mult, op1=ALU.add))
                        c.one(dve.scalar_tensor_tensor(out=ang, in0=trn, scalar=-TWO_PI_LO, in1=ang,
                                                       op0=ALU.mult, op1=ALU.add))

                    dve.wait_ge(consts, 1)
                    c.one(dve.scalar_tensor_tensor(out=absw[:], in0=WT[:], scalar=-1.0, in1=WT[:],
                                                   op0=ALU.mult, op1=ALU.max))
                    dve.tensor_reduce(rowsum[:], absw[:], AX_X, ALU.add).then_inc(v_abs, 1)
                    dve.wait_ge(t_sum, 1)
                    c.one(dve.tensor_scalar(scl[:], bank[0][0:96, 0:1], 1.0 / (96 * D), None, ALU.mult))
                    c.one(dve.tensor_scalar(half[:], scl[:], 1e-8, 0.5, ALU.add, ALU.mult))
                    c.one(dve.tensor_scalar(nhalf[:], half[:], -1.0, None, ALU.mult))
                    c.step(dve.tensor_scalar(wpos[:], WT[:], half[:], None, ALU.is_gt))
                    c.one(dve.tensor_scalar(wneg[:], WT[:], nhalf[:], None, ALU.is_lt))
                    c.one(dve.tensor_tensor(wpos[:], wpos[:], wneg[:], ALU.subtract))
                    c.one(dve.scalar_tensor_tensor(out=wneg[:], in0=wpos[:], scalar=scl[:], in1=WT[:],
                                                   op0=ALU.mult, op1=ALU.subtract))
                    dve.tensor_tensor(weff[:], wneg[:], WT[:], ALU.add).then_inc(v_weff, 1)
                    dve.wait_ge(t_tab, 1)
                    c.one(dve.tensor_copy(tabf[:].rearrange("p c d -> p (c d)"), bank[1][:, 0:4 * D]))
                    c.one(dve.tensor_tensor(tabf[0:64, 0, :], tabf[0:64, 0, :], tokb[0:64, :], ALU.add))
                    for x, r, parts in ((tabf, tabr, [table[:, :, i, :] for i in range(3)]),
                                        (b2f, b2r, [b2p[:, i, :] for i in range(3)])):
                        split3(dve, c, x[:], r[:], parts)
                    dve.wait_ge(t_bx, 1)
                    c.one(dve.tensor_copy(bx2[D:D + 1, :], bank[4][D:D + 1, 0:D]))
                    dve.wait_ge(a_dt, 2)
                    c.one(dve.tensor_scalar(are[:], are[:], -1.0, None, ALU.mult))
                    c.step(dve.tensor_tensor(w[:], dt_[:], aim[:], ALU.mult))
                    c.one(dve.tensor_tensor(a[:], dt_[:], are[:], ALU.mult))
                    dve.engine_nop().then_inc(v_a, 1)
                    kb = bc(kf[:].unsqueeze(1), [M, D, NK])
                    dve.tensor_tensor(mag[:], bc(a[:].unsqueeze(2), [M, D, NK]), kb, ALU.mult).then_inc(v_prod, 1)
                    c.one(dve.tensor_scalar(th2[:, 0, :], w[:], 0.5, None, ALU.mult))
                    c.one(dve.tensor_scalar(th2[:, 1, :], th2[:, 0, :], 1.0, None, ALU.mult))
                    reduced(th2[:, 0, :], tn2[:, 0, :], 0.0)
                    reduced(th2[:, 1, :], tn2[:, 1, :], 0.25)
                    c.one(dve.tensor_scalar(th2[:, 1, :], th2[:, 1, :], 1.5707963267948966, None, ALU.add))
                    c.one(dve.tensor_scalar(th2[:], th2[:], PI_SAFE, -PI_SAFE, ALU.min, ALU.max))
                    dve.engine_nop().then_inc(v_w2, 1)
                    c.one(dve.tensor_tensor(theta[:], bc(w[:].unsqueeze(2), [M, D, NK]), kb, ALU.mult))
                    reduced(theta[:], turns[:], phase[:, 0:1])
                    c.one(dve.tensor_scalar(q4[:, 0:1], phase[:], 4 * 1.5707963267948966, None, ALU.mult))
                    c.one(dve.tensor_scalar(theta[:], theta[:], q4[:, 0:1], PI_SAFE, ALU.add, ALU.min))
                    c.one(dve.tensor_scalar(theta[:], theta[:], -PI_SAFE, None, ALU.max))
                    dve.engine_nop().then_inc(v_theta, 1)
                    dve.wait_ge(a_tanh, 1)
                    c.one(dve.tensor_scalar(q2[:], q1[:], -1.0, 1.0, ALU.mult, ALU.add))
                    c.one(dve.reciprocal(q3[:], q2[:]))
                    c.one(dve.scalar_tensor_tensor(out=em[:], in0=q1[:], scalar=2.0, in1=q3[:],
                                                   op0=ALU.mult, op1=ALU.mult))
                    dve.wait_ge(a_sin2, 1)
                    c.step(dve.scalar_tensor_tensor(out=q1[:], in0=sc2[:, 0, :], scalar=-2.0, in1=sc2[:, 0, :],
                                                    op0=ALU.mult, op1=ALU.mult))
                    c.one(dve.scalar_tensor_tensor(out=q2[:], in0=sc2[:, 0, :], scalar=2.0, in1=sc2[:, 1, :],
                                                   op0=ALU.mult, op1=ALU.mult))
                    c.one(dve.scalar_tensor_tensor(out=q3[:], in0=q1[:], scalar=1.0, in1=em[:],
                                                   op0=ALU.add, op1=ALU.mult))
                    c.step(dve.tensor_tensor(er[:], q3[:], q1[:], ALU.add))
                    c.one(dve.scalar_tensor_tensor(out=ei[:], in0=em[:], scalar=1.0, in1=q2[:],
                                                   op0=ALU.add, op1=ALU.mult))
                    c.step(dve.tensor_tensor(q1[:], are[:], are[:], ALU.mult))
                    c.one(dve.tensor_tensor(q2[:], aim[:], aim[:], ALU.mult))
                    c.one(dve.tensor_tensor(q3[:], q1[:], q2[:], ALU.add))
                    c.one(dve.reciprocal(q1[:], q3[:]))
                    c.step(dve.tensor_tensor(yr[:], er[:], are[:], ALU.mult))
                    c.step(dve.tensor_tensor(q2[:], ei[:], aim[:], ALU.mult))
                    c.step(dve.tensor_tensor(yi[:], ei[:], are[:], ALU.mult))
                    c.one(dve.tensor_tensor(q4[:], er[:], aim[:], ALU.mult))
                    c.step(dve.tensor_tensor(yr[:], yr[:], q2[:], ALU.add))
                    c.one(dve.tensor_tensor(yi[:], yi[:], q4[:], ALU.subtract))
                    c.step(dve.scalar_tensor_tensor(out=yr[:], in0=yr[:], scalar=2.0, in1=q1[:], op0=ALU.mult, op1=ALU.mult))
                    c.one(dve.scalar_tensor_tensor(out=yi[:], in0=yi[:], scalar=2.0, in1=q1[:], op0=ALU.mult, op1=ALU.mult))
                    yrb, yib = bc(yr[:].unsqueeze(1), [M, 2, D]), bc(yi[:].unsqueeze(1), [M, 2, D])
                    c.step(dve.tensor_tensor(cr[:], cre[:], yrb, ALU.mult))
                    c.one(dve.tensor_tensor(cs[:], cim[:], yib, ALU.mult))
                    c.one(dve.tensor_tensor(cr[:], cr[:], cs[:], ALU.subtract))
                    c.step(dve.tensor_tensor(ci[:], cre[:], yib, ALU.mult))
                    c.one(dve.tensor_tensor(cs[:], cim[:], yrb, ALU.mult))
                    c.one(dve.tensor_tensor(ci[:], ci[:], cs[:], ALU.add))
                    c.step(dve.tensor_scalar(cr[:], cr[:], sgn[:, 0:1], None, ALU.mult))
                    c.one(dve.tensor_scalar(ci[:], ci[:], -1.0, None, ALU.mult))
                    dve.wait_ge(a_mag, 1)
                    dve.wait_ge(a_sin, 1)
                    c.one(dve.tensor_tensor(theta[:], theta[:], mag[:], ALU.mult))
                    c.step(dve.tensor_copy(hi_sw[0:NS], theta[NS:M, :, NLO:NK]))
                    c.step(dve.tensor_copy(hi_sw[NS:M], theta[0:NS, :, NLO:NK]))
                    c.one(dve.tensor_copy(lo_rev[:], theta[:, :, 0:NLO][:, :, ::-1]))
                    for way, src in ((0, 1), (1, 0)):
                        e1, e2 = theta[:, :, NLO:NK], hi_sw[:]
                        if way == 0:
                            e1, e2 = e1[:, :, ::-1], e2[:, :, ::-1]
                        c.step(dve.tensor_tensor(left[:, way], bc(cr[:, src, :].unsqueeze(2), [M, D, NHI]), e1, ALU.mult))
                        c.one(dve.tensor_tensor(lt2[:, way], bc(ci[:, src, :].unsqueeze(2), [M, D, NHI]), e2, ALU.mult))
                        c.one(dve.tensor_tensor(left[:, way], left[:, way], lt2[:, way], ALU.add))
                    dve.engine_nop().then_inc(v_left, 1)
                    with dve.Fori(0, D // HG) as g:
                        dve.tensor_copy(mbuf[:, 0], lo_rev[:, bass.ds(g * HG, HG), :]).then_inc(v_mbuf, 1)
                        dve.tensor_copy(mbuf[:, 1], theta[:, bass.ds(g * HG, HG), 0:NLO]).then_inc(v_mbuf, 1)
                        dve.tensor_copy(lbuf[:], left[:, :, bass.ds(g * HG, HG), :]).then_inc(v_lbuf, 1)
                        dve.wait_ge(t_taps, g + 1)
                        dve.tensor_copy(rows[:, 0, bass.ds(g * HG, HG), :],
                                        bank[2][0:NHI, 0:HG * NLO].rearrange("a (h b) -> a h b", h=HG))\
                           .then_inc(v_rows, 1)
                        dve.tensor_copy(rows[:, 1, bass.ds(g * HG, HG), :],
                                        bank[3][0:NHI, 0:HG * NLO].rearrange("a (h b) -> a h b", h=HG))\
                           .then_inc(v_rows, 1)
                    dve.wait_ge(v_rows, 2 * D // HG)
                    dve.tensor_tensor(rows[0:1, 1, :, 0], rows[0:1, 1, :, 0], skip[:], ALU.add).then_inc(v_rows, 1)

        def stats(dve, c, x, st, mv, done):
            apart(dve, spare)
            for j in range(TJ):
                c.step(dve.bn_stats(st[:, j, :], x[:, j, :]))
            c.settle()
            apart(dve, spare)
            for j in range(TJ):
                last = dve.bn_aggr(mv[:, j, :], st[:, j, :])
                if j < TJ - 1:
                    c.step(last)
            last.then_inc(done.sem, 1)

        def rstd(pool, c, ready, b, mv, rs, power, done):
            pool.wait_ge(ready.sem, ready.nth(b))
            apart(pool, spare)
            c.one(pool.tensor_scalar(rs[:], mv[:, :, 1], EPS, None, ALU.add))
            pool.tensor_tensor(rs[:], rs[:], power[:], ALU.pow).then_inc(done.sem, 1)

        def centre(dve, c, x, mv, rs, dst):
            for j in range(TJ):
                c.step(dve.tensor_scalar(dst[:, j, :], x[:, j, :], mv[:, j, 0:1], rs[:, j:j + 1],
                                         ALU.subtract, ALU.mult))

        def tiled(ap):
            return ap.rearrange("p (j d) -> p j d", j=TJ)

        with ExitStack() as own:
            def tmp(name, shape, dt=F32):
                return own.enter_context(nc.sbuf_tensor(name, shape, dt))

            ids = [tmp(f"ids{i}", [P, 4, S], I32) for i in range(2)]
            onehot = tmp("onehot", [P, 4, S], BF16)
            rowi = tmp("rowi", [P, 2], I32)
            rowf = tmp("rowf", [P, 2])
            st, mv, rs = tmp("st_e", [P, TJ, 6]), tmp("mv_e", [P, TJ, 2]), tmp("rs_e", [P, TJ])
            power = tmp("power_e", [P, TJ])
            xn, xg = tmp("xn_e", [P, TJ, D]), tmp("xg_e", [P, TJ, D])
            ids_in = [sem("ids_in_even"), sem("ids_in_odd")]
            g_row = sem("g_row")
            v_hot, t_z = Signal(sem("v_hot"), 2), Signal(sem("t_z"))
            v_stats, g_rstd = Signal(sem("v_stats_e")), Signal(sem("g_rstd_e"))
            v_norm, g_gain, g_h = Signal(sem("v_norm_e"), TJ), Signal(sem("g_gain_e")), Signal(sem("g_h"))
            g_step, v_step = sem("g_step_e"), sem("v_step_e")
            IDS = [(0, 0, 64, "x"), (0, 64, P, "itok_BS_0_255"), (2, 0, P, "itok_BS_0_511"),
                   (3, 0, P, "itok_BS_0_127"), (1, 0, 64, "itok_BS_0_63"), (1, 64, 68, "itok_BS_0_3")]
            VSTEP, GSTEP = 2 * TJ - 1, 1

            with nc.Block() as block:
                @block.sync
                def _(sp):
                    sp.wait_ge(g_row, 5)
                    with sp.Fori(0, NB // 2) as i:
                        for r in range(2):
                            sp.wait_ge(v_hot.sem, v_hot.before(2 * i))
                            for c, lo, hi, name in IDS:
                                src = A[name][bass.ds(2 * i + r, 1), :].rearrange("a s -> (a s)")
                                sp.dma_start(ids[r][lo:hi, c, :], src.partition_broadcast(hi - lo))\
                                  .then_inc(ids_in[r], 16)

                @block.gpsimd
                def _(pool):
                    c = Count(pool, g_row)
                    c.one(pool.memset(ids[0][64:P, 1, :], -1))
                    c.one(pool.memset(ids[1][64:P, 1, :], -1))
                    c.one(pool.memset(power[:], -0.5))
                    c.one(pool.iota(rowi[:, 1:2], pattern=[[0, 1]], base=0, channel_multiplier=1))
                    c.one(pool.iota(rowi[0:64, 0:1], pattern=[[0, 1]], base=0, channel_multiplier=1))
                    c.one(pool.iota(rowi[64:P, 0:1], pattern=[[0, 1]], base=0, channel_multiplier=1))
                    c.one(pool.tensor_copy(rowf[:], rowi[:]))
                    g_gain.grant(pool)
                    g_rstd.grant(pool)
                    g_h.grant(pool)
                    with pool.Fori(0, NB) as b:
                        c = Count(pool, g_step, GSTEP * b)
                        rstd(pool, c, v_stats, b, mv, rs, power, g_rstd)
                        pool.wait_ge(v_norm.sem, v_norm.nth(b))
                        pool.tensor_tensor(xg[:], xn[:], bc(gam0[:].unsqueeze(1), [P, TJ, D]), ALU.mult).then_inc(g_gain.sem, 1)
                        pool.wait_ge(g_gain.sem, g_gain.nth(b))
                        pool.tensor_tensor(tiled(h[:, ts(b, ROW)]), xg[:], bc(bet0[:].unsqueeze(1), [P, TJ, D]), ALU.add)\
                            .then_inc(g_h.sem, 1)

                @block.vector
                def _(dve):
                    dve.wait_ge(g_row, 7)
                    for s in (v_hot, v_stats, v_norm):
                        s.grant(dve)
                    with dve.Fori(0, NB // 2) as i:
                        for r in range(2):
                            b = 2 * i + r
                            c = Count(dve, v_step, VSTEP * b)
                            dve.wait_ge(ids_in[r], 96 * (i + 1))
                            dve.wait_ge(t_z.sem, t_z.before(b))
                            for half_, col in ((0, 0), (1, 1)):
                                dve.tensor_scalar(onehot[:, 2 * half_:2 * half_ + 2, :], ids[r][:, 2 * half_:2 * half_ + 2, :],
                                                  rowf[:, col:col + 1], None, ALU.is_equal).then_inc(v_hot.sem, 1)
                            dve.wait_ge(t_z.sem, t_z.nth(b))
                            z = tiled(bank[0][:, 0:ROW])
                            stats(dve, c, z, st, mv, v_stats)
                            dve.wait_ge(g_rstd.sem, g_rstd.nth(b))
                            dve.wait_ge(g_gain.sem, g_gain.before(b))
                            for j in range(TJ):
                                dve.tensor_scalar(xn[:, j, :], z[:, j, :], mv[:, j, 0:1], rs[:, j:j + 1],
                                                  ALU.subtract, ALU.mult).then_inc(v_norm.sem, 1)

                @block.tensor
                def _(pe):
                    t_z.grant(pe)
                    with pe.Fori(0, NB) as b:
                        pe.wait_ge(v_hot.sem, v_hot.nth(b))
                        pe.wait_ge(v_norm.sem, v_norm.before(b))
                        for j in range(TJ):
                            for k in range(12):
                                c, part = k // 3, k % 3
                                last = pe.matmul(bank[0][:, ts(j, D)], onehot[:, c, ts(j, P)], table[:, c, part, :],
                                                 start=(k == 0), stop=(k == 11))
                        last.then_inc(t_z.sem, 1)

        with ExitStack() as own:
            def tmp(name, shape, dt=F32):
                return own.enter_context(nc.sbuf_tensor(name, shape, dt))

            def signals(names, each=1):
                return (Signal(sem(n), each) for n in names.split())

            power = tmp("power", [P, TJ])
            tiny = [[tmp(f"{n}{k}", [P, TJ] + s) for n, s in (("st", [6]), ("mv", [2]), ("rs", []))] for k in range(3)]
            hb, xn = tmp("hb", [P, TJ, D]), tmp("xn", [P, TJ, D])
            xT, qT, kT, vT = tmp("xT", [P, S]), tmp("qT", [P, S]), tmp("kT", [P, S]), tmp("vT", [D, S])
            vo = tmp("vo", [P, TJ, D])
            sc, ms = tmp("sc", [P, TJ, S]), tmp("ms", [P, TJ, S])
            above = tmp("above", [P, S], BF16)
            mx, nm, rsum, rinv = (tmp(n, [P, TJ]) for n in ("mx", "nm", "rsum", "rinv"))
            ksum = tmp("ksum", [D, 1])
            point, low, high, gap = (tmp(n, [P, 2, TJ]) for n in ("point", "low", "high", "gap"))
            is_low, is_high = tmp("is_low", [P, TJ], U32), tmp("is_high", [P, TJ], U32)
            frac, inv, asum = tmp("frac", [P, TJ]), tmp("inv", [P, TJ]), tmp("asum", [P, TJ])
            exact, rank, thr, near, bad = (tmp(n, [P, TJ]) for n in ("exact", "rank", "thr", "near", "bad"))
            top8, hit8, order8 = tmp("top8", [P, TJ, 8]), tmp("hit8", [P, TJ, 8]), tmp("order8", [P, 8])
            order8i = tmp("order8i", [P, 8], I32)
            nbadf, nbad = tmp("nbadf", [1, 1]), tmp("nbad", [1, 1], I32)
            onecol = tmp("onecol", [P, 1])
            junk, ajunk = tmp("junk", [P, TJ, S], BF16), tmp("ajunk", [P, TJ, S], BF16)
            lo, mid, delta, cnt, up = (tmp(n, [P, TJ]) for n in ("lo", "mid", "delta", "cnt", "up"))
            eT = tmp("eT", [P, 2, TJ, P])
            xn2, x2T = tmp("xn2", [P, TJ, D]), tmp("x2T", [D + 1, S])
            gate, top = tmp("gate", [P, TJ, NE]), tmp("top", [P, TJ, NE])
            gd, ge, gm, comb, cres = (tmp(n, [P, TJ, NE]) for n in ("gd", "ge", "gm", "comb", "cres"))
            gsum, grec = tmp("gsum", [P, TJ]), tmp("grec", [P, TJ])
            c24 = tmp("c24", [P, TJ, 3, NE], BF16)
            cT = tmp("cT", [P, S], BF16)
            xe = tmp("xe", [P, 2, S])
            hid = tmp("hid", [P, 2, HH, S])

            v_stats, v_xn, v_k, v_nm = signals("v_stats v_xn v_k v_nm")
            g_rstd, g_hb = signals("g_rstd g_hb")
            t_xT, t_qk, t_vT, t_vo = signals("t_xT t_qk t_vT t_vo")
            a_xT, a_q, a_vT, a_vo, a_mean = signals("a_xT a_q a_vT a_vo a_mean")
            t_s, v_sc, v_ms, a_e, t_eT, t_o, v_h1 = signals("t_s v_sc v_ms a_e t_eT t_o v_h1", TJ)
            v_eT, a_eT = signals("v_eT a_eT", TJ // 2)
            v_st2, v_xn2, v_gd, v_c24 = signals("v_st2 v_xn2 v_gd v_c24")
            g_rs2, g_rs3 = signals("g_rs2 g_rs3")
            t_x2T, t_gate, t_cT = signals("t_x2T t_gate t_cT")
            a_x2T, a_ge, a_cT = signals("a_x2T a_ge a_cT")
            t_bc, v_xe, t_h0, t_h1, a_h0, a_h1, t_w2 = signals("t_bc v_xe t_h0 t_h1 a_h0 a_h1 t_w2", NE)
            v_h2, v_st3 = signals("v_h2 v_st3")
            g_step_a, g_step_x, v_step_a, v_step_x, v_bis, ones_in = (
                sem(n) for n in ("g_step_a", "g_step_x", "v_step_a", "v_step_x", "v_bis", "ones_in"))
            v_pt, v_cnt, a_cnt = (Signal(sem(n), k) for n, k in
                                  (("v_pt", SEARCH), ("v_cnt", SEARCH * OWN), ("a_cnt", SEARCH * (TJ - OWN))))
            v_bad, t_bad = Signal(sem("v_bad")), Signal(sem("t_bad"))
            BSTEP = 8
            FSTEP = 3 + BSTEP * BISECT + 1
            NFILL = 11
            VSTEP_A, VSTEP_X = 83, 38

            with nc.Block() as block:
                def pipeline(eng, both):
                    both(0, None)
                    with eng.Fori(1, NB) as b:
                        both(b, b - 1)
                    both(None, NB - 1)

                @block.gpsimd
                def _(pool):
                    fills = ((power[:], -0.5), (xT[D:P, :], 0.0), (xT[D:D + 1, :], 1.0), (x2T[D:D + 1, :], 1.0), (onecol[:], 1.0),
                             (qT[D:P, :], 0.0), (kT[D:P, :], 0.0), (cT[:], 0.0), (xe[D:P], 0.0))
                    for k, (t, value) in enumerate(fills):
                        pool.memset(t, value).then_inc(ones_in, 1)
                        pool.wait_ge(ones_in, k + 1)
                    pool.iota(order8i[:], pattern=[[1, 8]], base=0, channel_multiplier=0).then_inc(ones_in, 1)
                    pool.wait_ge(ones_in, len(fills) + 1)
                    pool.tensor_copy(order8[:], order8i[:]).then_inc(ones_in, 1)
                    for s in (g_rstd, g_hb, g_rs2, g_rs3):
                        s.grant(pool)

                    def both(a, x):
                        if a is not None:
                            ca = Count(pool, g_step_a, a)
                            rstd(pool, ca, v_stats, a, tiny[0][1], tiny[0][2], power, g_rstd)
                        if x is not None:
                            cx = Count(pool, g_step_x, 2 * x)
                            rstd(pool, cx, v_st2, x, tiny[1][1], tiny[1][2], power, g_rs2)
                        if a is not None:
                            pool.wait_ge(v_h1.sem, v_h1.before(a))
                            pool.tensor_tensor(hb[:], tiled(h[:, ts(a, ROW)]), bc(bo[:].unsqueeze(1), [P, TJ, D]), ALU.add)\
                                .then_inc(g_hb.sem, 1)
                        if x is not None:
                            rstd(pool, cx, v_st3, x, tiny[2][1], tiny[2][2], power, g_rs3)

                    pipeline(pool, both)

                @block.scalar
                def _(act):
                    for s in (a_mean, a_cnt, a_xT, a_q, a_vT, a_vo, a_e, a_eT, a_x2T, a_ge, a_cT, a_h0, a_h1):
                        s.grant(act)

                    def both(a, x):
                        if a is not None:
                            act.wait_ge(t_xT.sem, t_xT.nth(a))
                            act.activation(xT[0:D, :], bank[0][0:D, :], ACT.Copy).then_inc(a_xT.sem, 1)
                        if x is not None:
                            act.wait_ge(t_x2T.sem, t_x2T.nth(x))
                            act.activation(x2T[0:D, :], bank[4][0:D, :], ACT.Copy).then_inc(a_x2T.sem, 1)
                        if a is not None:
                            act.wait_ge(t_qk.sem, t_qk.nth(a))
                            act.activation(qT[0:D, :], bank[1][0:D, :], ACT.Copy).then_inc(a_q.sem, 1)
                            act.wait_ge(t_vT.sem, t_vT.nth(a))
                            act.activation(vT[:], bank[2][0:D, :], ACT.Copy).then_inc(a_vT.sem, 1)
                        if x is not None:
                            act.wait_ge(v_gd.sem, v_gd.nth(x))
                            act.activation(ge[:], gd[:], ACT.Exp).then_inc(a_ge.sem, 1)
                        if a is not None:
                            act.wait_ge(t_vo.sem, t_vo.nth(a))
                            act.activation(vo[:], tiled(bank[0][:, 0:ROW]), ACT.Copy).then_inc(a_vo.sem, 1)
                            act.activation(point[:, 0, :], bank[0][:, ROW:ROW + TJ], ACT.Copy, scale=1.0 / S)\
                               .then_inc(a_mean.sem, 1)
                        if x is not None:
                            act.wait_ge(t_cT.sem, t_cT.nth(x))
                            act.activation(cT[0:3 * NE, :], bank[4][:].bitcast(BF16)[0:3 * NE, 0:S], ACT.Copy).then_inc(a_cT.sem, 1)
                        for k in range(NE):
                            if a is not None and k < SEARCH:
                                act.wait_ge(v_pt.sem, v_pt.nth(a, k + 1))
                                for j in range(OWN, TJ):
                                    if k:
                                        act.wait_ge(a_cnt.sem, a_cnt.nth(a, (k - 1) * (TJ - OWN) + j - OWN + 1))
                                    act.activation(ajunk[:, j, :], sc[:, j, :], ACT.Sign, bias=point[:, 0, j:j + 1],
                                                   scale=-1.0, accum_out=asum[:, j:j + 1]).then_inc(a_cnt.sem, 1)
                            if x is not None:
                                for half_, hidden_in, done in ((0, t_h0, a_h0), (1, t_h1, a_h1)):
                                    act.wait_ge(hidden_in.sem, hidden_in.nth(x, k + 1))
                                    act.wait_ge(t_w2.sem, t_w2.nth(x, k - 1) if k > 1 else t_w2.before(x))
                                    act.activation(hid[:, k % 2, half_, :], bank[6 + half_][:], ACT.Relu).then_inc(done.sem, 1)
                        if a is not None:
                            act.wait_ge(v_nm.sem, v_nm.nth(a))
                            for j in range(TJ):
                                act.wait_ge(v_ms.sem, v_ms.nth(a, j + 1))
                                act.activation(ms[:, j, :], ms[:, j, :], ACT.Exp, bias=nm[:, j:j + 1], scale=0.125,
                                               accum_out=rsum[:, j:j + 1]).then_inc(a_e.sem, 1)
                                if j % 2:
                                    act.wait_ge(t_eT.sem, t_eT.nth(a, j + 1))
                                    act.wait_ge(t_o.sem, t_o.nth(a, j - 1) if j > 1 else t_o.before(a))
                                    act.activation(eT[:, 1], bank[3][:].rearrange("p (c q) -> p c q", c=TJ), ACT.Copy)\
                                       .then_inc(a_eT.sem, 1)

                    act.wait_ge(ones_in, NFILL)
                    pipeline(act, both)

                @block.tensor
                def _(pe):
                    for s in (t_bad, t_xT, t_qk, t_vT, t_vo, t_s, t_eT, t_o, t_x2T, t_gate, t_cT, t_bc, t_h0, t_h1, t_w2):
                        s.grant(pe)
                    pe.wait_ge(ones_in, NFILL)

                    def features(x, ready, into, done, b):
                        pe.wait_ge(ready.sem, ready.nth(b))
                        apart(pe, spare)
                        for j in range(TJ):
                            last = pe.transpose(into[0:D, ts(j, P)], x[:, j, :], identf[:])
                        last.then_inc(done.sem, 1)

                    def scores(a, j):
                        if j >= 2:
                            pe.wait_ge(v_sc.sem, v_sc.nth(a, j - 1))
                        pe.matmul(bank[2 + j % 2][:], qT[:, ts(j, P)], kT[:], start=True, stop=True).then_inc(t_s.sem, 1)

                    def weighted(a, j):
                        done = (v_eT, a_eT)[j % 2]
                        pe.wait_ge(done.sem, done.nth(a, j // 2 + 1))
                        for k in range(TJ):
                            last = pe.matmul(bank[0][:, ts(j, D)], eT[:, j % 2, k, :], vo[:, k, :],
                                             start=(k == 0), stop=(k == TJ - 1))
                        last.then_inc(t_o.sem, 1)

                    def share(x, e):
                        pe.wait_ge(v_xe.sem, v_xe.nth(x, e) if e else v_xe.before(x))
                        pe.matmul(bank[5][0:D + 1, :], sel[:, e, :], cT[:], start=True, stop=True).then_inc(t_bc.sem, 1)

                    def first(x, e):
                        pe.wait_ge(v_xe.sem, v_xe.nth(x, e + 1))
                        for half_, taken, done in ((0, a_h0, t_h0), (1, a_h1, t_h1)):
                            pe.wait_ge(taken.sem, taken.nth(x, e) if e else taken.before(x))
                            pe.matmul(bank[6 + half_][:], W1[:, ts(HH * e + half_, P)], xe[:, e % 2, :],
                                      start=True, stop=True).then_inc(done.sem, 1)

                    def second(x, e):
                        for half_, taken in ((0, a_h0), (1, a_h1)):
                            pe.wait_ge(taken.sem, taken.nth(x, e + 1))
                            for j in range(TJ):
                                last = pe.matmul(bank[4][:, ts(j, D)], hid[:, e % 2, half_, ts(j, P)],
                                                 W2[:, HH * e + half_, :], start=False,
                                                 stop=(e == NE - 1 and half_ == HH - 1), skip_group_check=True)
                        last.then_inc(t_w2.sem, 1)

                    def both(a, x):
                        if a is not None:
                            pe.wait_ge(v_h1.sem, v_h1.before(a))
                            features(xn, v_xn, bank[0], t_xT, a)
                        if x is not None:
                            pe.wait_ge(v_h2.sem, v_h2.before(x))
                            features(xn2, v_xn2, bank[4], t_x2T, x)
                        if a is not None:
                            pe.wait_ge(a_xT.sem, a_xT.nth(a))
                            pe.wait_ge(v_eT.sem, v_eT.before(a))
                            pe.matmul(bank[1][:], Wqkv[:, 0:2 * D], xT[:], start=True, stop=True).then_inc(t_qk.sem, 1)
                            pe.wait_ge(v_sc.sem, v_sc.before(a))
                            pe.matmul(bank[2][0:D, :], Wqkv[:, 2 * D:3 * D], xT[:], start=True, stop=True)\
                              .then_inc(t_vT.sem, 1)
                        if x is not None:
                            pe.wait_ge(a_x2T.sem, a_x2T.nth(x))
                            for j in range(TJ):
                                last = pe.matmul(bank[4][:, ts(j, NE)], x2T[:, ts(j, P)], Wg[:], start=True, stop=True)
                            last.then_inc(t_gate.sem, 1)
                        if a is not None:
                            pe.wait_ge(a_vT.sem, a_vT.nth(a))
                            for j in range(TJ):
                                pe.matmul(bank[0][:, ts(j, D)], vT[:, ts(j, P)], Wo[:], start=True, stop=True)
                            pe.wait_ge(a_q.sem, a_q.nth(a))
                            pe.wait_ge(v_k.sem, v_k.nth(a))
                            for j in range(TJ):
                                last = pe.matmul(bank[0][:, ROW + j:ROW + j + 1], qT[0:D, ts(j, P)], ksum[:], start=True, stop=True)
                            last.then_inc(t_vo.sem, 1)
                            pe.wait_ge(a_eT.sem, a_eT.before(a))
                            for j in range(TJ):
                                scores(a, j)
                        if x is not None:
                            pe.wait_ge(v_c24.sem, v_c24.nth(x))
                            for j in range(TJ):
                                last = pe.transpose(bank[4][:].bitcast(BF16)[0:3 * NE, ts(j, P)],
                                                    c24[:, j].rearrange("p k e -> p (k e)"), identb[:])
                            last.then_inc(t_cT.sem, 1)
                            pe.wait_ge(a_cT.sem, a_cT.nth(x))
                            share(x, 0)
                            for j in range(TJ):
                                for k in range(3):
                                    pe.matmul(bank[4][:, ts(j, D)], cT[0:3 * NE, ts(j, P)], b2p[:, k, :],
                                              start=(j == 0 and k == 0), stop=False, skip_group_check=True)
                            for e in range(NE):
                                first(x, e)
                                if e + 1 < NE:
                                    share(x, e + 1)
                                if e:
                                    second(x, e - 1)
                        if a is not None:
                            pe.wait_ge(a_vo.sem, a_vo.nth(a))
                            pe.wait_ge(v_sc.sem, v_sc.nth(a))
                            pe.wait_ge(v_bad.sem, v_bad.nth(a))
                            pe.matmul(bank[0][0:1, 0:TJ], onecol[:], bad[:], start=True, stop=True).then_inc(t_bad.sem, 1)
                        if x is not None:
                            second(x, NE - 1)
                        if a is not None:
                            for j in range(TJ):
                                pe.wait_ge(a_e.sem, a_e.nth(a, j + 1))
                                if j >= 2:
                                    weighted(a, j - 2)
                                for k in range(TJ):
                                    last = pe.transpose(bank[1 + 2 * (j % 2)][:, ts(k, P)], ms[:, j, ts(k, P)], identf[:])
                                last.then_inc(t_eT.sem, 1)
                            weighted(a, TJ - 2)
                            weighted(a, TJ - 1)

                    pipeline(pe, both)

                @block.vector
                def _(dve):
                    for s in (v_pt, v_cnt, v_bad, v_stats, v_xn, v_k, v_nm, v_sc, v_ms, v_h1, v_eT, v_st2, v_xn2, v_gd, v_c24,
                              v_xe, v_h2, v_st3):
                        s.grant(dve)
                    dve.wait_ge(ones_in, NFILL)

                    def pair(ap):
                        return bc(ap.unsqueeze(1), [P, 2, TJ])

                    def gates_open(c, x):
                        dve.wait_ge(t_gate.sem, t_gate.nth(x))
                        c.one(dve.tensor_copy(gate[:], bank[4][:, 0:TJ * NE].rearrange("p (j e) -> p j e", j=TJ)))
                        apart(dve, spare)
                        for j in range(TJ):
                            c.step(dve.max(top[:, j, :], gate[:, j, :]))
                        c.settle()
                        c.step(dve.tensor_tensor(gd[:], gate[:], bc(top[:, :, 0:1], [P, TJ, NE]), ALU.subtract))
                        c.one(dve.tensor_tensor(gm[:], gate[:], bc(top[:, :, 1:2], [P, TJ, NE]), ALU.is_ge))
                        dve.sem_inc(v_gd.sem, 1)

                    def gates_close(c, x):
                        dve.wait_ge(a_ge.sem, a_ge.nth(x))
                        c.one(dve.tensor_tensor(gm[:], ge[:], gm[:], ALU.mult))
                        c.one(dve.tensor_reduce(gsum[:], gm[:], AX_X, ALU.add))
                        c.one(dve.reciprocal(grec[:], gsum[:]))
                        c.one(dve.tensor_tensor(comb[:], gm[:], bc(grec[:].unsqueeze(2), [P, TJ, NE]), ALU.mult))
                        split3(dve, c, comb[:], cres[:], [c24[:, :, k, :] for k in range(3)])
                        dve.sem_inc(v_c24.sem, 1)
                        dve.wait_ge(a_x2T.sem, a_x2T.nth(x))

                    def score_tiles(a, tiles):
                        for j in tiles:
                            dve.wait_ge(t_s.sem, t_s.nth(a, j + 1))
                            dve.tensor_scalar(sc[:, j, :], bank[2 + j % 2][:], 1.0, None, ALU.mult, ALU.max,
                                              accum_out=mx[:, j:j + 1]).then_inc(v_sc.sem, 1)

                    def bracket(c, a):
                        dve.wait_ge(v_sc.sem, v_sc.nth(a))
                        c.step(dve.tensor_scalar(nm[:], mx[:], 0.0, -0.125, ALU.max, ALU.mult))
                        dve.wait_ge(a_mean.sem, a_mean.nth(a))
                        c.one(dve.tensor_tensor(frac[:], mx[:], point[:, 0, :], ALU.subtract))
                        dve.sem_inc(v_nm.sem, 1)
                        dve.sem_inc(v_pt.sem, 1)
                        c.step(dve.memset(low[:, 1, :], 0.84 * S))
                        c.step(dve.memset(high[:, 1, :], 0.16 * S))
                        c.one(dve.tensor_scalar(frac[:], frac[:], 1.0 / 3.0, None, ALU.mult))
                        c.step(dve.tensor_tensor(low[:, 0, :], point[:, 0, :], frac[:], ALU.subtract))
                        c.step(dve.tensor_tensor(high[:, 0, :], point[:, 0, :], frac[:], ALU.add))

                    def count(a):
                        for j in range(OWN):
                            dve.tensor_scalar(junk[:, j, :], sc[:, j, :], point[:, 0, j:j + 1], None, ALU.is_ge, ALU.add,
                                              accum_out=point[:, 1, j:j + 1]).then_inc(v_cnt.sem, 1)

                    def narrow(c, a, k):
                        dve.wait_ge(a_cnt.sem, a_cnt.nth(a, (k + 1) * (TJ - OWN)))
                        c.step(dve.tensor_scalar(point[:, 1, OWN:], asum[:, OWN:], -0.5, S / 2, ALU.mult, ALU.add))
                        dve.wait_ge(v_cnt.sem, v_cnt.nth(a, (k + 1) * OWN))
                        c.settle()
                        c.step(dve.tensor_scalar(is_low[:], point[:, 1, :], S / 2 - 0.5, None, ALU.is_ge))
                        c.one(dve.tensor_scalar(is_high[:], point[:, 1, :], S / 2 - 0.5, None, ALU.is_lt))
                        apart(dve, spare)
                        c.step(dve.copy_predicated(low[:], pair(is_low[:]), point[:]))
                        c.one(dve.copy_predicated(high[:], pair(is_high[:]), point[:]))
                        if k == SEARCH - 1:
                            return
                        c.step(dve.tensor_scalar(frac[:], high[:, 1, :], AIM, 0.0, ALU.subtract, ALU.min))
                        c.one(dve.tensor_tensor(gap[:], low[:], high[:], ALU.subtract))
                        c.step(dve.reciprocal(inv[:], gap[:, 1, :]))
                        c.one(dve.tensor_tensor(frac[:], frac[:], gap[:, 0, :], ALU.mult))
                        c.one(dve.tensor_tensor(frac[:], frac[:], inv[:], ALU.mult))
                        dve.tensor_tensor(point[:, 0, :], high[:, 0, :], frac[:], ALU.subtract).then_inc(v_pt.sem, 1)
                        dve.wait_ge(v_pt.sem, v_pt.nth(a, k + 2))

                    def count_high(c):
                        for j in range(TJ):
                            c.step(dve.tensor_scalar(ms[:, j, :], sc[:, j, :], high[:, 0, j:j + 1], None, ALU.is_ge, ALU.add,
                                                     accum_out=exact[:, j:j + 1]))
                        c.settle()

                    def push_high(c):
                        for j in range(TJ):
                            c.step(dve.scalar_tensor_tensor(out=ms[:, j, :], in0=ms[:, j, :], scalar=-FAR, in1=sc[:, j, :],
                                                            op0=ALU.mult, op1=ALU.add))
                        c.step(dve.tensor_scalar(rank[:], exact[:], -1.0, S / 2 - 1.0, ALU.mult, ALU.add))
                        c.settle()
                        apart(dve, spare)

                    def best_eight(c):
                        for j in range(TJ):
                            c.step(dve.max(top8[:, j, :], ms[:, j, :]))

                    def pick(c):
                        c.one(dve.tensor_tensor(hit8[:], bc(order8[:].unsqueeze(1), [P, TJ, 8]),
                                                bc(rank[:].unsqueeze(2), [P, TJ, 8]), ALU.is_equal))
                        c.step(dve.tensor_reduce(near[:], hit8[:], AX_X, ALU.add))
                        c.one(dve.tensor_tensor(top8[:], top8[:], hit8[:], ALU.mult))
                        dve.tensor_scalar(bad[:], near[:], -1.0, 1.0, ALU.mult, ALU.add).then_inc(v_bad.sem, 1)
                        c.one(dve.tensor_reduce(thr[:], top8[:], AX_X, ALU.add))

                    def general(c, a):
                        dve.wait_ge(t_bad.sem, t_bad.nth(a))
                        c.one(dve.tensor_reduce(nbadf[:], bank[0][0:1, 0:TJ], AX_X, ALU.add))
                        c.one(dve.tensor_copy(nbad[:], nbadf[:]))
                        apart(dve, spare)
                        missed = dve.value_load(nbad[:], min_val=0, max_val=P * TJ)
                        with dve.If(missed > 0):
                            f = Count(dve, v_bis, FSTEP * a)
                            f.one(dve.tensor_reduce(lo[:], sc[:], AX_X, ALU.min))
                            f.one(dve.tensor_tensor(delta[:], mx[:], lo[:], ALU.subtract))
                            f.one(dve.tensor_scalar(delta[:], delta[:], 0.50001, 1e-30, ALU.mult, ALU.add))
                            apart(dve, spare)
                            with dve.Fori(0, BISECT) as i:
                                k = Count(dve, v_bis, FSTEP * a + 3 + BSTEP * i)
                                k.one(dve.tensor_tensor(mid[:], lo[:], delta[:], ALU.add))
                                for j in range(TJ):
                                    k.step(dve.tensor_scalar(junk[:, j, :], sc[:, j, :], mid[:, j:j + 1], None, ALU.is_ge, ALU.add,
                                                             accum_out=cnt[:, j:j + 1]))
                                k.settle()
                                k.one(dve.scalar_tensor_tensor(out=up[:], in0=cnt[:], scalar=S / 2 - 0.5, in1=delta[:],
                                                               op0=ALU.is_ge, op1=ALU.mult))
                                k.step(dve.tensor_tensor(lo[:], lo[:], up[:], ALU.add))
                                k.one(dve.tensor_scalar(delta[:], delta[:], 0.5, None, ALU.mult))
                                assert k.n == BSTEP
                            f.n += BSTEP * BISECT
                            f.one(dve.tensor_copy(thr[:], lo[:]))
                            assert f.n == FSTEP
                            apart(dve, spare)
                        with dve.Else():
                            dve.sem_inc(v_bis, FSTEP)

                    def take_exps(a, j):
                        dve.wait_ge(t_eT.sem, t_eT.nth(a, j + 1))
                        dve.wait_ge(t_o.sem, t_o.nth(a, j - 1) if j else t_o.before(a))
                        dve.tensor_copy(eT[:, 0], bank[1][:].rearrange("p (c q) -> p c q", c=TJ)).then_inc(v_eT.sem, 1)

                    def both(a, x):
                        if a is not None:
                            ca = Count(dve, v_step_a, VSTEP_A * a)
                            ha = tiled(h[:, ts(a, ROW)])
                            st, mv, rs = tiny[0]
                            stats(dve, ca, ha, st, mv, v_stats)
                        if x is not None:
                            cx = Count(dve, v_step_x, VSTEP_X * x)
                            hx = tiled(h[:, ts(x, ROW)])
                            dve.wait_ge(v_h1.sem, v_h1.nth(x))
                            st2, mv2, rs2 = tiny[1]
                            stats(dve, cx, hx, st2, mv2, v_st2)
                        if a is not None:
                            dve.wait_ge(g_rstd.sem, g_rstd.nth(a))
                            centre(dve, ca, ha, mv, rs, xn)
                            ca.settle()
                            dve.sem_inc(v_xn.sem, 1)
                        if x is not None:
                            dve.wait_ge(g_rs2.sem, g_rs2.nth(x))
                            centre(dve, cx, hx, mv2, rs2, xn2)
                            cx.settle()
                            dve.sem_inc(v_xn2.sem, 1)
                        if a is not None:
                            dve.wait_ge(t_qk.sem, t_qk.nth(a))
                            dve.tensor_scalar(kT[0:D, :], bank[1][D:2 * D, :], 1.0, None, ALU.mult, ALU.add, accum_out=ksum[:])\
                               .then_inc(v_k.sem, 1)
                        if x is not None:
                            gates_open(cx, x)
                        if a is not None:
                            score_tiles(a, (0, 1))
                        if x is not None:
                            gates_close(cx, x)
                        if a is not None:
                            score_tiles(a, (2, 3))
                            bracket(ca, a)

                        def share_tokens(e):
                            if x is None:
                                return
                            dve.wait_ge(t_bc.sem, t_bc.nth(x, e + 1))
                            dve.wait_ge(t_h1.sem, t_h1.nth(x, e - 1) if e > 1 else t_h1.before(x))
                            dve.tensor_tensor(xe[0:D + 1, e % 2, :], x2T[:], bank[5][0:D + 1, :], ALU.mult).then_inc(v_xe.sem, 1)

                        for k in range(SEARCH):
                            if a is not None:
                                count(a)
                            share_tokens(k)
                            if a is not None:
                                narrow(ca, a, k)
                        for k, stage in enumerate((count_high, push_high, best_eight)):
                            share_tokens(SEARCH + k)
                            if a is not None:
                                stage(ca)
                        if a is not None:
                            pick(ca)
                            general(ca, a)
                            for j in range(TJ):
                                dve.scalar_tensor_tensor(out=ms[:, j, :], in0=sc[:, j, :], scalar=thr[:, j:j + 1],
                                                         in1=sc[:, j, :], op0=ALU.is_ge, op1=ALU.mult).then_inc(v_ms.sem, 1)
                        if x is not None:
                            dve.wait_ge(t_w2.sem, t_w2.nth(x))
                            dve.tensor_tensor(hx, hx, tiled(bank[4][:, 0:ROW]), ALU.add).then_inc(v_h2.sem, 1)
                            dve.wait_ge(v_h2.sem, v_h2.nth(x))
                            st3, mv3, rs3 = tiny[2]
                            stats(dve, cx, hx, st3, mv3, v_st3)
                        if a is not None:
                            take_exps(a, 0)
                        if x is not None:
                            dve.wait_ge(g_rs3.sem, g_rs3.nth(x))
                            centre(dve, cx, hx, mv3, rs3, u[:, bass.ds(TJ * x, TJ), :])
                            cx.settle()
                            assert cx.n == VSTEP_X, cx.n
                        if a is not None:
                            take_exps(a, 2)
                            dve.wait_ge(a_e.sem, a_e.nth(a))
                            ca.one(dve.reciprocal(rinv[:], rsum[:]))
                            dve.wait_ge(g_hb.sem, g_hb.nth(a))
                            dve.wait_ge(t_o.sem, t_o.nth(a))
                            for j in range(TJ):
                                dve.scalar_tensor_tensor(out=ha[:, j, :], in0=bank[0][:, ts(j, D)], scalar=rinv[:, j:j + 1],
                                                         in1=hb[:, j, :], op0=ALU.mult, op1=ALU.add).then_inc(v_h1.sem, 1)
                            assert ca.n == VSTEP_A, ca.n

                    pipeline(dve, both)

        with ExitStack() as own:
            def tmp(name, shape, dt=F32):
                return own.enter_context(nc.sbuf_tensor(name, shape, dt))

            skew = [tmp(f"skew{r}", [P, HG, TW]) for r in range(2)]
            skew_in = [sem("skew_in_even"), sem("skew_in_odd")]
            t_y, a_gy = Signal(sem("t_y")), Signal(sem("a_gy"))
            back = tmp("back", [P, NB * TJ, D])
            flip = tmp("flip", [P, P])
            cols = [tmp(f"cols{r}", [P, NB * TJ, HG]) for r in range(2)]
            v_cols = Signal(sem("v_cols"))
            t_flip, a_back, g_flip = Signal(sem("t_flip")), Signal(sem("a_back")), sem("g_flip")
            FL = S // D

            with nc.Block() as block:
                @block.sync
                def _(sp):
                    with sp.Fori(0, D // HG // 2) as i:
                        for r in range(2):
                            g = 2 * i + r
                            sp.wait_ge(t_y.sem, t_y.before(g) - r)
                            src = bass.AP(taps, g * (HG * KROW) + 1, [[1, P], [KROW, HG], [1, TW]])
                            sp.dma_start(skew[r][:], src).then_inc(skew_in[r], 16)

                @block.gpsimd
                def _(pool):
                    pool.memset(flip[:], 0.0).then_inc(g_flip, 1)
                    pool.wait_ge(g_flip, 1)
                    pool.affine_select(out=flip[:], in_=flip[:], compare_op=ALU.not_equal, fill=1.0, base=1 - P,
                                       pattern=[[1, P]], channel_multiplier=1).then_inc(g_flip, 1)

                @block.tensor
                def _(pe):
                    t_flip.grant(pe)
                    pe.wait_ge(g_flip, 2)
                    with pe.Fori(0, NB * TJ // FL // 2) as i:
                        for r in range(2):
                            n = 2 * i + r
                            pe.wait_ge(a_back.sem, a_back.before(n) - r)
                            pe.matmul(bank[2 + r][:], flip[:], u[:, bass.ds(n * FL, FL), :], start=True, stop=True)\
                              .then_inc(t_flip.sem, 1)
                    pe.wait_ge(a_back.sem, a_back.before(NB * TJ // FL))
                    t_y.grant(pe)
                    with pe.Fori(0, D // HG // 2) as i:
                        for r in range(2):
                            g = 2 * i + r
                            pe.wait_ge(skew_in[r], 16 * i + 16)
                            pe.wait_ge(v_cols.sem, v_cols.nth(g))
                            pe.wait_ge(a_gy.sem, a_gy.before(g) - r)
                            for hh in range(HG):
                                for lc in range(TJ):
                                    for s in range(TJ):
                                        at = P * (TJ - 1 + lc - s)
                                        last = pe.matmul(bank[r][:, ts(TJ * hh + lc, NB)], skew[r][:, hh, at:at + P],
                                                         cols[r][:, s::TJ, hh], start=(s == 0), stop=(s == TJ - 1))
                            last.then_inc(t_y.sem, 1)

                @block.vector
                def _(dve):
                    v_cols.grant(dve)
                    dve.wait_ge(a_back.sem, a_back.before(NB * TJ // FL))
                    with dve.Fori(0, D // HG // 2) as i:
                        for r in range(2):
                            g = 2 * i + r
                            dve.wait_ge(t_y.sem, t_y.before(g) - r)
                            dve.tensor_copy(cols[r][:], back[:, :, bass.ds(g * HG, HG)]).then_inc(v_cols.sem, 1)

                @block.scalar
                def _(act):
                    a_back.grant(act)
                    with act.Fori(0, NB * TJ // FL // 2) as i:
                        for r in range(2):
                            n = 2 * i + r
                            act.wait_ge(t_flip.sem, t_flip.nth(n))
                            act.activation(back[:, bass.ds(n * FL, FL), :],
                                           bank[2 + r][:].rearrange("p (t d) -> p t d", d=D), ACT.Copy).then_inc(a_back.sem, 1)
                    a_gy.grant(act)
                    with act.Fori(0, D // HG // 2) as i:
                        for r in range(2):
                            g = 2 * i + r
                            act.wait_ge(t_y.sem, t_y.nth(g))
                            src = bank[r][:, 0:HG * TJ * NB].rearrange("p (h l b) -> p h l b", h=HG, l=TJ)
                            dst = gy[:, :, :, bass.ds(g * HG, HG)].rearrange("p b l h -> p h l b")
                            act.activation(dst, src, ACT.Gelu).then_inc(a_gy.sem, 1)

        with ExitStack() as own:
            def tmp(name, shape, dt=F32):
                return own.enter_context(nc.sbuf_tensor(name, shape, dt))

            def signals(names, each=1):
                return (Signal(sem(n), each) for n in names.split())

            power = tmp("power_f", [P, TJ])
            tiny = [[tmp(f"{n}f{k}", [P, TJ] + s) for n, s in (("st", [6]), ("mv", [2]), ("rs", []))] for k in range(2)]
            gT = tmp("gT", [D + 1, S])
            sg, z, r_, rn, rg, xn = (tmp(n, [P, TJ, D]) for n in ("sg", "z", "r_", "rn", "rg", "xn_f"))
            rowsT = tmp("rowsT", [P, S])
            lg, best, off = tmp("lg", [P, TJ, NX]), tmp("best", [P, TJ, 8]), tmp("off", [P, TJ, NX])
            hid = tmp("hid_f", [P, XC, S])
            y = [tmp(f"y{r}", [P, TJ, D]) for r in range(2)]
            t_gT, t_glu, t_xT, t_lg, t_off, t_y = signals("t_gT t_glu t_xT_f t_lg t_off t_out_f")
            a_gT, a_sg, a_xT, a_off = signals("a_gT a_sg a_xT_f a_off")
            v_r, v_st, v_rn, v_h3, v_st4, v_xn, v_off, v_y, v_z = signals(
                "v_r v_st_f v_rn v_h3 v_st4 v_xn_f v_off v_y v_z")
            g_rs, g_rg, g_rs4 = signals("g_rs_f g_rg g_rs4")
            t_hid = Signal(sem("t_hid_f"), XC)
            a_hid, v_hid = signals("a_hid_f v_hid_f", XC // 2)
            y_out = [sem("y_out_even"), sem("y_out_odd")]
            v_step, g_step, ready = sem("v_step_f"), sem("g_step_f"), sem("ready_f")
            VSTEP, GSTEP = 32, 3

            with nc.Block() as block:
                @block.sync
                def _(sp):
                    with sp.Fori(0, NB // 2) as i:
                        for r in range(2):
                            b = 2 * i + r
                            sp.wait_ge(v_y.sem, v_y.nth(b))
                            sp.dma_start(out[bass.ds(b, 1)].rearrange("a (j p) d -> p (a j) d", p=P), y[r][:])\
                              .then_inc(y_out[r], 16)
                    for r in range(2):
                        sp.wait_ge(y_out[r], 16 * (NB // 2) + 16)

                @block.gpsimd
                def _(pool):
                    for k, (t, value) in enumerate(((power[:], -0.5), (gT[D:D + 1, :], 1.0), (rowsT[:], 0.0),
                                                    (rowsT[D:D + 1, :], 1.0))):
                        pool.memset(t, value).then_inc(ready, 1)
                        pool.wait_ge(ready, k + 1)
                    for s in (g_rs, g_rg, g_rs4):
                        s.grant(pool)
                    with pool.Fori(0, NB) as b:
                        c = Count(pool, g_step, GSTEP * b)
                        rstd(pool, c, v_st, b, tiny[0][1], tiny[0][2], power, g_rs)
                        pool.wait_ge(v_rn.sem, v_rn.nth(b))
                        c.one(pool.tensor_tensor(rg[:], rn[:], bc(gam1[:].unsqueeze(1), [P, TJ, D]), ALU.mult))
                        pool.tensor_tensor(rg[:], rg[:], bc(bet1[:].unsqueeze(1), [P, TJ, D]), ALU.add).then_inc(g_rg.sem, 1)
                        rstd(pool, c, v_st4, b, tiny[1][1], tiny[1][2], power, g_rs4)
                        assert c.n == GSTEP, c.n

                @block.scalar
                def _(act):
                    for s in (a_gT, a_sg, a_xT, a_off, a_hid):
                        s.grant(act)
                    act.wait_ge(ready, 4)
                    with act.Fori(0, NB) as b:
                        act.wait_ge(t_gT.sem, t_gT.nth(b))
                        act.activation(gT[0:D, :], bank[0][0:D, :], ACT.Copy).then_inc(a_gT.sem, 1)
                        act.wait_ge(t_glu.sem, t_glu.nth(b))
                        act.wait_ge(v_r.sem, v_r.before(b))
                        act.activation(sg[:], bank[1][:].rearrange("p (j f) -> p j f", j=TJ)[:, :, D:2 * D], ACT.Sigmoid)\
                           .then_inc(a_sg.sem, 1)
                        act.wait_ge(t_xT.sem, t_xT.nth(b))
                        act.activation(rowsT[0:D, :], bank[2][0:D, :], ACT.Copy).then_inc(a_xT.sem, 1)
                        act.wait_ge(t_off.sem, t_off.nth(b))
                        act.activation(rowsT[96:P, :], bank[3][0:NX, :], ACT.Copy).then_inc(a_off.sem, 1)
                        for k in range(0, XC, 2):
                            act.wait_ge(t_hid.sem, t_hid.nth(b, k + 1))
                            act.wait_ge(t_y.sem, t_y.before(b))
                            act.activation(hid[:, k, :], bank[4 + k][:], ACT.Relu).then_inc(a_hid.sem, 1)

                @block.tensor
                def _(pe):
                    for s in (t_gT, t_glu, t_xT, t_lg, t_off, t_y, t_hid):
                        s.grant(pe)
                    pe.wait_ge(ready, 4)
                    with pe.Fori(0, NB) as b:
                        pe.wait_ge(v_z.sem, v_z.nth(b))
                        pe.wait_ge(v_y.sem, v_y.before(b))
                        apart(pe, spare)
                        for j in range(TJ):
                            last = pe.transpose(bank[0][0:D, ts(j, P)], z[:, j, :], identf[:])
                        last.then_inc(t_gT.sem, 1)
                        pe.wait_ge(a_gT.sem, a_gT.nth(b))
                        pe.wait_ge(v_r.sem, v_r.before(b))
                        for j in range(TJ):
                            last = pe.matmul(bank[1][:, ts(j, 2 * D)], gT[:, ts(j, P)], Wglu[:], start=True, stop=True)
                        last.then_inc(t_glu.sem, 1)
                        pe.wait_ge(v_xn.sem, v_xn.nth(b))
                        apart(pe, spare)
                        for j in range(TJ):
                            last = pe.transpose(bank[2][0:D, ts(j, P)], xn[:, j, :], identf[:])
                        last.then_inc(t_xT.sem, 1)
                        pe.wait_ge(a_xT.sem, a_xT.nth(b))
                        for j in range(TJ):
                            last = pe.matmul(bank[3][:, ts(j, NX)], rowsT[0:D + 1, ts(j, P)], Wr[:], start=True, stop=True)
                        last.then_inc(t_lg.sem, 1)
                        pe.wait_ge(v_off.sem, v_off.nth(b))
                        apart(pe, spare)
                        for j in range(TJ):
                            last = pe.transpose(bank[3][0:NX, ts(j, P)], off[:, j, :], identf[:])
                        last.then_inc(t_off.sem, 1)
                        pe.wait_ge(a_off.sem, a_off.nth(b))
                        for k in range(XC):
                            pe.matmul(bank[4 + k][:], Wx1[:, ts(k, P)], rowsT[:], start=True, stop=True).then_inc(t_hid.sem, 1)
                        pe.wait_ge(a_hid.sem, a_hid.nth(b))
                        pe.wait_ge(v_hid.sem, v_hid.nth(b))
                        for j in range(TJ):
                            pe.matmul(bank[0][:, ts(j, D)], rowsT[:, ts(j, P)], bx2[:], start=True, stop=False)
                            for k in range(XC):
                                last = pe.matmul(bank[0][:, ts(j, D)], hid[:, k, ts(j, P)], Wx2[:, k, :],
                                                 start=False, stop=(k == XC - 1))
                        last.then_inc(t_y.sem, 1)

                @block.vector
                def _(dve):
                    for s in (v_r, v_st, v_rn, v_h3, v_st4, v_xn, v_off, v_y, v_hid, v_z):
                        s.grant(dve)
                    for r in range(2):
                        dve.sem_inc(y_out[r], 16)
                    dve.wait_ge(ready, 4)
                    with dve.Fori(0, NB // 2) as i:
                        for r in range(2):
                            b = 2 * i + r
                            c = Count(dve, v_step, VSTEP * b)
                            hrow = tiled(h[:, ts(b, ROW)])
                            dve.wait_ge(t_gT.sem, t_gT.before(b))
                            dve.tensor_copy(z[:], gy[:, bass.ds(b, 1)].rearrange("p a l h -> p (a l) h")).then_inc(v_z.sem, 1)
                            dve.wait_ge(a_sg.sem, a_sg.nth(b))
                            c.one(dve.tensor_tensor(r_[:], bank[1][:].rearrange("p (j f) -> p j f", j=TJ)[:, :, 0:D], sg[:], ALU.mult))
                            dve.tensor_tensor(r_[:], r_[:], u[:, bass.ds(TJ * b, TJ), :], ALU.add).then_inc(v_r.sem, 1)
                            dve.wait_ge(v_r.sem, v_r.nth(b))
                            st, mv, rs = tiny[0]
                            stats(dve, c, r_, st, mv, v_st)
                            dve.wait_ge(g_rs.sem, g_rs.nth(b))
                            centre(dve, c, r_, mv, rs, rn)
                            c.settle()
                            dve.sem_inc(v_rn.sem, 1)
                            dve.wait_ge(g_rg.sem, g_rg.nth(b))
                            dve.tensor_tensor(hrow, hrow, rg[:], ALU.add).then_inc(v_h3.sem, 1)
                            dve.wait_ge(v_h3.sem, v_h3.nth(b))
                            st, mv, rs = tiny[1]
                            stats(dve, c, hrow, st, mv, v_st4)
                            dve.wait_ge(g_rs4.sem, g_rs4.nth(b))
                            centre(dve, c, hrow, mv, rs, xn)
                            c.settle()
                            dve.sem_inc(v_xn.sem, 1)
                            dve.wait_ge(t_lg.sem, t_lg.nth(b))
                            c.one(dve.tensor_copy(lg[:], bank[3][:, 0:TJ * NX].rearrange("p (j e) -> p j e", j=TJ)))
                            apart(dve, spare)
                            for j in range(TJ):
                                c.step(dve.max(best[:, j, :], lg[:, j, :]))
                            c.settle()
                            for j in range(TJ):
                                c.step(dve.tensor_scalar(off[:, j, :], lg[:, j, :], best[:, j, 0:1], 1.0, ALU.is_ge, ALU.subtract))
                            c.settle()
                            dve.sem_inc(v_off.sem, 1)
                            for k in range(1, XC, 2):
                                dve.wait_ge(t_hid.sem, t_hid.nth(b, k + 1))
                                dve.tensor_scalar(hid[:, k, :], bank[4 + k][:], 0.0, None, ALU.max).then_inc(v_hid.sem, 1)
                            dve.wait_ge(t_y.sem, t_y.nth(b))
                            dve.wait_ge(y_out[r], 16 * i + 16)
                            dve.scalar_tensor_tensor(out=y[r][:], in0=tiled(bank[0][:, 0:ROW]), scalar=0.0, in1=hrow,
                                                     op0=ALU.max, op1=ALU.add).then_inc(v_y.sem, 1)
                            assert c.n == VSTEP, c.n


def kernel(**inputs):
    import numpy as np
    import concourse.bacc as bacc
    from concourse.bass_utils import run_bass_kernel_spmd

    v = {k: np.asarray(a) for k, a in inputs.items()}
    L = {k: v[k] for k in ("x", "itok_BS_0_255", "itok_BS_0_511", "itok_BS_0_127", "itok_BS_0_63", "itok_BS_0_3")}
    et = np.zeros((96, 4, P), np.float32)
    for t, (name, chunk, col) in enumerate((("et", 0, 0), ("fc", 0, 64), ("sc", 2, 0), ("of", 3, 0), ("tt", 1, 0), ("rc", 1, 64))):
        e = v[f"L0_tok_E_{name}"]
        et[16 * t:16 * t + 16, chunk, col:col + e.shape[0]] = e.T
    L["Et"] = et.reshape(96, 4 * P)
    L["WT"] = v["L0_tok_W"].T
    L.update(tokb=v["L0_tok_b"], gam0=v["L0_tok_gamma"], bet0=v["L0_tok_beta"])
    L.update(Wqkv=v["L0_attn_W_qkv"], bqkv=v["L0_attn_b_qkv"], Wo=v["L0_attn_W_out"], bo=v["L0_attn_b_out"])
    L.update(WgT=v["L0_ffn_Wg"].T, bg=v["L0_ffn_bg"], W1T=v["L0_ffn_W1"].reshape(-1, D).T, b1=v["L0_ffn_b1"].reshape(-1),
             W2T=v["L0_ffn_W2"].transpose(0, 2, 1).reshape(-1, D), b2=v["L0_ffn_b2"])
    L.update(ldt=v["L1_attn_log_dt"], ArlT=v["L1_attn_A_real_log"].T, AimT=v["L1_attn_A_imag"].T,
             CreT=v["L1_attn_C_re"].transpose(2, 0, 1).reshape(NS, -1), CimT=v["L1_attn_C_im"].transpose(2, 0, 1).reshape(NS, -1),
             skip=v["L1_attn_D"], WgluT=v["L1_attn_W_out"].T, bglu=v["L1_attn_b_out"], gam1=v["L1_attn_gamma"],
             bet1=v["L1_attn_beta"])
    L.update(WrT=v["L1_ffn_router_w"].T, br=v["L1_ffn_router_b"], Wx1=v["L1_ffn_W1"].transpose(1, 0, 2).reshape(D, -1),
             bx1=v["L1_ffn_b1"].reshape(-1), Wx2=v["L1_ffn_W2"].reshape(-1, D), bx2=v["L1_ffn_b2"])
    nc = bacc.Bacc("TRN2", target_bir_lowering=False, num_devices=1)
    arrays, A = {}, {}
    for name, a in L.items():
        arrays[f"in_{name}"] = a = np.ascontiguousarray(a)
        A[name] = nc.dram_tensor(f"in_{name}", a.shape, mybir.dt.from_np(a.dtype), kind="ExternalInput").ap()
    out = nc.dram_tensor("out_0", (NB, S, D), F32, kind="ExternalOutput").ap()
    tower(nc, A, out)
    return run_bass_kernel_spmd(nc, [arrays], core_ids=[0]).results[0]["out_0"]
```

```python
from contextlib import ExitStack

import concourse.bass as bass
from concourse import mybir

F32 = mybir.dt.float32
BF16 = mybir.dt.bfloat16
I32 = mybir.dt.int32
U32 = mybir.dt.uint32
ALU = mybir.AluOpType
ACT = mybir.ActivationFunctionType
AX_X = mybir.AxisListType.X
ts = bass.ts

P = 128
NB, S, D = 16, 512, 64
TJ = S // P
ROW = TJ * D
NE, HID = 8, 256
HH = HID // P
NX, XH = 32, 16
XC = NX * XH // P
NS = 32
NHI, NLO = 16, 32
KROW = 2 * S
TW = (2 * TJ - 1) * P
HG = 4
TG = 16
SEARCH = 5
OWN = 1
AIM = 9
BISECT = 32
FAR = 1e30
MAGIC = 1.5 * 2.0 ** 23
TWO_PI_HI = 6.28125
TWO_PI_LO = 0.0019353071795864769
PI_SAFE = 3.1415925
BIG = 2.0 ** 60
EPS = 1e-5


class Count:

    def __init__(self, eng, sem, base=0):
        self.eng, self.sem, self.base, self.n = eng, sem, base, 0

    def step(self, ins):
        ins.then_inc(self.sem, 1)
        self.n += 1

    def settle(self):
        self.eng.wait_ge(self.sem, self.base + self.n)

    def one(self, ins):
        self.step(ins)
        self.settle()


class Signal:

    def __init__(self, sem, each=1, ahead=1):
        self.sem, self.each, self.ahead = sem, each, ahead

    def grant(self, eng):
        eng.sem_inc(self.sem, self.each * self.ahead)

    def nth(self, b, n=None):
        return self.each * b + self.each * self.ahead + (self.each if n is None else n)

    def before(self, b, back=1):
        return self.each * b + self.each * (self.ahead - back + 1)


def apart(eng, spare):
    eng.sem_inc(spare, 1)


def bc(ap, shape):
    return ap.to_broadcast(shape)


def split3(dve, c, x, rest, parts):
    a, b, last = parts
    c.one(dve.tensor_copy(a, x))
    c.one(dve.tensor_tensor(rest, x, a, ALU.subtract))
    c.one(dve.tensor_copy(b, rest))
    c.one(dve.tensor_tensor(x, rest, b, ALU.subtract))
    c.one(dve.tensor_copy(last, x))


def tower(nc, A, out):
    with ExitStack() as ctx:
        def sb(name, shape, dt=F32):
            return ctx.enter_context(nc.sbuf_tensor(name, shape, dt))

        def sem(name):
            return ctx.enter_context(nc.semaphore(name))

        bank = [ctx.enter_context(nc.psum_tensor(f"bank{i}", [P, 512], F32)) for i in range(8)]
        taps = nc.dram_tensor("taps", (D, KROW), F32, kind="Internal")
        taps3 = nc.dram_tensor("taps3", (3, D, KROW), BF16, kind="Internal")

        h = sb("h", [P, NB * ROW])
        u = sb("u", [P, NB * TJ, D])
        gy = sb("gy", [P, NB, TJ, D])
        identf = sb("identf", [P, P])
        identb = sb("identb", [P, P], BF16)
        WT = sb("WT", [96, D])
        Et = sb("Et", [96, 4, P])
        table = sb("table", [P, 4, 3, D], BF16)
        gam0, bet0 = sb("gam0", [P, D]), sb("bet0", [P, D])
        gam1, bet1 = sb("gam1", [P, D]), sb("bet1", [P, D])
        tokb = sb("tokb", [P, D])
        Wqkv = sb("Wqkv", [P, 3 * D])
        Wo = sb("Wo", [D, D])
        bo = sb("bo", [P, D])
        Wg = sb("Wg", [D + 1, NE])
        W1 = sb("W1", [P, NE * HID])
        W2 = sb("W2", [P, NE * HH, D])
        b2f = sb("b2f", [3 * NE, D])
        b2p = sb("b2p", [3 * NE, 3, D], BF16)
        sel = sb("sel", [P, NE, D + 1], BF16)
        Wglu = sb("Wglu", [D + 1, 2 * D])
        Wr = sb("Wr", [D + 1, NX])
        Wx1 = sb("Wx1", [P, XC * P])
        Wx2 = sb("Wx2", [P, XC, D])
        bx2 = sb("bx2", [P, D])

        w_in = sem("w_in")
        spare = sem("spare")
        consts = sem("consts")
        LOADS = [
            (WT[:], A["WT"]), (Et[:], A["Et"].rearrange("k (c v) -> k c v", c=4)),
            (gam0[:], A["gam0"].partition_broadcast(P)), (bet0[:], A["bet0"].partition_broadcast(P)),
            (gam1[:], A["gam1"].partition_broadcast(P)), (bet1[:], A["bet1"].partition_broadcast(P)),
            (tokb[:], A["tokb"].partition_broadcast(P)),
            (Wqkv[0:D, :], A["Wqkv"]),
            (Wo[:], A["Wo"]), (bo[:], A["bo"].partition_broadcast(P)),
            (Wg[0:D, :], A["WgT"]), (Wg[D:D + 1, :], A["bg"].unsqueeze(0)),
            (W1[0:D, :], A["W1T"]),
            (W2[:], A["W2T"].rearrange("(c p) d -> p c d", p=P)),
            (Wglu[0:D, :], A["WgluT"]), (Wglu[D:D + 1, :], A["bglu"].unsqueeze(0)),
            (Wr[0:D, :], A["WrT"]), (Wr[D:D + 1, :], A["br"].unsqueeze(0)),
            (Wx2[:], A["Wx2"].rearrange("(c p) d -> p c d", p=P)),
        ] + [(b2f[NE * i:NE * i + NE, :], A["b2"]) for i in range(3)]

        with ExitStack() as own:
            def tmp(name, shape, dt=F32):
                return own.enter_context(nc.sbuf_tensor(name, shape, dt))

            onesf = tmp("onesf", [P, P])
            absw, rowsum, half, nhalf, scl = (tmp(n, [96, k]) for n, k in
                                              (("absw", D), ("rowsum", 1), ("half", 1), ("nhalf", 1), ("scl", 1)))
            wpos, wneg, weff = tmp("wpos", [96, D]), tmp("wneg", [96, D]), tmp("weff", [96, D])
            tabf, tabr = tmp("tabf", [P, 4, D]), tmp("tabr", [P, 4, D])
            b2r = tmp("b2r", [3 * NE, D])
            M = 2 * NS
            ldt, arl, aim = tmp("ldt", [M, D]), tmp("arl", [M, D]), tmp("aim", [M, D])
            cre, cim = tmp("cre", [M, 2, D]), tmp("cim", [M, 2, D])
            skip = tmp("skip", [1, D])
            ki = tmp("ki", [M, NLO + NHI], I32)
            kf = tmp("kf", [M, NLO + NHI])
            phase, sgn = tmp("phase", [M, 1]), tmp("sgn", [M, 1])
            dt_, are, w, a = (tmp(n, [M, D]) for n in ("dt_", "are", "w", "a"))
            NK = NLO + NHI
            theta, turns, mag = (tmp(n, [M, D, NK]) for n in ("theta", "turns", "mag"))
            th2, tn2, sc2 = (tmp(n, [M, 2, D]) for n in ("th2", "tn2", "sc2"))
            q1, q2, q3, q4, em = (tmp(n, [M, D]) for n in ("q1", "q2", "q3", "q4", "em"))
            er, ei, yr, yi = (tmp(n, [M, D]) for n in ("er", "ei", "yr", "yi"))
            cr, ci, cs = tmp("cr", [M, 2, D]), tmp("ci", [M, 2, D]), tmp("cs", [M, 2, D])
            hi_sw = tmp("hi_sw", [M, D, NHI])
            left, lt2 = tmp("left", [M, 2, D, NHI]), tmp("lt2", [M, 2, D, NHI])
            lo_rev = tmp("lo_rev", [M, D, NLO])
            lbuf, mbuf = tmp("lbuf", [M, 2, TG, NHI]), tmp("mbuf", [M, 2, TG, NLO])
            rows = tmp("rows", [NHI, 2, D, NLO])
            whole, rest, split = tmp("whole", [P, S]), tmp("rest", [P, S]), tmp("split", [P, 3, S], BF16)
            taps_in, v_split = sem("taps_in"), sem("v_split")
            p_in = sem("p_in")
            g_clear, g_modes = sem("g_clear"), sem("g_modes")
            PLOADS = [(cre[NS * r:NS * r + NS], A["CreT"].rearrange("n (c h) -> n c h", c=2)) for r in range(2)]
            PLOADS += [(cim[NS * r:NS * r + NS], A["CimT"].rearrange("n (c h) -> n c h", c=2)) for r in range(2)]
            PLOADS += [(arl[NS * r:NS * r + NS, :], A["ArlT"]) for r in range(2)]
            PLOADS += [(aim[NS * r:NS * r + NS, :], A["AimT"]) for r in range(2)]
            PLOADS += [(ldt[:], A["ldt"].partition_broadcast(M)), (skip[:], A["skip"].unsqueeze(0))]

            g_step, v_step = sem("g_step_setup"), sem("v_step_setup")
            a_dt, a_tanh, a_sin2, a_mag, a_sin = (sem(n) for n in ("a_dt", "a_tanh", "a_sin2", "a_mag", "a_sin"))
            v_a, v_w2, v_prod, v_theta, v_abs, v_weff = (
                sem(n) for n in ("v_a", "v_w2", "v_prod", "v_theta", "v_abs", "v_weff"))
            t_sum, t_tab, t_bx = sem("t_sum"), sem("t_tab"), sem("t_bx")
            v_left, v_lbuf, v_mbuf, t_taps, v_rows, taps_out = (
                sem(n) for n in ("v_left", "v_lbuf", "v_mbuf", "t_taps", "v_rows", "taps_out"))

            with nc.Block() as block:
                @block.sync
                def _(sp):
                    for dst, src in PLOADS:
                        sp.dma_start(dst, src).then_inc(p_in, 16)
                    for dst, src in LOADS:
                        sp.dma_start(dst, src).then_inc(w_in, 16)
                    sp.wait_ge(g_clear, 1)
                    sp.dma_start(Wx1[0:D, :], A["Wx1"]).then_inc(w_in, 16)
                    sp.dma_start(Wx1[D:D + 1, :], A["bx1"].unsqueeze(0)).then_inc(w_in, 16)
                    sp.dma_start(Wqkv[D:D + 1, :], A["bqkv"].unsqueeze(0)).then_inc(w_in, 16)
                    sp.dma_start(W1[D:D + 1, :], A["b1"].unsqueeze(0)).then_inc(w_in, 16)
                    sp.dma_start(bx2[96:P, :], A["bx2"]).then_inc(w_in, 16)
                    sp.wait_ge(v_rows, 2 * D // TG + 1)
                    sp.dma_start(taps.ap().rearrange("h (c a b) -> a c h b", c=2, a=NHI)[:, 0], rows[:, 0])\
                      .then_inc(taps_out, 16)
                    sp.dma_start(taps.ap().rearrange("h (c a b) -> a c h b", c=2, a=NHI)[:, 1], rows[:, 1])\
                      .then_inc(taps_out, 16)
                    sp.wait_ge(taps_out, 32)
                    sp.dma_start(whole[:], taps.ap().rearrange("h (c x) -> (h c) x", c=2)).then_inc(taps_in, 16)
                    sp.wait_ge(v_split, 1)
                    sp.dma_start(taps3.ap().rearrange("k h (c x) -> (h c) k x", c=2), split[:]).then_inc(taps_in, 16)
                    sp.wait_ge(taps_in, 32)

                @block.gpsimd
                def _(pool):
                    c = Count(pool, g_step)
                    c.one(pool.memset(phase[0:NS, :], 0.25))
                    c.one(pool.memset(phase[NS:M, :], 0.0))
                    c.one(pool.memset(sgn[0:NS, :], 1.0))
                    c.one(pool.memset(sgn[NS:M, :], -1.0))
                    c.one(pool.iota(ki[:, 0:NLO], pattern=[[1, NLO]], base=0, channel_multiplier=0))
                    c.one(pool.iota(ki[:, NLO:NK], pattern=[[NLO, NHI]], base=0, channel_multiplier=0))
                    c.one(pool.tensor_copy(kf[:], ki[:]))
                    pool.sem_inc(g_modes, 1)
                    c.one(pool.memset(identf[:], 0.0))
                    c.one(pool.memset(identb[:], 0.0))
                    c.one(pool.memset(sel[:], 0.0))
                    c.one(pool.memset(sel[0:3 * NE], 1.0))
                    c.one(pool.memset(Wqkv[D:P, :], 0.0))
                    c.one(pool.memset(W1[D:P, :], 0.0))
                    c.one(pool.memset(onesf[:], 1.0))
                    c.one(pool.memset(Wx1[:], 0.0))
                    c.settle()
                    for m in (identf, identb):
                        c.step(pool.affine_select(out=m[:], in_=m[:], compare_op=ALU.not_equal, fill=1.0, base=0,
                                                  pattern=[[-1, P]], channel_multiplier=1))
                    for lo in (0, NE, 2 * NE):
                        c.one(pool.affine_select(out=sel[0:3 * NE], in_=sel[0:3 * NE], compare_op=ALU.not_equal, fill=2.0, base=-lo,
                                                 pattern=[[-1, NE], [0, D + 1]], channel_multiplier=1))
                    c.one(pool.tensor_scalar(sel[0:3 * NE], sel[0:3 * NE], 1.0, None, ALU.subtract))
                    c.one(pool.memset(Wx1[96:P, :], BIG))
                    big = Wx1[96:P, :].rearrange("k (e x) -> k e x", x=XH)
                    c.one(pool.affine_select(out=big, in_=big, compare_op=ALU.is_equal, fill=0.0, base=0,
                                             pattern=[[-1, NX], [0, XH]], channel_multiplier=1))
                    pool.memset(bx2[:], 0.0).then_inc(g_clear, 1)
                    pool.wait_ge(w_in, 16 * (len(LOADS) + 5))
                    pool.sem_inc(consts, 1)

                @block.scalar
                def _(act):
                    act.wait_ge(p_in, 16 * len(PLOADS))
                    act.activation(dt_[:], ldt[:], ACT.Exp).then_inc(a_dt, 1)
                    act.activation(are[:], arl[:], ACT.Exp).then_inc(a_dt, 1)
                    act.wait_ge(v_a, 1)
                    act.activation(q1[:], a[:], ACT.Tanh, scale=0.5).then_inc(a_tanh, 1)
                    act.wait_ge(v_prod, 1)
                    act.activation(mag[:], mag[:], ACT.Exp).then_inc(a_mag, 1)
                    act.wait_ge(v_w2, 1)
                    act.activation(sc2[:], th2[:], ACT.Sin).then_inc(a_sin2, 1)
                    act.wait_ge(v_theta, 1)
                    act.activation(theta[:], theta[:], ACT.Sin).then_inc(a_sin, 1)

                @block.tensor
                def _(pe):
                    pe.wait_ge(v_abs, 1)
                    pe.matmul(bank[0][0:96, 0:1], onesf[0:96, 0:96], rowsum[:], start=True, stop=True).then_inc(t_sum, 1)
                    pe.wait_ge(v_weff, 1)
                    for c in range(4):
                        last = pe.matmul(bank[1][:, ts(c, D)], Et[:, c, :], weff[:], start=True, stop=True)
                    last.then_inc(t_tab, 1)
                    pe.wait_ge(consts, 1)
                    pe.matmul(bank[4][:, 0:D], onesf[96:P, :], bx2[96:P, :], start=True, stop=True).then_inc(t_bx, 1)
                    pe.wait_ge(v_left, 1)
                    with pe.Fori(0, D // TG) as g:
                        pe.wait_ge(v_lbuf, g + 1)
                        pe.wait_ge(v_mbuf, 2 * g + 2)
                        apart(pe, spare)
                        for hh in range(TG):
                            for c in range(2):
                                last = pe.matmul(bank[2 + c][0:NHI, ts(hh, NLO)], lbuf[:, c, hh, :], mbuf[:, c, hh, :],
                                                 start=True, stop=True)
                        last.then_inc(t_taps, 1)

                @block.vector
                def _(dve):
                    c = Count(dve, v_step)

                    def reduced(ang, trn, plus):
                        c.one(dve.tensor_scalar(trn, ang, 1.0 / (2.0 * 3.141592653589793), plus, ALU.mult, ALU.add))
                        c.one(dve.tensor_scalar(trn, trn, MAGIC, MAGIC, ALU.add, ALU.subtract))
                        c.one(dve.scalar_tensor_tensor(out=ang, in0=trn, scalar=-TWO_PI_HI, in1=ang,
                                                       op0=ALU.mult, op1=ALU.add))
                        c.one(dve.scalar_tensor_tensor(out=ang, in0=trn, scalar=-TWO_PI_LO, in1=ang,
                                                       op0=ALU.mult, op1=ALU.add))

                    dve.wait_ge(g_modes, 1)
                    dve.wait_ge(a_dt, 2)
                    c.one(dve.tensor_scalar(are[:], are[:], -1.0, None, ALU.mult))
                    c.step(dve.tensor_tensor(w[:], dt_[:], aim[:], ALU.mult))
                    c.one(dve.tensor_tensor(a[:], dt_[:], are[:], ALU.mult))
                    dve.engine_nop().then_inc(v_a, 1)
                    kb = bc(kf[:].unsqueeze(1), [M, D, NK])
                    dve.tensor_tensor(mag[:], bc(a[:].unsqueeze(2), [M, D, NK]), kb, ALU.mult).then_inc(v_prod, 1)
                    c.one(dve.tensor_scalar(th2[:, 0, :], w[:], 0.5, None, ALU.mult))
                    c.one(dve.tensor_scalar(th2[:, 1, :], th2[:, 0, :], 1.0, None, ALU.mult))
                    reduced(th2[:, 0, :], tn2[:, 0, :], 0.0)
                    reduced(th2[:, 1, :], tn2[:, 1, :], 0.25)
                    c.one(dve.tensor_scalar(th2[:, 1, :], th2[:, 1, :], 1.5707963267948966, None, ALU.add))
                    c.one(dve.tensor_scalar(th2[:], th2[:], PI_SAFE, -PI_SAFE, ALU.min, ALU.max))
                    dve.engine_nop().then_inc(v_w2, 1)
                    c.one(dve.tensor_tensor(theta[:], bc(w[:].unsqueeze(2), [M, D, NK]), kb, ALU.mult))
                    reduced(theta[:], turns[:], phase[:, 0:1])
                    c.one(dve.tensor_scalar(q4[:, 0:1], phase[:], 4 * 1.5707963267948966, None, ALU.mult))
                    c.one(dve.tensor_scalar(theta[:], theta[:], q4[:, 0:1], PI_SAFE, ALU.add, ALU.min))
                    c.one(dve.tensor_scalar(theta[:], theta[:], -PI_SAFE, None, ALU.max))
                    dve.engine_nop().then_inc(v_theta, 1)
                    dve.wait_ge(consts, 1)
                    c.one(dve.scalar_tensor_tensor(out=absw[:], in0=WT[:], scalar=-1.0, in1=WT[:],
                                                   op0=ALU.mult, op1=ALU.max))
                    dve.tensor_reduce(rowsum[:], absw[:], AX_X, ALU.add).then_inc(v_abs, 1)
                    dve.wait_ge(t_sum, 1)
                    c.one(dve.tensor_scalar(scl[:], bank[0][0:96, 0:1], 1.0 / (96 * D), None, ALU.mult))
                    c.one(dve.tensor_scalar(half[:], scl[:], 1e-8, 0.5, ALU.add, ALU.mult))
                    c.one(dve.tensor_scalar(nhalf[:], half[:], -1.0, None, ALU.mult))
                    c.step(dve.tensor_scalar(wpos[:], WT[:], half[:], None, ALU.is_gt))
                    c.one(dve.tensor_scalar(wneg[:], WT[:], nhalf[:], None, ALU.is_lt))
                    c.one(dve.tensor_tensor(wpos[:], wpos[:], wneg[:], ALU.subtract))
                    c.one(dve.scalar_tensor_tensor(out=wneg[:], in0=wpos[:], scalar=scl[:], in1=WT[:],
                                                   op0=ALU.mult, op1=ALU.subtract))
                    dve.tensor_tensor(weff[:], wneg[:], WT[:], ALU.add).then_inc(v_weff, 1)
                    dve.wait_ge(t_tab, 1)
                    c.one(dve.tensor_copy(tabf[:].rearrange("p c d -> p (c d)"), bank[1][:, 0:4 * D]))
                    c.one(dve.tensor_tensor(tabf[0:64, 0, :], tabf[0:64, 0, :], tokb[0:64, :], ALU.add))
                    for x, r, parts in ((tabf, tabr, [table[:, :, i, :] for i in range(3)]),
                                        (b2f, b2r, [b2p[:, i, :] for i in range(3)])):
                        split3(dve, c, x[:], r[:], parts)
                    dve.wait_ge(t_bx, 1)
                    c.one(dve.tensor_copy(bx2[D:D + 1, :], bank[4][D:D + 1, 0:D]))
                    dve.wait_ge(a_tanh, 1)
                    c.one(dve.tensor_scalar(q2[:], q1[:], -1.0, 1.0, ALU.mult, ALU.add))
                    c.one(dve.reciprocal(q3[:], q2[:]))
                    c.one(dve.scalar_tensor_tensor(out=em[:], in0=q1[:], scalar=2.0, in1=q3[:],
                                                   op0=ALU.mult, op1=ALU.mult))
                    dve.wait_ge(a_sin2, 1)
                    c.step(dve.scalar_tensor_tensor(out=q1[:], in0=sc2[:, 0, :], scalar=-2.0, in1=sc2[:, 0, :],
                                                    op0=ALU.mult, op1=ALU.mult))
                    c.one(dve.scalar_tensor_tensor(out=q2[:], in0=sc2[:, 0, :], scalar=2.0, in1=sc2[:, 1, :],
                                                   op0=ALU.mult, op1=ALU.mult))
                    c.one(dve.scalar_tensor_tensor(out=q3[:], in0=q1[:], scalar=1.0, in1=em[:],
                                                   op0=ALU.add, op1=ALU.mult))
                    c.step(dve.tensor_tensor(er[:], q3[:], q1[:], ALU.add))
                    c.one(dve.scalar_tensor_tensor(out=ei[:], in0=em[:], scalar=1.0, in1=q2[:],
                                                   op0=ALU.add, op1=ALU.mult))
                    c.step(dve.tensor_tensor(q1[:], are[:], are[:], ALU.mult))
                    c.one(dve.tensor_tensor(q2[:], aim[:], aim[:], ALU.mult))
                    c.one(dve.tensor_tensor(q3[:], q1[:], q2[:], ALU.add))
                    c.one(dve.reciprocal(q1[:], q3[:]))
                    c.step(dve.tensor_tensor(yr[:], er[:], are[:], ALU.mult))
                    c.step(dve.tensor_tensor(q2[:], ei[:], aim[:], ALU.mult))
                    c.step(dve.tensor_tensor(yi[:], ei[:], are[:], ALU.mult))
                    c.one(dve.tensor_tensor(q4[:], er[:], aim[:], ALU.mult))
                    c.step(dve.tensor_tensor(yr[:], yr[:], q2[:], ALU.add))
                    c.one(dve.tensor_tensor(yi[:], yi[:], q4[:], ALU.subtract))
                    c.step(dve.scalar_tensor_tensor(out=yr[:], in0=yr[:], scalar=2.0, in1=q1[:], op0=ALU.mult, op1=ALU.mult))
                    c.one(dve.scalar_tensor_tensor(out=yi[:], in0=yi[:], scalar=2.0, in1=q1[:], op0=ALU.mult, op1=ALU.mult))
                    yrb, yib = bc(yr[:].unsqueeze(1), [M, 2, D]), bc(yi[:].unsqueeze(1), [M, 2, D])
                    c.step(dve.tensor_tensor(cr[:], cre[:], yrb, ALU.mult))
                    c.one(dve.tensor_tensor(cs[:], cim[:], yib, ALU.mult))
                    c.one(dve.tensor_tensor(cr[:], cr[:], cs[:], ALU.subtract))
                    c.step(dve.tensor_tensor(ci[:], cre[:], yib, ALU.mult))
                    c.one(dve.tensor_tensor(cs[:], cim[:], yrb, ALU.mult))
                    c.one(dve.tensor_tensor(ci[:], ci[:], cs[:], ALU.add))
                    c.step(dve.tensor_scalar(cr[:], cr[:], sgn[:, 0:1], None, ALU.mult))
                    c.one(dve.tensor_scalar(ci[:], ci[:], -1.0, None, ALU.mult))
                    dve.wait_ge(a_mag, 1)
                    dve.wait_ge(a_sin, 1)
                    c.one(dve.tensor_tensor(theta[:], theta[:], mag[:], ALU.mult))
                    c.step(dve.tensor_copy(hi_sw[0:NS], theta[NS:M, :, NLO:NK]))
                    c.step(dve.tensor_copy(hi_sw[NS:M], theta[0:NS, :, NLO:NK]))
                    c.one(dve.tensor_copy(lo_rev[:], theta[:, :, 0:NLO][:, :, ::-1]))
                    for way, src in ((0, 1), (1, 0)):
                        e1, e2 = theta[:, :, NLO:NK], hi_sw[:]
                        if way == 0:
                            e1, e2 = e1[:, :, ::-1], e2[:, :, ::-1]
                        c.step(dve.tensor_tensor(left[:, way], bc(cr[:, src, :].unsqueeze(2), [M, D, NHI]), e1, ALU.mult))
                        c.one(dve.tensor_tensor(lt2[:, way], bc(ci[:, src, :].unsqueeze(2), [M, D, NHI]), e2, ALU.mult))
                        c.one(dve.tensor_tensor(left[:, way], left[:, way], lt2[:, way], ALU.add))
                    dve.engine_nop().then_inc(v_left, 1)
                    with dve.Fori(0, D // TG) as g:
                        dve.tensor_copy(mbuf[:, 0], lo_rev[:, bass.ds(g * TG, TG), :]).then_inc(v_mbuf, 1)
                        dve.tensor_copy(mbuf[:, 1], theta[:, bass.ds(g * TG, TG), 0:NLO]).then_inc(v_mbuf, 1)
                        dve.tensor_copy(lbuf[:], left[:, :, bass.ds(g * TG, TG), :]).then_inc(v_lbuf, 1)
                        dve.wait_ge(t_taps, g + 1)
                        dve.tensor_copy(rows[:, 0, bass.ds(g * TG, TG), :],
                                        bank[2][0:NHI, 0:TG * NLO].rearrange("a (h b) -> a h b", h=TG))\
                           .then_inc(v_rows, 1)
                        dve.tensor_copy(rows[:, 1, bass.ds(g * TG, TG), :],
                                        bank[3][0:NHI, 0:TG * NLO].rearrange("a (h b) -> a h b", h=TG))\
                           .then_inc(v_rows, 1)
                    dve.wait_ge(v_rows, 2 * D // TG)
                    dve.tensor_tensor(rows[0:1, 1, :, 0], rows[0:1, 1, :, 0], skip[:], ALU.add).then_inc(v_rows, 1)
                    dve.wait_ge(taps_in, 16)
                    split3(dve, c, whole[:], rest[:], [split[:, k, :] for k in range(3)])
                    dve.sem_inc(v_split, 1)

        def stats(dve, c, x, st, mv, done):
            apart(dve, spare)
            for j in range(TJ):
                c.step(dve.bn_stats(st[:, j, :], x[:, j, :]))
            c.settle()
            apart(dve, spare)
            for j in range(TJ):
                last = dve.bn_aggr(mv[:, j, :], st[:, j, :])
                if j < TJ - 1:
                    c.step(last)
            last.then_inc(done.sem, 1)

        def rstd(pool, c, ready, b, mv, rs, power, done, n=None):
            pool.wait_ge(ready.sem, ready.nth(b, n))
            apart(pool, spare)
            c.one(pool.tensor_scalar(rs[:], mv[:, :, 1], EPS, None, ALU.add))
            pool.tensor_tensor(rs[:], rs[:], power[:], ALU.pow).then_inc(done.sem, 1)

        def centre(dve, c, x, mv, rs, dst):
            for j in range(TJ):
                c.step(dve.tensor_scalar(dst[:, j, :], x[:, j, :], mv[:, j, 0:1], rs[:, j:j + 1],
                                         ALU.subtract, ALU.mult))

        def tiled(ap):
            return ap.rearrange("p (j d) -> p j d", j=TJ)

        with ExitStack() as own:
            def tmp(name, shape, dt=F32):
                return own.enter_context(nc.sbuf_tensor(name, shape, dt))

            ids = [tmp(f"ids{r}", [P, 4, 2, S], I32) for r in range(2)]
            onehot = [tmp(f"onehot{r}", [P, 4, 2, S], BF16) for r in range(2)]
            rowi = tmp("rowi", [P, 2], I32)
            rowf = tmp("rowf", [P, 2])
            power = tmp("power_e", [P, TJ])
            tiny = [[tmp(f"{n}e{q}", [P, TJ] + s) for n, s in (("st", [6]), ("mv", [2]), ("rs", []))] for q in range(2)]
            xn = [tmp(f"xn_e{q}", [P, TJ, D]) for q in range(2)]
            xg = [tmp(f"xg_e{q}", [P, TJ, D]) for q in range(2)]
            ids_in = [sem("ids_in_even"), sem("ids_in_odd")]
            g_row = sem("g_row")
            v_hot, t_z = Signal(sem("v_hot"), 2, 2), Signal(sem("t_z"), 2, 2)
            v_stats, g_rstd = Signal(sem("v_stats_e"), 2), Signal(sem("g_rstd_e"), 2)
            v_norm, g_gain, g_h = Signal(sem("v_norm_e"), 2 * TJ, 2), Signal(sem("g_gain_e"), 2), Signal(sem("g_h"), 2)
            g_step, v_step = sem("g_step_e"), sem("v_step_e")
            IDS = [(0, 0, 64, "x"), (0, 64, P, "itok_BS_0_255"), (2, 0, P, "itok_BS_0_511"),
                   (3, 0, P, "itok_BS_0_127"), (1, 0, 64, "itok_BS_0_63"), (1, 64, 68, "itok_BS_0_3")]
            NP = NB // 2
            VSTEP, GSTEP = 2 * (2 * TJ - 1), 2

            def pairs(eng, step):
                step(0, 0, None)
                with eng.Fori(0, NP // 2 - 1) as i:
                    step(2 * i + 1, 1, 2 * i)
                    step(2 * i + 2, 0, 2 * i + 1)
                step(NP - 1, 1, NP - 2)
                step(None, 0, NP - 1)

            with nc.Block() as block:
                @block.sync
                def _(sp):
                    sp.wait_ge(g_row, 5)
                    with sp.Fori(0, NP // 2) as i:
                        for r in range(2):
                            p = 2 * i + r
                            sp.wait_ge(v_hot.sem, v_hot.before(p, 2))
                            for c, lo, hi, name in IDS:
                                src = A[name][bass.ds(2 * p, 2), :].rearrange("a s -> (a s)")
                                sp.dma_start(ids[r][lo:hi, c].rearrange("v a s -> v (a s)"), src.partition_broadcast(hi - lo))\
                                  .then_inc(ids_in[r], 16)

                @block.gpsimd
                def _(pool):
                    c = Count(pool, g_row)
                    c.one(pool.memset(ids[0][64:P, 1], -1))
                    c.one(pool.memset(ids[1][64:P, 1], -1))
                    c.one(pool.memset(power[:], -0.5))
                    c.one(pool.iota(rowi[:, 1:2], pattern=[[0, 1]], base=0, channel_multiplier=1))
                    c.one(pool.iota(rowi[0:64, 0:1], pattern=[[0, 1]], base=0, channel_multiplier=1))
                    c.one(pool.iota(rowi[64:P, 0:1], pattern=[[0, 1]], base=0, channel_multiplier=1))
                    c.one(pool.tensor_copy(rowf[:], rowi[:]))
                    g_gain.grant(pool)
                    g_rstd.grant(pool)
                    g_h.grant(pool)
                    with pool.Fori(0, NP) as p:
                        c = Count(pool, g_step, GSTEP * p)
                        for k in range(2):
                            rstd(pool, c, v_stats, p, tiny[k][1], tiny[k][2], power, g_rstd, k + 1)
                        for k in range(2):
                            pool.wait_ge(v_norm.sem, v_norm.nth(p, (k + 1) * TJ))
                            pool.tensor_tensor(xg[k][:], xn[k][:], bc(gam0[:].unsqueeze(1), [P, TJ, D]), ALU.mult)\
                                .then_inc(g_gain.sem, 1)
                            pool.wait_ge(g_gain.sem, g_gain.nth(p, k + 1))
                            pool.tensor_tensor(tiled(h[:, ts(2 * p + k, ROW)]), xg[k][:], bc(bet0[:].unsqueeze(1), [P, TJ, D]),
                                               ALU.add).then_inc(g_h.sem, 1)

                @block.vector
                def _(dve):
                    dve.wait_ge(g_row, 7)
                    for s in (v_hot, v_stats, v_norm):
                        s.grant(dve)

                    def step(p, r, q):
                        if p is not None:
                            dve.wait_ge(ids_in[r], 48 * p - 48 * r + 96)
                            dve.wait_ge(t_z.sem, t_z.before(p, 2))
                            for half_ in range(2):
                                dve.tensor_scalar(onehot[r][:, 2 * half_:2 * half_ + 2], ids[r][:, 2 * half_:2 * half_ + 2],
                                                  rowf[:, half_:half_ + 1], None, ALU.is_equal).then_inc(v_hot.sem, 1)
                        if q is not None:
                            c = Count(dve, v_step, VSTEP * q)
                            z = [tiled(bank[2 * (1 - r) + k][:, 0:ROW]) for k in range(2)]
                            for k in range(2):
                                dve.wait_ge(t_z.sem, t_z.nth(q, k + 1))
                                stats(dve, c, z[k], tiny[k][0], tiny[k][1], v_stats)
                            for k in range(2):
                                dve.wait_ge(g_rstd.sem, g_rstd.nth(q, k + 1))
                                dve.wait_ge(g_gain.sem, g_gain.before(q))
                                for j in range(TJ):
                                    dve.tensor_scalar(xn[k][:, j, :], z[k][:, j, :], tiny[k][1][:, j, 0:1], tiny[k][2][:, j:j + 1],
                                                      ALU.subtract, ALU.mult).then_inc(v_norm.sem, 1)
                            assert c.n == VSTEP, c.n

                    pairs(dve, step)

                @block.tensor
                def _(pe):
                    t_z.grant(pe)

                    def step(p, r, q):
                        if p is None:
                            return
                        pe.wait_ge(v_hot.sem, v_hot.nth(p))
                        pe.wait_ge(v_norm.sem, v_norm.before(p, 2))
                        for k in range(2):
                            for j in range(TJ):
                                for m in range(12):
                                    c, part = m // 3, m % 3
                                    last = pe.matmul(bank[2 * r + k][:, ts(j, D)], onehot[r][:, c, k, ts(j, P)],
                                                     table[:, c, part, :], start=(m == 0), stop=(m == 11))
                            last.then_inc(t_z.sem, 1)

                    pairs(pe, step)

        with ExitStack() as own:
            def tmp(name, shape, dt=F32):
                return own.enter_context(nc.sbuf_tensor(name, shape, dt))

            def signals(names, each=1):
                return (Signal(sem(n), each) for n in names.split())

            power = tmp("power", [P, TJ])
            tiny = [[tmp(f"{n}{k}", [P, TJ] + s) for n, s in (("st", [6]), ("mv", [2]), ("rs", []))] for k in range(3)]
            hb, xn = tmp("hb", [P, TJ, D]), tmp("xn", [P, TJ, D])
            xT, qT, kT, vT = tmp("xT", [P, S]), tmp("qT", [P, S]), tmp("kT", [P, S]), tmp("vT", [D, S])
            vo = tmp("vo", [P, TJ, D])
            sc, ms = tmp("sc", [P, TJ, S]), tmp("ms", [P, TJ, S])
            mx, nm, rsum, rinv = (tmp(n, [P, TJ]) for n in ("mx", "nm", "rsum", "rinv"))
            ksum = tmp("ksum", [D, 1])
            point, low, high, gap = (tmp(n, [P, 2, TJ]) for n in ("point", "low", "high", "gap"))
            is_low, is_high = tmp("is_low", [P, TJ], U32), tmp("is_high", [P, TJ], U32)
            frac, inv, tally = tmp("frac", [P, TJ]), tmp("inv", [P, TJ]), tmp("tally", [P, OWN])
            exact, rank, thr, near, bad = (tmp(n, [P, TJ]) for n in ("exact", "rank", "thr", "near", "bad"))
            top8, hit8, order8 = tmp("top8", [P, TJ, 8]), tmp("hit8", [P, TJ, 8]), tmp("order8", [P, 8])
            order8i = tmp("order8i", [P, 8], I32)
            nbadf, nbad = tmp("nbadf", [1, 1]), tmp("nbad", [1, 1], I32)
            onecol = tmp("onecol", [P, 1])
            junk, ajunk = tmp("junk", [P, TJ, S], BF16), tmp("ajunk", [P, TJ, S], BF16)
            lo, mid, delta, cnt, up = (tmp(n, [P, TJ]) for n in ("lo", "mid", "delta", "cnt", "up"))
            eT = tmp("eT", [P, 2, TJ, P])
            xn2, x2T = tmp("xn2", [P, TJ, D]), tmp("x2T", [D + 1, S])
            gate, top = tmp("gate", [P, TJ, NE]), tmp("top", [P, TJ, NE])
            gd, ge, gm, comb, cres = (tmp(n, [P, TJ, NE]) for n in ("gd", "ge", "gm", "comb", "cres"))
            gsum, grec = tmp("gsum", [P, TJ]), tmp("grec", [P, TJ])
            c24 = tmp("c24", [P, TJ, 3, NE], BF16)
            cT = tmp("cT", [P, S], BF16)
            xe = tmp("xe", [P, 2, S])
            hid = tmp("hid", [P, 2, HH, S])

            v_stats, v_k, v_nm = signals("v_stats v_k v_nm")
            g_rstd, g_hb = signals("g_rstd g_hb")
            t_xT, t_qk, t_vT, t_vo = signals("t_xT t_qk t_vT t_vo")
            a_xT, a_q, a_vT, a_vo, a_mean = signals("a_xT a_q a_vT a_vo a_mean")
            t_s, v_sc, v_ms, a_e, t_eT, t_o, v_h1 = signals("t_s v_sc v_ms a_e t_eT t_o v_h1", TJ)
            v_eT, a_eT = signals("v_eT a_eT", TJ // 2)
            v_st2, v_gd, v_c24 = signals("v_st2 v_gd v_c24")
            g_rs2, g_rs3 = signals("g_rs2 g_rs3")
            g_xn, g_xn2, g_u = signals("g_xn g_xn2 g_u", 2)
            dif = tmp("dif", [P, TJ, D])
            t_x2T, t_gate, t_cT = signals("t_x2T t_gate t_cT")
            a_x2T, a_ge, a_cT = signals("a_x2T a_ge a_cT")
            t_bc, v_xe, t_h0, t_h1, a_h0, a_h1, t_w2 = signals("t_bc v_xe t_h0 t_h1 a_h0 a_h1 t_w2", NE)
            v_h2, v_st3 = signals("v_h2 v_st3")
            a_yT, a_oT, t_y2, t_o2 = signals("a_yT a_oT t_y2 t_o2")
            yT, oT = tmp("yT", [D, S]), tmp("oT", [D, S])
            g_step_n, g_step_g, g_step_x = (sem(n) for n in ("g_step_n", "g_step_g", "g_step_x"))
            v_step_n, v_step_a, v_step_g, v_step_x = (sem(n) for n in ("v_step_n", "v_step_a", "v_step_g", "v_step_x"))
            v_bis, ones_in = sem("v_bis"), sem("ones_in")
            v_pt, v_cnt, a_cnt = (Signal(sem(n), k) for n, k in
                                  (("v_pt", SEARCH), ("v_cnt", SEARCH * OWN), ("a_cnt", SEARCH * (TJ - OWN))))
            v_bad, t_bad = Signal(sem("v_bad")), Signal(sem("t_bad"))
            BSTEP = 8
            FSTEP = 3 + BSTEP * BISECT + 1
            NFILL = 11
            VSTEP_N, VSTEP_A, VSTEP_G, VSTEP_X = 7, 72, 23, 7
            XT_SLOT, QKV_SLOT = 2, 4

            def stages(eng, step):
                step(0, None, None, None)
                step(1, 0, None, None)
                step(2, 1, 0, None)
                with eng.Fori(2, NB - 1) as b:
                    step(b + 1, b, b - 1, b - 2)
                step(None, NB - 1, NB - 2, NB - 3)
                step(None, None, NB - 1, NB - 2)
                step(None, None, None, NB - 1)

            with nc.Block() as block:
                @block.gpsimd
                def _(pool):
                    fills = ((power[:], -0.5), (xT[D:P, :], 0.0), (xT[D:D + 1, :], 1.0), (x2T[D:D + 1, :], 1.0), (onecol[:], 1.0),
                             (qT[D:P, :], 0.0), (kT[D:P, :], 0.0), (cT[:], 0.0), (xe[D:P], 0.0))
                    for k, (t, value) in enumerate(fills):
                        pool.memset(t, value).then_inc(ones_in, 1)
                        pool.wait_ge(ones_in, k + 1)
                    pool.iota(order8i[:], pattern=[[1, 8]], base=0, channel_multiplier=0).then_inc(ones_in, 1)
                    pool.wait_ge(ones_in, len(fills) + 1)
                    pool.tensor_copy(order8[:], order8i[:]).then_inc(ones_in, 1)
                    for s in (g_rstd, g_hb, g_rs2, g_rs3, g_xn, g_xn2, g_u):
                        s.grant(pool)

                    def step(n, a, g, x):
                        if a is not None:
                            pool.wait_ge(v_h1.sem, v_h1.before(a))
                            pool.tensor_tensor(hb[:], tiled(h[:, ts(a, ROW)]), bc(bo[:].unsqueeze(1), [P, TJ, D]), ALU.add)\
                                .then_inc(g_hb.sem, 1)
                        if n is not None:
                            rstd(pool, Count(pool, g_step_n, n), v_stats, n, tiny[0][1], tiny[0][2], power, g_rstd)
                            pool.wait_ge(t_xT.sem, t_xT.before(n))
                            normalise(n, tiny[0], xn[:], g_rstd, g_xn)
                        if g is not None:
                            rstd(pool, Count(pool, g_step_g, g), v_st2, g, tiny[1][1], tiny[1][2], power, g_rs2)
                            pool.wait_ge(t_x2T.sem, t_x2T.before(g))
                            normalise(g, tiny[1], xn2[:], g_rs2, g_xn2)
                        if x is not None:
                            rstd(pool, Count(pool, g_step_x, x), v_st3, x, tiny[2][1], tiny[2][2], power, g_rs3)
                            normalise(x, tiny[2], u[:, bass.ds(TJ * x, TJ), :], g_rs3, g_u)

                    def normalise(b, small, dst, ready, done):
                        pool.wait_ge(ready.sem, ready.nth(b))
                        pool.tensor_tensor(dif[:], tiled(h[:, ts(b, ROW)]), bc(small[1][:, :, 0:1], [P, TJ, D]),
                                           ALU.subtract).then_inc(done.sem, 1)
                        pool.wait_ge(done.sem, done.nth(b, 1))
                        pool.tensor_tensor(dst, dif[:], bc(small[2][:].unsqueeze(2), [P, TJ, D]), ALU.mult).then_inc(done.sem, 1)

                    stages(pool, step)

                @block.scalar
                def _(act):
                    for s in (a_mean, a_cnt, a_xT, a_q, a_vT, a_vo, a_e, a_eT, a_x2T, a_ge, a_cT, a_h0, a_h1, a_yT, a_oT):
                        s.grant(act)

                    def counts(a, k):
                        act.wait_ge(v_pt.sem, v_pt.nth(a, k + 1))
                        for j in range(OWN, TJ):
                            if k:
                                act.wait_ge(a_cnt.sem, a_cnt.nth(a, (k - 1) * (TJ - OWN) + j - OWN + 1))
                            act.activation(ajunk[:, j, :], sc[:, j, :], ACT.Sign, bias=point[:, 0, j:j + 1],
                                           scale=-1.0, accum_out=point[:, 1, j:j + 1]).then_inc(a_cnt.sem, 1)

                    def hidden(x, e):
                        for half_, hidden_in, done in ((0, t_h0, a_h0), (1, t_h1, a_h1)):
                            act.wait_ge(hidden_in.sem, hidden_in.nth(x, e + 1))
                            act.wait_ge(t_w2.sem, t_w2.nth(x, e - 1) if e > 1 else t_w2.before(x))
                            act.activation(hid[:, e % 2, half_, :], bank[6 + half_][:], ACT.Relu).then_inc(done.sem, 1)

                    def exps(a, j):
                        act.wait_ge(v_ms.sem, v_ms.nth(a, j + 1))
                        act.activation(ms[:, j, :], ms[:, j, :], ACT.Exp, bias=nm[:, j:j + 1], scale=0.125,
                                       accum_out=rsum[:, j:j + 1]).then_inc(a_e.sem, 1)

                    def take_exps(a, j):
                        act.wait_ge(t_eT.sem, t_eT.nth(a, j + 1))
                        act.wait_ge(t_o.sem, t_o.nth(a, j - 1) if j > 1 else t_o.before(a))
                        act.activation(eT[:, 1], bank[3][:].rearrange("p (c q) -> p c q", c=TJ), ACT.Copy)\
                           .then_inc(a_eT.sem, 1)

                    def step(n, a, g, x):
                        if a is not None:
                            act.wait_ge(t_vo.sem, t_vo.nth(a))
                            act.activation(vo[:], tiled(bank[0][:, 0:ROW]), ACT.Copy).then_inc(a_vo.sem, 1)
                            act.activation(point[:, 0, :], bank[0][:, ROW:ROW + TJ], ACT.Copy, scale=1.0 / S)\
                               .then_inc(a_mean.sem, 1)
                        if x is not None:
                            hidden(x, 0)
                        for k in range(NE):
                            if a is not None and k < SEARCH:
                                counts(a, k)
                            if x is not None and k + 1 < NE:
                                hidden(x, k + 1)
                            if n is not None and k == XT_SLOT:
                                act.wait_ge(t_xT.sem, t_xT.nth(n))
                                act.activation(xT[0:D, :], bank[2][0:D, :], ACT.Copy).then_inc(a_xT.sem, 1)
                            if n is not None and k == QKV_SLOT:
                                act.wait_ge(t_qk.sem, t_qk.nth(n))
                                act.activation(qT[0:D, :], bank[1][0:D, :], ACT.Copy).then_inc(a_q.sem, 1)
                                act.wait_ge(t_vT.sem, t_vT.nth(n))
                                act.activation(vT[:], bank[2][0:D, :], ACT.Copy).then_inc(a_vT.sem, 1)
                        if g is not None:
                            act.wait_ge(t_x2T.sem, t_x2T.nth(g))
                            act.activation(x2T[0:D, :], bank[5][0:D, :], ACT.Copy).then_inc(a_x2T.sem, 1)
                        if x is not None:
                            act.wait_ge(t_w2.sem, t_w2.nth(x))
                            act.activation(yT[:], bank[4][0:D, :], ACT.Copy).then_inc(a_yT.sem, 1)
                        if a is not None:
                            act.wait_ge(v_nm.sem, v_nm.nth(a))
                            exps(a, 0)
                            exps(a, 1)
                            take_exps(a, 1)
                            exps(a, 2)
                            exps(a, 3)
                        if g is not None:
                            act.wait_ge(v_gd.sem, v_gd.nth(g))
                            act.activation(ge[:], gd[:], ACT.Exp).then_inc(a_ge.sem, 1)
                        if a is not None:
                            take_exps(a, 3)
                            act.wait_ge(t_o.sem, t_o.nth(a))
                            act.activation(oT[:], bank[0][0:D, :], ACT.Copy).then_inc(a_oT.sem, 1)
                        if g is not None:
                            act.wait_ge(t_cT.sem, t_cT.nth(g))
                            act.activation(cT[0:3 * NE, :], bank[5][:].bitcast(BF16)[0:3 * NE, 0:S], ACT.Copy)\
                               .then_inc(a_cT.sem, 1)

                    act.wait_ge(ones_in, NFILL)
                    stages(act, step)

                @block.tensor
                def _(pe):
                    for s in (t_bad, t_xT, t_qk, t_vT, t_vo, t_s, t_eT, t_o, t_x2T, t_gate, t_cT, t_bc, t_h0, t_h1, t_w2, t_y2, t_o2):
                        s.grant(pe)
                    pe.wait_ge(ones_in, NFILL)

                    def features(x, ready, into, done, b):
                        pe.wait_ge(ready.sem, ready.nth(b))
                        apart(pe, spare)
                        for j in range(TJ):
                            last = pe.transpose(into[0:D, ts(j, P)], x[:, j, :], identf[:])
                        last.then_inc(done.sem, 1)

                    def scores(a, j):
                        if j == 0:
                            pe.wait_ge(a_vT.sem, a_vT.nth(a))
                            pe.wait_ge(a_q.sem, a_q.nth(a))
                            pe.wait_ge(v_k.sem, v_k.nth(a))
                        if j >= 2:
                            pe.wait_ge(v_sc.sem, v_sc.nth(a, j - 1))
                        pe.matmul(bank[2 + j % 2][:], qT[:, ts(j, P)], kT[:], start=True, stop=True).then_inc(t_s.sem, 1)

                    def weighted(a, j):
                        done = (v_eT, a_eT)[j % 2]
                        pe.wait_ge(done.sem, done.nth(a, j // 2 + 1))
                        for k in range(TJ):
                            last = pe.matmul(bank[0][0:D, ts(j, P)], vo[:, k, :], eT[:, j % 2, k, :],
                                             start=(k == 0), stop=(k == TJ - 1))
                        last.then_inc(t_o.sem, 1)

                    def share(x, e):
                        pe.wait_ge(v_xe.sem, v_xe.nth(x, e) if e else v_xe.before(x))
                        pe.matmul(bank[5][0:D + 1, :], sel[:, e, :], cT[:], start=True, stop=True).then_inc(t_bc.sem, 1)

                    def first(x, e):
                        pe.wait_ge(v_xe.sem, v_xe.nth(x, e + 1))
                        for half_, taken, done in ((0, a_h0, t_h0), (1, a_h1, t_h1)):
                            pe.wait_ge(taken.sem, taken.nth(x, e) if e else taken.before(x))
                            pe.matmul(bank[6 + half_][:], W1[:, ts(HH * e + half_, P)], xe[:, e % 2, :],
                                      start=True, stop=True).then_inc(done.sem, 1)

                    def second(x, e, half_):
                        taken = (a_h0, a_h1)[half_]
                        pe.wait_ge(taken.sem, taken.nth(x, e + 1))
                        last = pe.matmul(bank[4][0:D, :], W2[:, HH * e + half_, :], hid[:, e % 2, half_, :], start=False,
                                         stop=(e == NE - 1 and half_ == HH - 1))
                        if half_ == HH - 1:
                            last.then_inc(t_w2.sem, 1)

                    def to_tokens(src, ready, into, done, b):
                        pe.wait_ge(ready.sem, ready.nth(b))
                        apart(pe, spare)
                        for j in range(TJ):
                            last = pe.transpose(into[:, ts(j, D)], src[:, ts(j, P)], identf[0:D, 0:D])
                        last.then_inc(done.sem, 1)

                    def exps_back(a, j):
                        pe.wait_ge(a_e.sem, a_e.nth(a, j + 1))
                        for k in range(TJ):
                            last = pe.transpose(bank[1 + 2 * (j % 2)][:, ts(k, P)], ms[:, j, ts(k, P)], identf[:])
                        last.then_inc(t_eT.sem, 1)

                    def step(n, a, g, x):
                        if x is not None:
                            pe.wait_ge(a_cT.sem, a_cT.nth(x))
                            share(x, 0)
                        if a is not None:
                            scores(a, 0)
                            pe.wait_ge(a_eT.sem, a_eT.before(a))
                            scores(a, 1)
                            pe.wait_ge(v_h1.sem, v_h1.before(a))
                            for j in range(TJ):
                                pe.matmul(bank[0][:, ts(j, D)], vT[:, ts(j, P)], Wo[:], start=True, stop=True)
                            for j in range(TJ):
                                last = pe.matmul(bank[0][:, ROW + j:ROW + j + 1], qT[0:D, ts(j, P)], ksum[:],
                                                 start=True, stop=True)
                            last.then_inc(t_vo.sem, 1)
                            scores(a, 2)
                            scores(a, 3)
                        if x is not None:
                            pe.wait_ge(v_h2.sem, v_h2.before(x))
                            for k in range(3):
                                pe.matmul(bank[4][0:D, :], b2p[:, k, :], cT[0:3 * NE, :], start=(k == 0), stop=False)
                            first(x, 0)
                        for e in range(NE):
                            if x is not None:
                                if e:
                                    first(x, e)
                                if e + 1 < NE:
                                    share(x, e + 1)
                                if e:
                                    second(x, e - 1, 0)
                                    if e < NE - 1:
                                        second(x, e - 1, 1)
                            if n is not None and e == XT_SLOT:
                                if a is not None:
                                    pe.wait_ge(v_sc.sem, v_sc.nth(a))
                                features(xn, g_xn, bank[2], t_xT, n)
                            if n is not None and e == QKV_SLOT:
                                pe.wait_ge(a_xT.sem, a_xT.nth(n))
                                if a is not None:
                                    pe.wait_ge(v_eT.sem, v_eT.before(a))
                                pe.matmul(bank[1][:], Wqkv[:, 0:2 * D], xT[:], start=True, stop=True).then_inc(t_qk.sem, 1)
                                pe.matmul(bank[2][0:D, :], Wqkv[:, 2 * D:3 * D], xT[:], start=True, stop=True)\
                                  .then_inc(t_vT.sem, 1)
                        if a is not None:
                            pe.wait_ge(a_vo.sem, a_vo.nth(a))
                            pe.wait_ge(v_sc.sem, v_sc.nth(a))
                            pe.wait_ge(v_bad.sem, v_bad.nth(a))
                            pe.matmul(bank[0][0:1, 0:TJ], onecol[:], bad[:], start=True, stop=True).then_inc(t_bad.sem, 1)
                        if x is not None:
                            second(x, NE - 2, 1)
                        if g is not None:
                            pe.wait_ge(v_xe.sem, v_xe.before(g))
                            features(xn2, g_xn2, bank[5], t_x2T, g)
                        if x is not None:
                            second(x, NE - 1, 0)
                            second(x, NE - 1, 1)
                        if g is not None:
                            pe.wait_ge(a_x2T.sem, a_x2T.nth(g))
                            for j in range(TJ):
                                last = pe.matmul(bank[5][:, ts(j, NE)], x2T[:, ts(j, P)], Wg[:], start=True, stop=True)
                            last.then_inc(t_gate.sem, 1)
                        if a is not None:
                            exps_back(a, 0)
                            exps_back(a, 1)
                        if x is not None:
                            to_tokens(yT, a_yT, bank[4], t_y2, x)
                        if a is not None:
                            weighted(a, 0)
                            exps_back(a, 2)
                            weighted(a, 1)
                            exps_back(a, 3)
                            weighted(a, 2)
                            weighted(a, 3)
                        if g is not None:
                            pe.wait_ge(v_c24.sem, v_c24.nth(g))
                            for j in range(TJ):
                                last = pe.transpose(bank[5][:].bitcast(BF16)[0:3 * NE, ts(j, P)],
                                                    c24[:, j].rearrange("p k e -> p (k e)"), identb[:])
                            last.then_inc(t_cT.sem, 1)
                        if a is not None:
                            to_tokens(oT, a_oT, bank[0], t_o2, a)

                    stages(pe, step)

                @block.vector
                def _(dve):
                    for s in (v_pt, v_cnt, v_bad, v_stats, v_k, v_nm, v_sc, v_ms, v_h1, v_eT, v_st2, v_gd, v_c24,
                              v_xe, v_h2, v_st3):
                        s.grant(dve)
                    dve.wait_ge(ones_in, NFILL)

                    def pair(ap):
                        return bc(ap.unsqueeze(1), [P, 2, TJ])

                    def gates_open(c, x):
                        dve.wait_ge(t_gate.sem, t_gate.nth(x))
                        c.one(dve.tensor_copy(gate[:], bank[5][:, 0:TJ * NE].rearrange("p (j e) -> p j e", j=TJ)))
                        apart(dve, spare)
                        for j in range(TJ):
                            c.step(dve.max(top[:, j, :], gate[:, j, :]))
                        c.settle()
                        c.step(dve.tensor_tensor(gd[:], gate[:], bc(top[:, :, 0:1], [P, TJ, NE]), ALU.subtract))
                        c.one(dve.tensor_tensor(gm[:], gate[:], bc(top[:, :, 1:2], [P, TJ, NE]), ALU.is_ge))
                        dve.sem_inc(v_gd.sem, 1)

                    def gates_close(c, x):
                        dve.wait_ge(a_ge.sem, a_ge.nth(x))
                        c.one(dve.tensor_tensor(gm[:], ge[:], gm[:], ALU.mult))
                        c.one(dve.tensor_reduce(gsum[:], gm[:], AX_X, ALU.add))
                        c.one(dve.reciprocal(grec[:], gsum[:]))
                        c.one(dve.tensor_tensor(comb[:], gm[:], bc(grec[:].unsqueeze(2), [P, TJ, NE]), ALU.mult))
                        split3(dve, c, comb[:], cres[:], [c24[:, :, k, :] for k in range(3)])
                        dve.sem_inc(v_c24.sem, 1)

                    def score_tiles(a, tiles):
                        for j in tiles:
                            dve.wait_ge(t_s.sem, t_s.nth(a, j + 1))
                            dve.tensor_scalar(sc[:, j, :], bank[2 + j % 2][:], 1.0, None, ALU.mult, ALU.max,
                                              accum_out=mx[:, j:j + 1]).then_inc(v_sc.sem, 1)

                    def bracket(c, a):
                        dve.wait_ge(v_sc.sem, v_sc.nth(a))
                        c.step(dve.tensor_scalar(nm[:], mx[:], 0.0, -0.125, ALU.max, ALU.mult))
                        dve.wait_ge(a_mean.sem, a_mean.nth(a))
                        c.one(dve.tensor_tensor(frac[:], mx[:], point[:, 0, :], ALU.subtract))
                        dve.sem_inc(v_nm.sem, 1)
                        dve.sem_inc(v_pt.sem, 1)
                        c.step(dve.memset(low[:, 1, :], -0.68 * S))
                        c.step(dve.memset(high[:, 1, :], 0.68 * S))
                        c.one(dve.tensor_scalar(frac[:], frac[:], 1.0 / 3.0, None, ALU.mult))
                        c.step(dve.tensor_tensor(low[:, 0, :], point[:, 0, :], frac[:], ALU.subtract))
                        c.step(dve.tensor_tensor(high[:, 0, :], point[:, 0, :], frac[:], ALU.add))

                    def count(a):
                        for j in range(OWN):
                            dve.tensor_scalar(junk[:, j, :], sc[:, j, :], point[:, 0, j:j + 1], None, ALU.is_ge, ALU.add,
                                              accum_out=tally[:, j:j + 1]).then_inc(v_cnt.sem, 1)

                    def narrow(c, a, k):
                        dve.wait_ge(v_cnt.sem, v_cnt.nth(a, (k + 1) * OWN))
                        c.one(dve.tensor_scalar(point[:, 1, 0:OWN], tally[:], -2.0, S, ALU.mult, ALU.add))
                        dve.wait_ge(a_cnt.sem, a_cnt.nth(a, (k + 1) * (TJ - OWN)))
                        c.step(dve.tensor_scalar(is_low[:], point[:, 1, :], 1.0, None, ALU.is_le))
                        c.one(dve.tensor_scalar(is_high[:], point[:, 1, :], 1.0, None, ALU.is_gt))
                        apart(dve, spare)
                        c.step(dve.copy_predicated(low[:], pair(is_low[:]), point[:]))
                        c.one(dve.copy_predicated(high[:], pair(is_high[:]), point[:]))
                        if k == SEARCH - 1:
                            return
                        c.step(dve.tensor_scalar(frac[:], high[:, 1, :], AIM, 0.0, ALU.subtract, ALU.max))
                        c.one(dve.tensor_tensor(gap[:], high[:], low[:], ALU.subtract))
                        c.step(dve.reciprocal(inv[:], gap[:, 1, :]))
                        c.one(dve.tensor_tensor(frac[:], frac[:], gap[:, 0, :], ALU.mult))
                        c.one(dve.tensor_tensor(frac[:], frac[:], inv[:], ALU.mult))
                        dve.tensor_tensor(point[:, 0, :], high[:, 0, :], frac[:], ALU.subtract).then_inc(v_pt.sem, 1)
                        dve.wait_ge(v_pt.sem, v_pt.nth(a, k + 2))

                    def count_high(c):
                        for j in range(TJ):
                            c.step(dve.tensor_scalar(ms[:, j, :], sc[:, j, :], high[:, 0, j:j + 1], None, ALU.is_ge, ALU.add,
                                                     accum_out=exact[:, j:j + 1]))
                        c.settle()

                    def push_high(c):
                        for j in range(TJ):
                            c.step(dve.scalar_tensor_tensor(out=ms[:, j, :], in0=ms[:, j, :], scalar=-FAR, in1=sc[:, j, :],
                                                            op0=ALU.mult, op1=ALU.add))
                        c.step(dve.tensor_scalar(rank[:], exact[:], -1.0, S / 2 - 1.0, ALU.mult, ALU.add))
                        c.settle()
                        apart(dve, spare)

                    def best_eight(c):
                        for j in range(TJ):
                            c.step(dve.max(top8[:, j, :], ms[:, j, :]))

                    def pick(c):
                        c.one(dve.tensor_tensor(hit8[:], bc(order8[:].unsqueeze(1), [P, TJ, 8]),
                                                bc(rank[:].unsqueeze(2), [P, TJ, 8]), ALU.is_equal))
                        c.step(dve.tensor_reduce(near[:], hit8[:], AX_X, ALU.add))
                        c.one(dve.tensor_tensor(top8[:], top8[:], hit8[:], ALU.mult))
                        dve.tensor_scalar(bad[:], near[:], -1.0, 1.0, ALU.mult, ALU.add).then_inc(v_bad.sem, 1)
                        c.one(dve.tensor_reduce(thr[:], top8[:], AX_X, ALU.add))

                    def load_missed(c, a):
                        dve.wait_ge(t_bad.sem, t_bad.nth(a))
                        c.one(dve.tensor_reduce(nbadf[:], bank[0][0:1, 0:TJ], AX_X, ALU.add))
                        c.one(dve.tensor_copy(nbad[:], nbadf[:]))

                    def general(a):
                        apart(dve, spare)
                        missed = dve.value_load(nbad[:], min_val=0, max_val=P * TJ)
                        with dve.If(missed > 0):
                            f = Count(dve, v_bis, FSTEP * a)
                            f.one(dve.tensor_reduce(lo[:], sc[:], AX_X, ALU.min))
                            f.one(dve.tensor_tensor(delta[:], mx[:], lo[:], ALU.subtract))
                            f.one(dve.tensor_scalar(delta[:], delta[:], 0.50001, 1e-30, ALU.mult, ALU.add))
                            apart(dve, spare)
                            with dve.Fori(0, BISECT) as i:
                                k = Count(dve, v_bis, FSTEP * a + 3 + BSTEP * i)
                                k.one(dve.tensor_tensor(mid[:], lo[:], delta[:], ALU.add))
                                for j in range(TJ):
                                    k.step(dve.tensor_scalar(junk[:, j, :], sc[:, j, :], mid[:, j:j + 1], None, ALU.is_ge, ALU.add,
                                                             accum_out=cnt[:, j:j + 1]))
                                k.settle()
                                k.one(dve.scalar_tensor_tensor(out=up[:], in0=cnt[:], scalar=S / 2 - 0.5, in1=delta[:],
                                                               op0=ALU.is_ge, op1=ALU.mult))
                                k.step(dve.tensor_tensor(lo[:], lo[:], up[:], ALU.add))
                                k.one(dve.tensor_scalar(delta[:], delta[:], 0.5, None, ALU.mult))
                                assert k.n == BSTEP
                            f.n += BSTEP * BISECT
                            f.one(dve.tensor_copy(thr[:], lo[:]))
                            assert f.n == FSTEP
                            apart(dve, spare)
                        with dve.Else():
                            dve.sem_inc(v_bis, FSTEP)

                    def take_exps(a, j):
                        dve.wait_ge(t_eT.sem, t_eT.nth(a, j + 1))
                        dve.wait_ge(t_o.sem, t_o.nth(a, j - 1) if j else t_o.before(a))
                        dve.tensor_copy(eT[:, 0], bank[1][:].rearrange("p (c q) -> p c q", c=TJ)).then_inc(v_eT.sem, 1)

                    def share_tokens(x, e):
                        dve.wait_ge(t_bc.sem, t_bc.nth(x, e + 1))
                        dve.wait_ge(t_h1.sem, t_h1.nth(x, e - 1) if e > 1 else t_h1.before(x))
                        dve.tensor_tensor(xe[0:D + 1, e % 2, :], x2T[:], bank[5][0:D + 1, :], ALU.mult).then_inc(v_xe.sem, 1)

                    def step(n, a, g, x):
                        if n is not None:
                            cn, hn = Count(dve, v_step_n, VSTEP_N * n), tiled(h[:, ts(n, ROW)])
                        if a is not None:
                            ca, ha = Count(dve, v_step_a, VSTEP_A * a), tiled(h[:, ts(a, ROW)])
                        if g is not None:
                            cg, hg = Count(dve, v_step_g, VSTEP_G * g), tiled(h[:, ts(g, ROW)])
                        if x is not None:
                            cx, hx = Count(dve, v_step_x, VSTEP_X * x), tiled(h[:, ts(x, ROW)])
                        if a is not None:
                            score_tiles(a, (0, 1))
                        if x is not None:
                            dve.wait_ge(a_x2T.sem, a_x2T.nth(x))
                            share_tokens(x, 0)
                        if a is not None:
                            score_tiles(a, (2, 3))
                            bracket(ca, a)

                        def meanwhile(k):
                            if x is not None:
                                share_tokens(x, k + 1)
                            if n is not None and k == 0:
                                dve.wait_ge(g_xn.sem, g_xn.before(n))
                                stats(dve, cn, hn, *tiny[0][0:2], v_stats)
                            if g is not None and k == 1:
                                dve.wait_ge(g_xn2.sem, g_xn2.before(g))
                                dve.wait_ge(v_h1.sem, v_h1.nth(g))
                                stats(dve, cg, hg, *tiny[1][0:2], v_st2)

                        for k in range(SEARCH):
                            if a is not None:
                                count(a)
                            meanwhile(k)
                            if a is not None:
                                narrow(ca, a, k)
                        if a is not None:
                            count_high(ca)
                        if x is not None:
                            share_tokens(x, SEARCH + 1)
                        if a is not None:
                            push_high(ca)
                        if x is not None:
                            share_tokens(x, SEARCH + 2)
                        if a is not None:
                            best_eight(ca)
                            pick(ca)
                            load_missed(ca, a)
                        if n is not None:
                            dve.wait_ge(t_qk.sem, t_qk.nth(n))
                            if a is not None:
                                dve.wait_ge(t_vo.sem, t_vo.nth(a))
                            dve.tensor_scalar(kT[0:D, :], bank[1][D:2 * D, :], 1.0, None, ALU.mult, ALU.add,
                                              accum_out=ksum[:]).then_inc(v_k.sem, 1)
                        if a is not None:
                            general(a)
                            for j in range(TJ):
                                dve.scalar_tensor_tensor(out=ms[:, j, :], in0=sc[:, j, :], scalar=thr[:, j:j + 1],
                                                         in1=sc[:, j, :], op0=ALU.is_ge, op1=ALU.mult).then_inc(v_ms.sem, 1)
                            take_exps(a, 0)
                        if x is not None:
                            dve.wait_ge(t_y2.sem, t_y2.nth(x))
                            dve.tensor_tensor(hx, hx, tiled(bank[4][:, 0:ROW]), ALU.add).then_inc(v_h2.sem, 1)
                            dve.wait_ge(v_h2.sem, v_h2.nth(x))
                            dve.wait_ge(g_u.sem, g_u.before(x))
                            stats(dve, cx, hx, *tiny[2][0:2], v_st3)
                        if g is not None:
                            gates_open(cg, g)
                        if a is not None:
                            take_exps(a, 2)
                        if g is not None:
                            gates_close(cg, g)
                            assert cg.n == VSTEP_G, cg.n
                        if x is not None:
                            assert cx.n == VSTEP_X, cx.n
                        if a is not None:
                            dve.wait_ge(a_e.sem, a_e.nth(a))
                            ca.one(dve.reciprocal(rinv[:], rsum[:]))
                            dve.wait_ge(g_hb.sem, g_hb.nth(a))
                            dve.wait_ge(t_o2.sem, t_o2.nth(a))
                            for j in range(TJ):
                                dve.scalar_tensor_tensor(out=ha[:, j, :], in0=bank[0][:, ts(j, D)], scalar=rinv[:, j:j + 1],
                                                         in1=hb[:, j, :], op0=ALU.mult, op1=ALU.add).then_inc(v_h1.sem, 1)
                            assert ca.n == VSTEP_A, ca.n
                        if n is not None:
                            assert cn.n == VSTEP_N, cn.n

                    stages(dve, step)

        with ExitStack() as own:
            def tmp(name, shape, dt=F32):
                return own.enter_context(nc.sbuf_tensor(name, shape, dt))

            skew = [tmp(f"skew{r}", [P, 3, HG, TW], BF16) for r in range(2)]
            skew_in = [sem("skew_in_even"), sem("skew_in_odd")]
            t_y, a_y = Signal(sem("t_y"), HG, 2), Signal(sem("a_y"), HG)
            t_z, a_gy = Signal(sem("t_z2"), 1, 2), Signal(sem("a_gy"), 1, 2)
            yb = tmp("yb", [3 * NB, 2, HG, S])
            back = tmp("back", [P, NB * TJ, D])
            flip = tmp("flip", [P, P])
            cols = [tmp(f"cols{r}", [P, HG, TJ, 3, NB], BF16) for r in range(2)]
            colf, colr = tmp("colf", [P, HG, TJ, NB]), tmp("colr", [P, HG, TJ, NB])
            ysum = tmp("ysum", [P, 2, HG // 2 * TJ, NB])
            v_sum, v_add = Signal(sem("v_sum"), 1, 2), sem("v_add")
            v_part = sem("v_part")
            v_cols = Signal(sem("v_cols"))
            t_flip, a_back, g_flip = Signal(sem("t_flip")), Signal(sem("a_back"), 1, 2), sem("g_flip")
            FL = S // D

            with nc.Block() as block:
                @block.sync
                def _(sp):
                    with sp.Fori(0, D // HG // 2) as i:
                        for r in range(2):
                            g = 2 * i + r
                            sp.wait_ge(t_y.sem, t_y.before(g, 2))
                            for k in range(3):
                                src = bass.AP(taps3, g * (HG * KROW) + (k * D * KROW + 1), [[1, P], [KROW, HG], [1, TW]])
                                sp.dma_start(skew[r][:, k], src).then_inc(skew_in[r], 16)

                @block.gpsimd
                def _(pool):
                    pool.memset(flip[:], 0.0).then_inc(g_flip, 1)
                    pool.wait_ge(g_flip, 1)
                    pool.affine_select(out=flip[:], in_=flip[:], compare_op=ALU.not_equal, fill=1.0, base=1 - P,
                                       pattern=[[1, P]], channel_multiplier=1).then_inc(g_flip, 1)

                @block.tensor
                def _(pe):
                    for s in (t_flip, t_y, t_z):
                        s.grant(pe)
                    pe.wait_ge(g_flip, 2)
                    with pe.Fori(0, NB * TJ // FL // 2) as i:
                        for r in range(2):
                            n = 2 * i + r
                            pe.wait_ge(a_back.sem, a_back.before(n, 2))
                            pe.matmul(bank[2 + r][:], flip[:], u[:, bass.ds(n * FL, FL), :], start=True, stop=True)\
                              .then_inc(t_flip.sem, 1)
                    pe.wait_ge(a_back.sem, a_back.before(NB * TJ // FL))
                    with pe.Fori(0, D // HG // 2) as i:
                        for r in range(2):
                            g = 2 * i + r
                            pe.wait_ge(skew_in[r], 48 * i + 48)
                            pe.wait_ge(v_cols.sem, v_cols.nth(g))
                            def back_to_tokens(hh):
                                pe.wait_ge(a_y.sem, a_y.nth(g, hh + 1))
                                apart(pe, spare)
                                for lc in range(TJ):
                                    last = pe.transpose(bank[4 + 2 * r + hh // 2][:, ts(TJ * (hh % 2) + lc, 3 * NB)],
                                                        yb[:, r, hh, ts(lc, P)], identf[0:3 * NB, 0:3 * NB])
                                return last

                            for hh in range(HG):
                                pe.wait_ge(a_y.sem, a_y.before(g) - HG + hh + 1)
                                for sc in range(TJ):
                                    at = P * (TJ - 1 - sc)
                                    for k in range(3):
                                        last = pe.matmul(bank[hh][0:3 * NB, :], cols[r][:, hh, sc].rearrange("p k b -> p (k b)"),
                                                         skew[r][:, k, hh, at:at + S],
                                                         start=(sc == 0 and k == 0), stop=(sc == TJ - 1 and k == 2))
                                last.then_inc(t_y.sem, 1)
                                if hh == 0:
                                    pe.wait_ge(v_sum.sem, v_sum.before(g, 2))
                                else:
                                    back_to_tokens(hh - 1)
                            back_to_tokens(HG - 1).then_inc(t_z.sem, 1)

                @block.vector
                def _(dve):
                    v_cols.grant(dve)
                    v_sum.grant(dve)
                    dve.wait_ge(a_back.sem, a_back.before(NB * TJ // FL))

                    def columns(g, r):
                        c = Count(dve, v_part, 6 * g)
                        dve.wait_ge(t_y.sem, t_y.before(g, 2))
                        c.one(dve.tensor_copy(colf[:].rearrange("p h t b -> p b t h"),
                                              back[:, :, bass.ds(g * HG, HG)].rearrange("p (b t) h -> p b t h", t=TJ)))
                        split3(dve, c, colf[:], colr[:], [cols[r][:, :, :, k, :] for k in range(3)])
                        dve.sem_inc(v_cols.sem, 1)

                    def add_parts(g, r):
                        c = Count(dve, v_add, 5 * g)
                        dve.wait_ge(t_z.sem, t_z.nth(g))
                        dve.wait_ge(a_gy.sem, a_gy.before(g))
                        part = [[bank[4 + 2 * r + q][:, 0:HG // 2 * TJ * 3 * NB].rearrange("p (m k b) -> p m k b", k=3, b=NB)[:, :, k]
                                 for k in range(3)] for q in range(2)]
                        for q in range(2):
                            c.step(dve.tensor_copy(ysum[:, q], part[q][2]))
                        c.settle()
                        for q in range(2):
                            c.step(dve.tensor_tensor(ysum[:, q], ysum[:, q], part[q][1], ALU.add))
                        c.settle()
                        for q in range(2):
                            last = dve.tensor_tensor(ysum[:, q], ysum[:, q], part[q][0], ALU.add)
                            if q == 0:
                                c.step(last)
                        last.then_inc(v_sum.sem, 1)

                    NG = D // HG
                    columns(0, 0)
                    with dve.Fori(0, NG // 2 - 1) as i:
                        for r in range(2):
                            columns(2 * i + r + 1, 1 - r)
                            add_parts(2 * i + r, r)
                    columns(NG - 1, 1)
                    add_parts(NG - 2, 0)
                    add_parts(NG - 1, 1)

                @block.scalar
                def _(act):
                    a_back.grant(act)
                    with act.Fori(0, NB * TJ // FL // 2) as i:
                        for r in range(2):
                            n = 2 * i + r
                            act.wait_ge(t_flip.sem, t_flip.nth(n))
                            act.activation(back[:, bass.ds(n * FL, FL), :],
                                           bank[2 + r][:].rearrange("p (t d) -> p t d", d=D), ACT.Copy).then_inc(a_back.sem, 1)
                    a_y.grant(act)
                    a_gy.grant(act)
                    with act.Fori(0, D // HG // 2) as i:
                        for r in range(2):
                            g = 2 * i + r
                            for hh in range(HG):
                                act.wait_ge(t_y.sem, t_y.nth(g, hh + 1))
                                if hh == 0:
                                    act.wait_ge(t_z.sem, t_z.before(g, 2))
                                act.activation(yb[:, r, hh, :], bank[hh][0:3 * NB, :], ACT.Copy).then_inc(a_y.sem, 1)
                            act.wait_ge(v_sum.sem, v_sum.nth(g))
                            act.activation(gy[:, :, :, bass.ds(g * HG, HG)].rearrange("p b l h -> p h l b"),
                                           ysum[:].rearrange("p q (h l) b -> p (q h) l b", l=TJ), ACT.Gelu).then_inc(a_gy.sem, 1)

        with ExitStack() as own:
            def tmp(name, shape, dt=F32):
                return own.enter_context(nc.sbuf_tensor(name, shape, dt))

            def signals(names, each=1):
                return (Signal(sem(n), each) for n in names.split())

            power = tmp("power_f", [P, TJ])
            tiny = [[tmp(f"{n}f{k}", [P, TJ] + s) for n, s in (("st", [6]), ("mv", [2]), ("rs", []))] for k in range(2)]
            gT = tmp("gT", [D + 1, S])
            sg, z, r_, rn, rg, xn = (tmp(n, [P, TJ, D]) for n in ("sg", "z", "r_", "rn", "rg", "xn_f"))
            rowsT, rows_in = tmp("rowsT", [P, S]), tmp("rows_in", [P, S])
            lg, best, off = tmp("lg", [P, TJ, NX]), tmp("best", [P, TJ, 8]), tmp("off", [P, TJ, NX])
            hid = tmp("hid_f", [P, XC, S])
            y = tmp("y", [P, TJ, D])
            t_gT, t_glu, t_xT, t_lg, t_off, t_y = signals("t_gT t_glu t_xT_f t_lg t_off t_out_f")
            a_gT, a_sg, a_xT, a_off = signals("a_gT a_sg a_xT_f a_off")
            v_r, v_st, v_rn, v_h3, v_st4, v_xn, v_off, v_y, v_z = signals(
                "v_r v_st_f v_rn v_h3 v_st4 v_xn_f v_off v_y v_z")
            g_rs, g_rg, g_rs4, a_rows = signals("g_rs_f g_rg g_rs4 a_rows")
            t_hid = Signal(sem("t_hid_f"), XC)
            a_hid = Signal(sem("a_hid_f"), XC)
            y_out = sem("y_out")
            v_step_n, v_step_a, v_step_x = sem("v_step_fn"), sem("v_step_fa"), sem("v_step_fx")
            g_step, ready = sem("g_step_f"), sem("ready_f")
            VSTEP_A, VSTEP_X, GSTEP = 22, 9, 3

            def stages(eng, step):
                step(0, None, None, None)
                step(1, 0, None, None)
                step(2, 1, 0, None)
                with eng.Fori(2, NB - 1) as b:
                    step(b + 1, b, b - 1, b - 2)
                step(None, NB - 1, NB - 2, NB - 3)
                step(None, None, NB - 1, NB - 2)
                step(None, None, None, NB - 1)

            with nc.Block() as block:
                @block.sync
                def _(sp):
                    with sp.Fori(0, NB) as b:
                        sp.wait_ge(v_y.sem, v_y.nth(b))
                        sp.dma_start(out[bass.ds(b, 1)].rearrange("a (j p) d -> p (a j) d", p=P), y[:]).then_inc(y_out, 16)
                    sp.wait_ge(y_out, 16 * NB + 16)

                @block.gpsimd
                def _(pool):
                    for k, (t, value) in enumerate(((power[:], -0.5), (gT[D:D + 1, :], 1.0), (rowsT[:], 0.0),
                                                    (rowsT[D:D + 1, :], 1.0))):
                        pool.memset(t, value).then_inc(ready, 1)
                        pool.wait_ge(ready, k + 1)
                    for s in (g_rs, g_rg, g_rs4):
                        s.grant(pool)

                    def step(n, a, x, e):
                        if a is not None:
                            norms(a)

                    def norms(b):
                        c = Count(pool, g_step, GSTEP * b)
                        rstd(pool, c, v_st, b, tiny[0][1], tiny[0][2], power, g_rs)
                        pool.wait_ge(v_rn.sem, v_rn.nth(b))
                        c.one(pool.tensor_tensor(rg[:], rn[:], bc(gam1[:].unsqueeze(1), [P, TJ, D]), ALU.mult))
                        pool.tensor_tensor(rg[:], rg[:], bc(bet1[:].unsqueeze(1), [P, TJ, D]), ALU.add).then_inc(g_rg.sem, 1)
                        rstd(pool, c, v_st4, b, tiny[1][1], tiny[1][2], power, g_rs4)
                        assert c.n == GSTEP, c.n

                    stages(pool, step)

                @block.scalar
                def _(act):
                    for s in (a_gT, a_sg, a_xT, a_off, a_hid, a_rows):
                        s.grant(act)
                    act.wait_ge(ready, 4)

                    def step(n, a, x, e):
                        if n is not None:
                            act.wait_ge(t_gT.sem, t_gT.nth(n))
                            act.activation(gT[0:D, :], bank[0][0:D, :], ACT.Copy).then_inc(a_gT.sem, 1)
                        if x is not None:
                            act.wait_ge(t_xT.sem, t_xT.nth(x))
                            act.wait_ge(a_rows.sem, a_rows.before(x))
                            act.activation(rowsT[0:D, :], bank[2][0:D, :], ACT.Copy).then_inc(a_xT.sem, 1)
                        if n is not None:
                            act.wait_ge(t_glu.sem, t_glu.nth(n))
                            act.wait_ge(v_r.sem, v_r.before(n))
                            act.activation(sg[:], bank[1][:].rearrange("p (j f) -> p j f", j=TJ)[:, :, D:2 * D], ACT.Sigmoid)\
                               .then_inc(a_sg.sem, 1)
                        if e is not None:
                            hidden(e, 0)
                            hidden(e, 1)
                        if x is not None:
                            act.wait_ge(t_off.sem, t_off.nth(x))
                            act.activation(rowsT[96:P, :], bank[3][0:NX, :], ACT.Copy).then_inc(a_off.sem, 1)
                        if e is not None:
                            hidden(e, 2)
                            hidden(e, 3)
                        if x is not None:
                            act.wait_ge(a_off.sem, a_off.nth(x))
                            if e is not None:
                                act.wait_ge(t_y.sem, t_y.nth(e))
                            act.activation(rows_in[:], rowsT[:], ACT.Copy).then_inc(a_rows.sem, 1)

                    def hidden(e, k):
                        act.wait_ge(t_hid.sem, t_hid.nth(e, k + 1))
                        act.wait_ge(t_y.sem, t_y.before(e))
                        act.activation(hid[:, k, :], bank[4 + k][:], ACT.Relu).then_inc(a_hid.sem, 1)

                    stages(act, step)

                @block.tensor
                def _(pe):
                    for s in (t_gT, t_glu, t_xT, t_lg, t_off, t_y, t_hid):
                        s.grant(pe)
                    pe.wait_ge(ready, 4)

                    def step(n, a, x, e):
                        if x is not None:
                            pe.wait_ge(v_xn.sem, v_xn.nth(x))
                            apart(pe, spare)
                            for j in range(TJ):
                                last = pe.transpose(bank[2][0:D, ts(j, P)], xn[:, j, :], identf[:])
                            last.then_inc(t_xT.sem, 1)
                        if n is not None:
                            pe.wait_ge(v_z.sem, v_z.nth(n))
                            if e is not None:
                                pe.wait_ge(v_y.sem, v_y.before(e))
                            apart(pe, spare)
                            for j in range(TJ):
                                last = pe.transpose(bank[0][0:D, ts(j, P)], z[:, j, :], identf[:])
                            last.then_inc(t_gT.sem, 1)
                        if e is not None:
                            hidden(e, 0)
                        if x is not None:
                            pe.wait_ge(a_xT.sem, a_xT.nth(x))
                            for j in range(TJ):
                                last = pe.matmul(bank[3][:, ts(j, NX)], rowsT[0:D + 1, ts(j, P)], Wr[:], start=True, stop=True)
                            last.then_inc(t_lg.sem, 1)
                        if n is not None:
                            pe.wait_ge(a_gT.sem, a_gT.nth(n))
                            pe.wait_ge(v_r.sem, v_r.before(n))
                            for j in range(TJ):
                                last = pe.matmul(bank[1][:, ts(j, 2 * D)], gT[:, ts(j, P)], Wglu[:], start=True, stop=True)
                            last.then_inc(t_glu.sem, 1)
                        if e is not None:
                            hidden(e, 1)
                            hidden(e, 2)
                        if x is not None:
                            pe.wait_ge(v_off.sem, v_off.nth(x))
                            apart(pe, spare)
                            for j in range(TJ):
                                last = pe.transpose(bank[3][0:NX, ts(j, P)], off[:, j, :], identf[:])
                            last.then_inc(t_off.sem, 1)
                        if e is not None:
                            hidden(e, 3)
                            pe.wait_ge(a_hid.sem, a_hid.nth(e))
                            pe.wait_ge(v_y.sem, v_y.before(e))
                            for j in range(TJ):
                                pe.matmul(bank[0][:, ts(j, D)], rows_in[:, ts(j, P)], bx2[:], start=True, stop=False)
                                for k in range(XC):
                                    last = pe.matmul(bank[0][:, ts(j, D)], hid[:, k, ts(j, P)], Wx2[:, k, :],
                                                     start=False, stop=(k == XC - 1))
                            last.then_inc(t_y.sem, 1)

                    def hidden(e, k):
                        if k == 0:
                            pe.wait_ge(a_rows.sem, a_rows.nth(e))
                        pe.wait_ge(a_hid.sem, a_hid.before(e) - XC + k + 1)
                        pe.matmul(bank[4 + k][:], Wx1[:, ts(k, P)], rows_in[:], start=True, stop=True).then_inc(t_hid.sem, 1)

                    stages(pe, step)

                @block.vector
                def _(dve):
                    for s in (v_r, v_st, v_rn, v_h3, v_st4, v_xn, v_off, v_y, v_z):
                        s.grant(dve)
                    dve.sem_inc(y_out, 16)
                    dve.wait_ge(ready, 4)

                    def step(n, a, x, e):
                        if n is not None:
                            cn = Count(dve, v_step_n, n)
                            dve.wait_ge(t_gT.sem, t_gT.before(n))
                            dve.tensor_copy(z[:], gy[:, bass.ds(n, 1)].rearrange("p a l h -> p (a l) h")).then_inc(v_z.sem, 1)
                        if a is not None:
                            ca = Count(dve, v_step_a, VSTEP_A * a)
                            ha = tiled(h[:, ts(a, ROW)])
                            dve.wait_ge(v_r.sem, v_r.nth(a))
                            st, mv, rs = tiny[0]
                            stats(dve, ca, r_, st, mv, v_st)
                        if x is not None:
                            cx = Count(dve, v_step_x, VSTEP_X * x)
                            dve.wait_ge(t_lg.sem, t_lg.nth(x))
                            cx.one(dve.tensor_copy(lg[:], bank[3][:, 0:TJ * NX].rearrange("p (j e) -> p j e", j=TJ)))
                            apart(dve, spare)
                            for j in range(TJ):
                                cx.step(dve.max(best[:, j, :], lg[:, j, :]))
                            cx.settle()
                            for j in range(TJ):
                                cx.step(dve.tensor_scalar(off[:, j, :], lg[:, j, :], best[:, j, 0:1], 1.0,
                                                          ALU.is_ge, ALU.subtract))
                            cx.settle()
                            dve.sem_inc(v_off.sem, 1)
                            assert cx.n == VSTEP_X, cx.n
                        if a is not None:
                            dve.wait_ge(g_rs.sem, g_rs.nth(a))
                            centre(dve, ca, r_, mv, rs, rn)
                            ca.settle()
                            dve.sem_inc(v_rn.sem, 1)
                        if n is not None:
                            dve.wait_ge(a_sg.sem, a_sg.nth(n))
                            cn.one(dve.tensor_tensor(r_[:], bank[1][:].rearrange("p (j f) -> p j f", j=TJ)[:, :, 0:D], sg[:],
                                                     ALU.mult))
                            dve.tensor_tensor(r_[:], r_[:], u[:, bass.ds(TJ * n, TJ), :], ALU.add).then_inc(v_r.sem, 1)
                        if a is not None:
                            dve.wait_ge(g_rg.sem, g_rg.nth(a))
                            dve.tensor_tensor(ha, ha, rg[:], ALU.add).then_inc(v_h3.sem, 1)
                            dve.wait_ge(v_h3.sem, v_h3.nth(a))
                            st4, mv4, rs4 = tiny[1]
                            stats(dve, ca, ha, st4, mv4, v_st4)
                            dve.wait_ge(g_rs4.sem, g_rs4.nth(a))
                            if x is not None:
                                dve.wait_ge(t_xT.sem, t_xT.nth(x))
                            centre(dve, ca, ha, mv4, rs4, xn)
                            ca.settle()
                            dve.sem_inc(v_xn.sem, 1)
                            assert ca.n == VSTEP_A, ca.n
                        if e is not None:
                            dve.wait_ge(t_y.sem, t_y.nth(e))
                            dve.wait_ge(y_out, 16 * e + 16)
                            dve.scalar_tensor_tensor(out=y[:], in0=tiled(bank[0][:, 0:ROW]), scalar=0.0,
                                                     in1=tiled(h[:, ts(e, ROW)]), op0=ALU.max, op1=ALU.add).then_inc(v_y.sem, 1)

                    stages(dve, step)


def kernel(**inputs):
    import numpy as np
    import concourse.bacc as bacc
    from concourse.bass_utils import run_bass_kernel_spmd

    v = {k: np.asarray(a) for k, a in inputs.items()}
    L = {k: v[k] for k in ("x", "itok_BS_0_255", "itok_BS_0_511", "itok_BS_0_127", "itok_BS_0_63", "itok_BS_0_3")}
    et = np.zeros((96, 4, P), np.float32)
    for t, (name, chunk, col) in enumerate((("et", 0, 0), ("fc", 0, 64), ("sc", 2, 0), ("of", 3, 0), ("tt", 1, 0), ("rc", 1, 64))):
        e = v[f"L0_tok_E_{name}"]
        et[16 * t:16 * t + 16, chunk, col:col + e.shape[0]] = e.T
    L["Et"] = et.reshape(96, 4 * P)
    L["WT"] = v["L0_tok_W"].T
    L.update(tokb=v["L0_tok_b"], gam0=v["L0_tok_gamma"], bet0=v["L0_tok_beta"])
    L.update(Wqkv=v["L0_attn_W_qkv"], bqkv=v["L0_attn_b_qkv"], Wo=v["L0_attn_W_out"], bo=v["L0_attn_b_out"])
    L.update(WgT=v["L0_ffn_Wg"].T, bg=v["L0_ffn_bg"], W1T=v["L0_ffn_W1"].reshape(-1, D).T, b1=v["L0_ffn_b1"].reshape(-1),
             W2T=v["L0_ffn_W2"].transpose(0, 2, 1).reshape(-1, D), b2=v["L0_ffn_b2"])
    L.update(ldt=v["L1_attn_log_dt"], ArlT=v["L1_attn_A_real_log"].T, AimT=v["L1_attn_A_imag"].T,
             CreT=v["L1_attn_C_re"].transpose(2, 0, 1).reshape(NS, -1), CimT=v["L1_attn_C_im"].transpose(2, 0, 1).reshape(NS, -1),
             skip=v["L1_attn_D"], WgluT=v["L1_attn_W_out"].T, bglu=v["L1_attn_b_out"], gam1=v["L1_attn_gamma"],
             bet1=v["L1_attn_beta"])
    L.update(WrT=v["L1_ffn_router_w"].T, br=v["L1_ffn_router_b"], Wx1=v["L1_ffn_W1"].transpose(1, 0, 2).reshape(D, -1),
             bx1=v["L1_ffn_b1"].reshape(-1), Wx2=v["L1_ffn_W2"].reshape(-1, D), bx2=v["L1_ffn_b2"])
    nc = bacc.Bacc("TRN2", target_bir_lowering=False, num_devices=1)
    arrays, A = {}, {}
    for name, a in L.items():
        arrays[f"in_{name}"] = a = np.ascontiguousarray(a)
        A[name] = nc.dram_tensor(f"in_{name}", a.shape, mybir.dt.from_np(a.dtype), kind="ExternalInput").ap()
    out = nc.dram_tensor("out_0", (NB, S, D), F32, kind="ExternalOutput").ap()
    tower(nc, A, out)
    return run_bass_kernel_spmd(nc, [arrays], core_ids=[0]).results[0]["out_0"]
```
